# Optimizing a Trainium2 kernel written in Bass

```python
import numpy as np
import jax
import jax.numpy as jnp

def _softmax(x, axis=-1):
    return jax.nn.softmax(x, axis=axis)

def _gelu(x):
    return jax.nn.gelu(x, approximate=True)

def _silu(x):
    return jax.nn.silu(x)

def _sigmoid(x):
    return jax.nn.sigmoid(x)

def _layernorm(x, axis=-1, eps=1e-05):
    m = jnp.mean(x, axis=axis, keepdims=True)
    v = jnp.var(x, axis=axis, keepdims=True)
    return (x - m) / jnp.sqrt(v + eps)

def _scatter_add(tgt, idx, src, axis=0):
    return tgt.at[idx].add(src)

def _segment_sum(src, seg, n):
    return jax.ops.segment_sum(src, seg, n)
kernel_name = 'mk_adj_ffn_d1_adj_r2_f22177'

def setup_inputs(seed: int=0):
    np.random.seed(seed)
    _w = jnp.asarray

    def _rec_inputs():
        import jax
        import jax.numpy as jnp
        _gk = jax.random.key(seed)
        x = -0.0005963 + 1.001 * jax.random.normal(jax.random.fold_in(_gk, 1), (2048, 256), jnp.float32)
        _a = jax.random.bernoulli(jax.random.fold_in(_gk, 2), 0.000976562, (2048, 2048))
        _a = jnp.logical_or(_a, jnp.swapaxes(_a, -1, -2))
        _a = jnp.logical_or(_a, jnp.eye(2048, dtype=bool))
        _af = _a.astype(jnp.float32)
        adj = _af
        return (x, adj)
    x, adj = _rec_inputs()

    def _L0_gnn_setup():
        import jax, jax.numpy as jnp
        import numpy as np
        N = 3072
        D_IN = 256
        D_OUT = 256
        DENSITY = 0.005
        key = jax.random.key(seed)
        ks = jax.random.split(key, 12)
        x = jax.random.normal(ks[0], (N, D_IN), dtype=jnp.float32)
        adj_a = (jax.random.uniform(ks[1], (N, N)) < DENSITY).astype(jnp.float32)
        adj_b = (jax.random.uniform(ks[2], (N, N)) < DENSITY).astype(jnp.float32)
        W_sa = jax.random.normal(ks[3], (D_IN, D_OUT), dtype=jnp.float32) * (1.414 / np.sqrt(D_IN + D_OUT))
        a_sa = jax.random.normal(ks[4], (1, 2 * D_OUT), dtype=jnp.float32) * (1.414 / np.sqrt(1 + 2 * D_OUT))
        stdv = 1.0 / np.sqrt(D_OUT)
        W_gcnb = jax.random.uniform(ks[5], (D_IN, D_OUT), minval=-stdv, maxval=stdv, dtype=jnp.float32)
        b_gcnb = jax.random.uniform(ks[6], (D_OUT,), minval=-stdv, maxval=stdv, dtype=jnp.float32)
        s = 1.0 / np.sqrt(2 * D_IN)
        Wa = jax.random.uniform(ks[7], (1, 2 * D_IN), minval=-s, maxval=s, dtype=jnp.float32)
        ba = jax.random.uniform(ks[8], (1,), minval=-s, maxval=s, dtype=jnp.float32)
        Wb = jax.random.uniform(ks[9], (1, 2 * D_IN), minval=-s, maxval=s, dtype=jnp.float32)
        bb = jax.random.uniform(ks[10], (1,), minval=-s, maxval=s, dtype=jnp.float32)
        return {'x': x, 'adj_a': adj_a, 'adj_b': adj_b, 'W_sa': W_sa, 'a_sa': a_sa, 'W_gcnb': W_gcnb, 'b_gcnb': b_gcnb, 'Wa': Wa, 'ba': ba, 'Wb': Wb, 'bb': bb}
    _L0_gnn_all = _L0_gnn_setup()
    _L0_gnn_in = {k: v for k, v in _L0_gnn_all.items() if k in ('W_sa', 'a_sa', 'W_gcnb', 'b_gcnb', 'Wa', 'ba', 'Wb', 'bb')}
    del _L0_gnn_all

    def _L0_ffn_setup():
        import jax, jax.numpy as jnp
        import numpy as np
        D_MODEL = 256
        D_FF = 1024
        N_HEADS = 8
        N_EXPERTS = 8
        TOP_K = 2
        CAPACITY_FACTOR = 1.6
        BATCH = 2048
        SEQ = 16
        LN_EPS = 1e-05

        def _layernorm(x, g, b):
            mu = x.mean(-1, keepdims=True)
            var = ((x - mu) ** 2).mean(-1, keepdims=True)
            return (x - mu) * jax.lax.rsqrt(var + LN_EPS) * g + b

        def _moe(xf, router_w, router_b, w1, b1, w2, b2):
            T = xf.shape[0]
            probs = jax.nn.softmax(xf @ router_w + router_b, axis=-1)
            _, topk_idx = jax.lax.top_k(probs, TOP_K)
            capacity = int(np.ceil(T * CAPACITY_FACTOR / N_EXPERTS))
            out = jnp.zeros_like(xf)
            tok = jnp.arange(T)
            for i in range(N_EXPERTS):
                mask = (topk_idx == i).any(-1)
                pos = jnp.where(mask, tok, T)
                sel = jnp.sort(pos)[:capacity]
                xi = xf[jnp.minimum(sel, T - 1)]
                hi = jax.nn.gelu(xi @ w1[i] + b1[i], approximate=False)
                yi = hi @ w2[i] + b2[i]
                out = out.at[sel].set(yi, mode='drop')
            return out
        key = jax.random.key(seed)
        ks = jax.random.split(key, 24)
        s = 0.02
        d, f, e = (D_MODEL, D_FF, N_EXPERTS)
        inp = {'x': jax.random.normal(ks[0], (BATCH, SEQ, d), dtype=jnp.float32), 'ln1_g': jnp.ones((d,), jnp.float32), 'ln1_b': jnp.zeros((d,), jnp.float32), 'ln2_g': jnp.ones((d,), jnp.float32), 'ln2_b': jnp.zeros((d,), jnp.float32), 'wq': jax.random.normal(ks[1], (d, d)) * s, 'bq': jnp.zeros((d,)), 'wk': jax.random.normal(ks[2], (d, d)) * s, 'bk': jnp.zeros((d,)), 'wv': jax.random.normal(ks[3], (d, d)) * s, 'bv': jnp.zeros((d,)), 'wo': jax.random.normal(ks[4], (d, d)) * s, 'bo': jnp.zeros((d,)), 'router_w': jax.random.normal(ks[5], (d, e)) * s, 'router_b': jnp.zeros((e,)), 'w1': jax.random.normal(ks[6], (e, d, f)) * s, 'b1': jnp.zeros((e, f)), 'w2': jax.random.normal(ks[7], (e, f, d)) * s, 'b2': jnp.zeros((e, d))}
        return inp
    _L0_ffn_all = _L0_ffn_setup()
    _L0_ffn_in = {k: v for k, v in _L0_ffn_all.items() if k in ('ln1_g', 'ln1_b', 'ln2_g', 'ln2_b', 'wq', 'bq', 'wk', 'bk', 'wv', 'bv', 'wo', 'bo', 'router_w', 'router_b', 'w1', 'b1', 'w2', 'b2')}
    del _L0_ffn_all
    return {'x': x, 'adj': adj, 'L0_gnn_W_sa': _L0_gnn_in['W_sa'], 'L0_gnn_a_sa': _L0_gnn_in['a_sa'], 'L0_gnn_W_gcnb': _L0_gnn_in['W_gcnb'], 'L0_gnn_b_gcnb': _L0_gnn_in['b_gcnb'], 'L0_gnn_Wa': _L0_gnn_in['Wa'], 'L0_gnn_ba': _L0_gnn_in['ba'], 'L0_gnn_Wb': _L0_gnn_in['Wb'], 'L0_gnn_bb': _L0_gnn_in['bb'], 'L0_ffn_ln1_g': _L0_ffn_in['ln1_g'], 'L0_ffn_ln1_b': _L0_ffn_in['ln1_b'], 'L0_ffn_ln2_g': _L0_ffn_in['ln2_g'], 'L0_ffn_ln2_b': _L0_ffn_in['ln2_b'], 'L0_ffn_wq': _L0_ffn_in['wq'], 'L0_ffn_bq': _L0_ffn_in['bq'], 'L0_ffn_wk': _L0_ffn_in['wk'], 'L0_ffn_bk': _L0_ffn_in['bk'], 'L0_ffn_wv': _L0_ffn_in['wv'], 'L0_ffn_bv': _L0_ffn_in['bv'], 'L0_ffn_wo': _L0_ffn_in['wo'], 'L0_ffn_bo': _L0_ffn_in['bo'], 'L0_ffn_router_w': _L0_ffn_in['router_w'], 'L0_ffn_router_b': _L0_ffn_in['router_b'], 'L0_ffn_w1': _L0_ffn_in['w1'], 'L0_ffn_b1': _L0_ffn_in['b1'], 'L0_ffn_w2': _L0_ffn_in['w2'], 'L0_ffn_b2': _L0_ffn_in['b2']}

def reference(x, adj, L0_gnn_W_sa, L0_gnn_a_sa, L0_gnn_W_gcnb, L0_gnn_b_gcnb, L0_gnn_Wa, L0_gnn_ba, L0_gnn_Wb, L0_gnn_bb, L0_ffn_ln1_g, L0_ffn_ln1_b, L0_ffn_ln2_g, L0_ffn_ln2_b, L0_ffn_wq, L0_ffn_bq, L0_ffn_wk, L0_ffn_bk, L0_ffn_wv, L0_ffn_bv, L0_ffn_wo, L0_ffn_bo, L0_ffn_router_w, L0_ffn_router_b, L0_ffn_w1, L0_ffn_b1, L0_ffn_w2, L0_ffn_b2):
    import jax
    import jax.numpy as jnp

    def _L0_gnn_ref(x, adj_a, adj_b, W_sa, a_sa, W_gcnb, b_gcnb, Wa, ba, Wb, bb):
        import jax, jax.numpy as jnp
        import numpy as np
        N = 3072
        D_IN = 256
        D_OUT = 256
        DENSITY = 0.005
        type_sum_a = adj_a @ x
        type_sum_b = adj_b @ x
        attn_a = jax.nn.sigmoid(jnp.concatenate([type_sum_a, x], axis=1) @ Wa.T + ba)
        attn_b = jax.nn.sigmoid(jnp.concatenate([type_sum_b, x], axis=1) @ Wb.T + bb)
        h = x @ W_sa
        Hd = h.shape[1]
        s_left = h @ a_sa[0, :Hd]
        s_right = h @ a_sa[0, Hd:]
        scores = s_left[:, None] + s_right[None, :]
        e = jnp.where(adj_a != 0, jnp.exp(-jax.nn.leaky_relu(scores, 0.01)), 0.0)
        attn = e / (jnp.sum(e, axis=1, keepdims=True) + 1e-05)
        x_a = attn @ h
        x_b = adj_b @ (x @ W_gcnb) + b_gcnb
        return jax.nn.sigmoid(attn_a * x_a + attn_b * x_b)

    def _L0_ffn_ref(x, ln1_g, ln1_b, ln2_g, ln2_b, wq, bq, wk, bk, wv, bv, wo, bo, router_w, router_b, w1, b1, w2, b2):
        import jax, jax.numpy as jnp
        import numpy as np
        D_MODEL = 256
        D_FF = 1024
        N_HEADS = 8
        N_EXPERTS = 8
        TOP_K = 2
        CAPACITY_FACTOR = 1.6
        BATCH = 2048
        SEQ = 16
        LN_EPS = 1e-05

        def _layernorm(x, g, b):
            mu = x.mean(-1, keepdims=True)
            var = ((x - mu) ** 2).mean(-1, keepdims=True)
            return (x - mu) * jax.lax.rsqrt(var + LN_EPS) * g + b

        def _moe(xf, router_w, router_b, w1, b1, w2, b2):
            T = xf.shape[0]
            probs = jax.nn.softmax(xf @ router_w + router_b, axis=-1)
            _, topk_idx = jax.lax.top_k(probs, TOP_K)
            capacity = int(np.ceil(T * CAPACITY_FACTOR / N_EXPERTS))
            out = jnp.zeros_like(xf)
            tok = jnp.arange(T)
            for i in range(N_EXPERTS):
                mask = (topk_idx == i).any(-1)
                pos = jnp.where(mask, tok, T)
                sel = jnp.sort(pos)[:capacity]
                xi = xf[jnp.minimum(sel, T - 1)]
                hi = jax.nn.gelu(xi @ w1[i] + b1[i], approximate=False)
                yi = hi @ w2[i] + b2[i]
                out = out.at[sel].set(yi, mode='drop')
            return out
        B, S, D = x.shape
        dk = D // N_HEADS
        h = _layernorm(x, ln1_g, ln1_b)
        q = (h @ wq + bq).reshape(B, S, N_HEADS, dk)
        k = (h @ wk + bk).reshape(B, S, N_HEADS, dk)
        v = (h @ wv + bv).reshape(B, S, N_HEADS, dk)
        scores = jnp.einsum('bqhd,bkhd->bhqk', q, k) / np.sqrt(dk).astype(np.float32)
        attn = jax.nn.softmax(scores, axis=-1)
        ctx = jnp.einsum('bhqk,bkhd->bqhd', attn, v).reshape(B, S, D)
        x = x + ctx @ wo + bo
        h2 = _layernorm(x, ln2_g, ln2_b)
        moe_out = _moe(h2.reshape(-1, D), router_w, router_b, w1, b1, w2, b2)
        return x + moe_out.reshape(B, S, D)
    x = x + _L0_gnn_ref(_layernorm(x, axis=-1), adj, adj, L0_gnn_W_sa, L0_gnn_a_sa, L0_gnn_W_gcnb, L0_gnn_b_gcnb, L0_gnn_Wa, L0_gnn_ba, L0_gnn_Wb, L0_gnn_bb)
    x = x + _L0_ffn_ref(_layernorm(x, axis=-1)[None], L0_ffn_ln1_g, L0_ffn_ln1_b, L0_ffn_ln2_g, L0_ffn_ln2_b, L0_ffn_wq, L0_ffn_bq, L0_ffn_wk, L0_ffn_bk, L0_ffn_wv, L0_ffn_bv, L0_ffn_wo, L0_ffn_bo, L0_ffn_router_w, L0_ffn_router_b, L0_ffn_w1, L0_ffn_b1, L0_ffn_w2, L0_ffn_b2)[0]
    return x

_drawn_inputs = setup_inputs


def setup_inputs(seed=0):
    import zlib

    import numpy as np

    out = dict(_drawn_inputs(seed))
    spreads = {'L0_ffn_ln1_g': (1.0, 0.6),
     'L0_ffn_ln1_b': (0.0, 0.454),
     'L0_ffn_ln2_g': (1.0, 0.2),
     'L0_ffn_ln2_b': (0.0, 0.1),
     'L0_ffn_bq': (0.0, 0.8),
     'L0_ffn_bk': (0.0, 0.8),
     'L0_ffn_bv': (0.0, 0.332),
     'L0_ffn_bo': (0.0, 0.1),
     'L0_ffn_router_b': (0.0, 0.1),
     'L0_ffn_b1': (0.0, 0.486),
     'L0_ffn_b2': (0.0, 0.1)}
    factors = {'L0_gnn_b_gcnb': 6.957, 'L0_ffn_wq': 8.0, 'L0_ffn_wk': 8.0, 'L0_ffn_wv': 4.057}
    for name, (base, spread) in spreads.items():
        noise = np.random.default_rng([zlib.crc32(name.encode()), seed]).standard_normal(out[name].shape)
        drawn = base * np.exp(spread * noise) if base else spread * noise
        out[name] = jnp.asarray(drawn.astype(out[name].dtype))
    for name, factor in factors.items():
        out[name] = (out[name] * factor).astype(out[name].dtype)
    return out
```

```python
from contextlib import ExitStack

import concourse.bass as bass
from concourse import mybir

ALU = mybir.AluOpType
ACT = mybir.ActivationFunctionType
AX = mybir.AxisListType
F32 = mybir.dt.float32
F16 = mybir.dt.float16
U32 = mybir.dt.uint32

P = 128
N, D = 2048, 256
T, KT = N // P, D // P
HEADS, DK = 8, 32
FF, EXPERTS, TOPK = 1024, 8, 2
FT = FF // P
CAP = -(-N * 16 // (10 * EXPERTS))
SLOTS = EXPERTS * CAP
SKIP = 2 * 4096
EPS = 1e-5
LEAK = 0.01
SCALE = 1.0 / float(DK) ** 0.5
QC = 512
PAIR = 2
BANK = 512
HROWS = 3 * DK


def gnn_moe_kernel(nc: bass.Bass, x, adj, W_sa, a_sa, W_gcnb, b_gcnb, Wa, ba, Wb, bb,
                   ln1_g, ln1_b, ln2_g, ln2_b, wq, bq, wk, bk, wv, bv, wo, bo,
                   router_w, router_b, w1, b1, w2, b2, out):
    with ExitStack() as ctx:
        def sb(name, shape, dt=F32):
            return ctx.enter_context(nc.sbuf_tensor(name, shape, dt))

        def sem(name):
            return ctx.enter_context(nc.semaphore(name))

        moe_in = nc.dram_tensor("moe_in", (SLOTS + 1, D), F32, kind="Internal").ap()
        moe_out = nc.dram_tensor("moe_out", (SLOTS + 1, D), F32, kind="Internal").ap()

        X = sb("X", [P, T, D])
        Z = sb("Z", [P, T, D])
        T3 = sb("T3", [P, KT * N])
        R1 = sb("R1", [P, 16384])
        R2 = sb("R2", [P, 12736])
        xT = T3[:, :].rearrange("p (k n) -> p k n", k=KT)

        adj_rows = R1[:, :].rearrange("p (b i n) -> p b i n", b=4, i=PAIR)
        stacks = R1[:, :].bitcast(F16).rearrange("p (s h n) -> p s h n", s=2, h=HEADS)
        q_stack, k_stack = stacks[:, 0], stacks[:, 1]
        NB = R1[:, 0:T * D].rearrange("p (t d) -> p t d", t=T)
        w1_sb = [R1[:, s * 4096:s * 4096 + 2048].rearrange("p (k f) -> p k f", k=KT) for s in range(4)]
        w2_sb = [R1[:, s * 4096 + 2048:(s + 1) * 4096].rearrange("p (f d) -> p f d", f=FT) for s in range(4)]

        HW = D + 1
        GW = D + 2
        H = R2[:, 0:T * HW].rearrange("p (t d) -> p t d", t=T)
        o = T * HW
        G = R2[:, o:o + T * GW].bitcast(F16).rearrange("p (s t d) -> p s t d", s=2, t=T)
        o += T * GW
        neg_sl = R2[:, o:o + N]
        neg_leak_sl = R2[:, o + N:o + 2 * N]
        assert o + 2 * N <= 12736
        V = R2[:, 0:T * D].rearrange("p (t d) -> p t d", t=T)
        PTS = 12
        PT = [R2[:, 4096 + s * QC:4096 + (s + 1) * QC] for s in range(PTS)]
        parts = R2[:, 4096:8192].bitcast(F16).rearrange("p (b s n) -> p b s n", b=2, s=2)
        H2 = R2[:, 0:T * D].rearrange("p (t d) -> p t d", t=T)
        hid = [R2[:, 4096 + b * FT * CAP:4096 + (b + 1) * FT * CAP].rearrange("p (f n) -> p f n", f=FT) for b in range(2)]
        o = 4096 + 2 * FT * CAP
        yrow = [R2[:, o + b * 1024:o + (b + 1) * 1024].rearrange("p (t d) -> p t d", t=4) for b in range(2)]
        assert o + 2048 <= 12736
        YG = R2[:, 4096:8192].rearrange("p (t d) -> p t d", t=T)
        xrow = [T3[:, b * 1024:(b + 1) * 1024].rearrange("p (t d) -> p t d", t=4) for b in range(2)]
        xeT = [T3[:, 2048 + b * KT * CAP:2048 + (b + 1) * KT * CAP].rearrange("p (k n) -> p k n", k=KT) for b in range(2)]

        WA, WB = D + 2, D + 4
        WG = sb("WG", [P, KT, WA + WB])
        wqkvo = sb("wqkvo", [P, 4, KT, D])
        rw = sb("rw", [P, KT, EXPERTS])
        rows = sb("rows", [P, 5, D])
        rb_bc = sb("rb_bc", [P, EXPERTS])
        gate_b = sb("gate_b", [P, 2])
        cols = sb("cols", [P, 4, KT])
        b1c = sb("b1c", [P, EXPERTS, FT])
        b2c = sb("b2c", [P, EXPERTS, KT])
        identf = sb("identf", [P, P])
        ident16 = sb("ident16", [P, P], F16)
        tri16 = sb("tri16", [P, P], F16)
        ones16 = sb("ones16", [P, P], F16)
        onesf = sb("onesf", [P, DK])
        zeros = sb("zeros", [P, D])
        half = sb("half", [P, T])
        stats = sb("stats", [P, T, 6])
        mv = sb("mv", [P, T, 2])
        veps = sb("veps", [P, T])
        rstd = sb("rstd", [P, T])
        sc = sb("sc", [P, T, 2])
        neg_sr = sb("neg_sr", [P, 2, T])
        u2 = sb("u2", [P, T, 2])
        junk = sb("junk", [P, D])
        tb = sb("tb", [P, 2, BANK])
        ex = sb("ex", [P, 2, BANK])
        Eb = sb("Eb", [P, 3, BANK])
        Ab = sb("Ab", [P, 3, BANK], F16)
        wsl_bc = tb[:, 1, 0:KT * P].rearrange("p (k n) -> p k n", k=KT)
        a_bc = ex[:, 0, :]
        rden = tb[:, 0, :]
        yT = Eb[:, :, :].rearrange("p b n -> p (b n)")[:, 0:KT * CAP].rearrange("p (k n) -> p k n", k=KT)
        gt = sb("gt", [P, PAIR, 8])
        gv = sb("gv", [P, PAIR, 3, D])
        mx = sb("mx", [P, 16, 4])
        nm = sb("nm", [P, 16])
        nm16 = sb("nm16", [P, 16], F16)
        small = gv[:, :, :, :].rearrange("p a b c -> p (a b c)")

        def piece(at, words):
            return small[:, at * P:at * P + words]

        lg = piece(0, P).rearrange("p (t e) -> p t e", t=T)
        top = piece(1, P).rearrange("p (t e) -> p t e", t=T)
        topi = piece(2, P).bitcast(U32).rearrange("p (t e) -> p t e", t=T)
        topf = piece(3, P).rearrange("p (t e) -> p t e", t=T)
        chosen = piece(4, 2 * P).rearrange("p (s t e) -> p s t e", s=2, t=T)
        pre = piece(6, 2 * P).rearrange("p (s t e) -> p s t e", s=2, t=T)
        kept = piece(8, P).rearrange("p (t e) -> p t e", t=T)
        val = piece(9, P).rearrange("p (t e) -> p t e", t=T)
        sel16 = piece(10, P // 2).bitcast(F16).rearrange("p (t e) -> p t e", t=T)
        pre16 = piece(11, P // 2).bitcast(F16).rearrange("p (t e) -> p t e", t=T)
        eid = sb("eid", [P, EXPERTS])
        eoff = sb("eoff", [P, EXPERTS])
        slot = sb("slot", [P, T])
        slot_off = sb("slot_off", [P, T])
        slot_sc = sb("slot_sc", [P, T])
        slot_g = sb("slot_g", [P, T], U32)
        slot_s = sb("slot_s", [P, T], U32)

        B = [ctx.enter_context(nc.psum_tensor(f"B{i}", [P, BANK], F32)) for i in range(8)]

        x_in = [sem(f"x_in{i}") for i in range(4)]
        adj_in = [sem(f"adj_in{i}") for i in range(4)]
        gnn_w_in, block_w_in, bias_in, experts_b_in = sem("gnn_w_in"), sem("block_w_in"), sem("bias_in"), sem("experts_b_in")
        moe_zeroed = sem("moe_zeroed")
        const_made = sem("const_made")
        pool_step = sem("pool_step")
        rstd_made = sem("rstd_made")
        var_made = sem("var_made")
        dve_step = sem("dve_step")
        act_step = sem("act_step")
        rows_ready = sem("rows_ready")
        turned = sem("turned")
        turned_kept = sem("turned_kept")
        wsl_made = sem("wsl_made")
        proj_done = sem("proj_done")
        proj_act = sem("proj_act")
        proj_dve = sem("proj_dve")
        sl_done = sem("sl_done")
        sl_kept = sem("sl_kept")
        adjT_done = sem("adjT_done")
        adjT_kept = sem("adjT_kept")
        logit_made = sem("logit_made")
        e_made = sem("e_made")
        e_masked = sem("e_masked")
        gnn_mm = sem("gnn_mm")
        gate_v = sem("gate_v")
        gate_e = sem("gate_e")
        gnn_v = sem("gnn_v")
        gnn_e = sem("gnn_e")
        gnn_read = sem("gnn_read")
        qk_done = sem("qk_done")
        qk_hi = sem("qk_hi")
        qk_lo = sem("qk_lo")
        stacked = [sem(f"stacked{i}") for i in range(2)]
        v_done = sem("v_done")
        v_kept = sem("v_kept")
        ones_row = sem("ones_row")
        max_mm = sem("max_mm")
        max_read = sem("max_read")
        negmax = sem("negmax")
        max_turned = sem("max_turned")
        max_placed = sem("max_placed")
        s_mm = sem("s_mm")
        p_made = sem("p_made")
        pv_done = sem("pv_done")
        ctx_kept = sem("ctx_kept")
        wo_done = sem("wo_done")
        x2_made = sem("x2_made")
        lg_done = sem("lg_done")
        sel_made = sem("sel_made")
        pos_done = sem("pos_done")
        slots_made = sem("slots_made")
        scattered = sem("scattered")
        w_in = [sem(f"w_in{i}") for i in range(4)]
        xe_in = [sem(f"xe_in{i}") for i in range(2)]
        xe_turned = sem("xe_turned")
        xe_kept = sem("xe_kept")
        f1_done = sem("f1_done")
        f1_kept = sem("f1_kept")
        f2_done = sem("f2_done")
        f2_kept = sem("f2_kept")
        y_turned = sem("y_turned")
        y_kept = sem("y_kept")
        y_out = [sem(f"y_out{i}") for i in range(2)]
        gathered = sem("gathered")
        summed = sem("summed")
        stored = sem("stored")

        xv = x.rearrange("(t p) d -> p t d", p=P)
        outv = out.rearrange("(t p) d -> p t d", p=P)
        CH = T // PAIR
        JP = T // 2
        UNITS = (HEADS // 4) * (N // QC)
        full = CAP // P
        rest = CAP - full * P
        tile_rows = [P] * full + [rest]

        def column(v):
            return v.rearrange("(k p) -> p k", p=P)

        block = ctx.enter_context(nc.Block())

        @block.sync
        def _(sp):
            with nc.allow_non_contiguous_dma(reason="small vectors"):
                for i in range(4):
                    sp.dma_start(X[:, 4 * i:4 * i + 4, :], xv[:, 4 * i:4 * i + 4, :]).then_inc(x_in[i], 16)
                sp.dma_start(WG[:, :, 0:D], W_sa.rearrange("(k p) d -> p k d", p=P)).then_inc(gnn_w_in, 16)
                sp.dma_start(WG[:, :, WA:WA + D], W_gcnb.rearrange("(k p) d -> p k d", p=P)).then_inc(gnn_w_in, 16)
                for w, at in ((Wa, 0), (Wb, 1)):
                    wv_ = w.rearrange("o (s k p) -> p (o s) k", s=2, p=P)
                    for s in range(2):
                        for k in range(KT):
                            c = WA + D + 2 * s + at
                            sp.dma_start(WG[:, k, c:c + 1], wv_[:, s, k:k + 1]).then_inc(gnn_w_in, 16)
                sp.dma_start(a_bc, a_sa.to_broadcast((P, 2 * D))).then_inc(gnn_w_in, 16)
                sp.dma_start(gate_b[:, 0:1], ba.rearrange("(o d) -> o d", o=1).to_broadcast((P, 1))).then_inc(gnn_w_in, 16)
                sp.dma_start(gate_b[:, 1:2], bb.rearrange("(o d) -> o d", o=1).to_broadcast((P, 1))).then_inc(gnn_w_in, 16)
                for c in range(CH):
                    if c >= 4:
                        sp.wait_ge(adjT_done, (c - 3) * JP)
                    sp.dma_start(adj_rows[:, c % 4],
                                 adj.rearrange("(c i p) n -> c p i n", i=PAIR, p=P)[c]).then_inc(adj_in[c % 4], 16)
                    if c == 1:
                        for i, b in enumerate((b_gcnb, bv, bo, ln2_g, ln2_b)):
                            sp.dma_start(rows[:, i, :], b.rearrange("(o d) -> o d", o=1).to_broadcast((P, D))).then_inc(bias_in, 16)
                        sp.dma_start(rb_bc[:, :], router_b.rearrange("(o d) -> o d", o=1).to_broadcast((P, EXPERTS))).then_inc(bias_in, 16)
                        for i, b in enumerate((ln1_g, ln1_b, bq, bk)):
                            sp.dma_start(cols[:, i, :], column(b)).then_inc(bias_in, 16)
                    if c == 3:
                        for i, w in enumerate((wq, wk, wv, wo)):
                            sp.dma_start(wqkvo[:, i], w.rearrange("(k p) d -> p k d", p=P)).then_inc(block_w_in, 16)
                        sp.dma_start(rw[:, :, :], router_w.rearrange("(k p) e -> p k e", p=P)).then_inc(block_w_in, 16)
                        for e in range(EXPERTS):
                            sp.dma_start(b1c[:, e, :], column(b1[e])).then_inc(experts_b_in, 16)
                            sp.dma_start(b2c[:, e, :], column(b2[e])).then_inc(experts_b_in, 16)
                sp.wait_ge(const_made, 7)
                full_rows = (SLOTS + 1) // P * P
                sp.dma_start(moe_in[0:full_rows].rearrange("(t p) d -> p t d", p=P),
                             zeros[:, :].unsqueeze(1).to_broadcast((P, full_rows // P, D))).then_inc(moe_zeroed, 16)
                sp.dma_start(moe_in[full_rows:SLOTS + 1], zeros[0:SLOTS + 1 - full_rows, :]).then_inc(moe_zeroed, 16)
                sp.dma_start(moe_out[0:1], zeros[0:1, :]).then_inc(moe_zeroed, 16)
                for n in range(4):
                    s, g = n // 2, n % 2
                    sp.wait_ge(qk_hi, 4 * (n + 1))
                    sp.wait_ge(qk_lo, 4 * (n + 1))
                    for j in range(4):
                        for r, part in enumerate(((0, 0, 1), (0, 1, 0))[s]):
                            sp.dma_start(stacks[r * DK:(r + 1) * DK, s, 4 * g + j, :],
                                         parts[j * DK:(j + 1) * DK, n % 2, part, :]).then_inc(stacked[n % 2], 16)
                sp.wait_ge(s_mm, UNITS * 64)
                for e in range(4):
                    sp.dma_start(w1_sb[e], w1[e].rearrange("(k p) f -> p k f", p=P)).then_inc(w_in[e], 16)
                    sp.dma_start(w2_sb[e], w2[e].rearrange("(f p) d -> p f d", p=P)).then_inc(w_in[e], 16)
                sp.wait_ge(scattered, 16 * T)
                sp.wait_ge(lg_done, 1)

                def load_xe(e):
                    if e >= 2:
                        sp.wait_ge(xe_turned, 2 * (e - 1))
                    r = 1 + e * CAP
                    sp.dma_start(xrow[e % 2][:, 0:full, :],
                                 moe_in[r:r + full * P].rearrange("(t p) d -> p t d", p=P)).then_inc(xe_in[e % 2], 16)
                    sp.dma_start(xrow[e % 2][0:rest, full, :], moe_in[r + full * P:r + CAP]).then_inc(xe_in[e % 2], 16)

                load_xe(0)
                for e in range(EXPERTS):
                    if e + 1 < EXPERTS:
                        load_xe(e + 1)
                    sp.wait_ge(y_kept, 4 * (e + 1))
                    r = 1 + e * CAP
                    sp.dma_start(moe_out[r:r + full * P].rearrange("(t p) d -> p t d", p=P),
                                 yrow[e % 2][:, 0:full, :]).then_inc(y_out[e % 2], 16)
                    sp.dma_start(moe_out[r + full * P:r + CAP], yrow[e % 2][0:rest, full, :]).then_inc(y_out[e % 2], 16)
                    if e + 4 < EXPERTS:
                        sp.wait_ge(f2_done, KT * (e + 1))
                        sp.dma_start(w1_sb[e % 4], w1[e + 4].rearrange("(k p) f -> p k f", p=P)).then_inc(w_in[e % 4], 16)
                        sp.dma_start(w2_sb[e % 4], w2[e + 4].rearrange("(f p) d -> p f d", p=P)).then_inc(w_in[e % 4], 16)
                for i in range(4):
                    sp.wait_ge(summed, 4 * (i + 1))
                    sp.dma_start(outv[:, 4 * i:4 * i + 4, :], X[:, 4 * i:4 * i + 4, :]).then_inc(stored, 16)
                sp.wait_ge(stored, 64)

        @block.gpsimd
        def _(pool):
            nc.gpsimd.memset(identf[:, :], 0.0).then_inc(pool_step, 1)
            nc.gpsimd.memset(tri16[:, :], 1.0).then_inc(pool_step, 1)
            nc.gpsimd.memset(zeros[:, :], 0.0).then_inc(const_made, 1)
            nc.gpsimd.memset(ones16[:, :], 1.0).then_inc(const_made, 1)
            nc.gpsimd.memset(onesf[:, :], 1.0).then_inc(const_made, 1)
            nc.gpsimd.memset(half[:, :], -0.5).then_inc(const_made, 1)
            nc.gpsimd.iota(eid[:, :], [[1, EXPERTS]], base=0, channel_multiplier=0,
                           allow_small_or_imprecise_dtypes=True).then_inc(const_made, 1)
            nc.gpsimd.iota(eoff[:, :], [[CAP, EXPERTS]], base=0, channel_multiplier=0,
                           allow_small_or_imprecise_dtypes=True).then_inc(const_made, 1)
            pool.wait_ge(pool_step, 2)
            nc.gpsimd.affine_select(out=identf[:, :], in_=identf[:, :], compare_op=ALU.not_equal, fill=1.0,
                                    base=0, pattern=[[-1, P]], channel_multiplier=1).then_inc(pool_step, 1)
            nc.gpsimd.affine_select(out=tri16[:, :], in_=tri16[:, :], compare_op=ALU.is_ge, fill=0.0,
                                    base=0, pattern=[[1, P]], channel_multiplier=-1).then_inc(const_made, 1)
            pool.wait_ge(pool_step, 3)
            nc.gpsimd.tensor_copy(ident16[:, :], identf[:, :]).then_inc(const_made, 1)
            pool.wait_ge(const_made, 8)
            for n in range(4):
                pool.wait_ge(var_made, n + 1)
                nc.gpsimd.tensor_tensor(rstd[:, :], veps[:, :], half[:, :], ALU.pow).then_inc(rstd_made, 1)
            pool.wait_ge(slots_made, 1)
            pool.wait_ge(moe_zeroed, 48)
            for t in range(T):
                pool.indirect_dma_start(moe_in[:, :], bass.IndirectOffsetOnAxis(ap=slot_s[:, t:t + 1], axis=0),
                                        H2[:, t, :], None, bounds_check=SLOTS, oob_is_err=False).then_inc(scattered, 16)
            for b in range(2):
                pool.wait_ge(y_out[b], 16 * EXPERTS)
            pool.wait_ge(f2_done, KT * EXPERTS)
            for t in range(T):
                pool.indirect_dma_start(YG[:, t, :], None, moe_out[:, :],
                                        bass.IndirectOffsetOnAxis(ap=slot_g[:, t:t + 1], axis=0),
                                        bounds_check=SLOTS, oob_is_err=False).then_inc(gathered, 16)

        @block.tensor
        def _(pe):
            mm = nc.tensor.matmul
            pe.wait_ge(const_made, 8)

            turn_n = [0]

            def turn_rows(src, ready0):
                for c in range(4):
                    pe.wait_ge(rows_ready, ready0 + 4 * (c + 1))
                    for k in range(KT):
                        i = turn_n[0]
                        if i >= 2:
                            pe.wait_ge(turned_kept, i - 1)
                        for j in range(4):
                            ins = nc.tensor.transpose(B[i % 2][:, j * P:(j + 1) * P],
                                                      src[:, 4 * c + j, k * P:(k + 1) * P], identf[:, :])
                        ins.then_inc(turned, 1)
                        turn_n[0] += 1

            turn_rows(Z, 0)
            pe.wait_ge(turned_kept, 8)
            pe.wait_ge(wsl_made, 1)
            for t in range(T):
                if t >= 2:
                    pe.wait_ge(proj_act, t - 1)
                    pe.wait_ge(proj_dve, t - 1)
                for lo, hi, b in ((0, WA, 2 + t % 2), (WA, WA + WB, 4 + t % 2)):
                    for k in range(KT):
                        ins = mm(B[b][:, 0:hi - lo], xT[:, k, t * P:(t + 1) * P], WG[:, k, lo:hi],
                                 start=(k == 0), stop=(k == KT - 1))
                ins.then_inc(proj_done, 1)
            for c in range(4):
                if c >= 2:
                    pe.wait_ge(sl_kept, c - 1)
                for k in range(KT):
                    ins = mm(B[6 + c % 2][:, :], wsl_bc[:, k, :], xT[:, k, c * BANK:(c + 1) * BANK],
                             start=(k == 0), stop=(k == KT - 1))
                ins.then_inc(sl_done, 1)

            def turn_adj(c, jp):
                n = c * JP + jp
                if jp == 0:
                    pe.wait_ge(adj_in[c % 4], 16 * (c // 4 + 1))
                if n >= 4:
                    pe.wait_ge(adjT_kept, n - 3)
                    pe.wait_ge(e_masked, n - 3)
                for j in range(2):
                    for i in range(PAIR):
                        ins = nc.tensor.transpose(B[n % 4][:, (j * PAIR + i) * P:(j * PAIR + i + 1) * P],
                                                  adj_rows[:, c % 4, i, (2 * jp + j) * P:(2 * jp + j + 1) * P], identf[:, :])
                ins.then_inc(adjT_done, 1)

            pe.wait_ge(proj_dve, T)
            pe.wait_ge(proj_act, T)
            pe.wait_ge(sl_kept, 4)
            for n in range(3):
                turn_adj(n // JP, n % JP)
            for c in range(CH):
                for jp in range(JP):
                    n = c * JP + jp
                    if n + 3 < CH * JP:
                        turn_adj((n + 3) // JP, (n + 3) % JP)
                    if jp == 0 and c > 0:
                        pe.wait_ge(gnn_read, c)
                    pe.wait_ge(adjT_kept, n + 1)
                    pe.wait_ge(e_masked, n + 1)
                    for j in range(2):
                        jt = 2 * jp + j
                        for i in range(PAIR):
                            a = (j * PAIR + i) * P
                            mm(B[6 + i][:, 0:GW], Ab[:, n % 3, a:a + P], G[:, 0, jt, :], start=(jt == 0), stop=False)
                            mm(B[6 + i][:, 0:GW], Ab[:, n % 3, a:a + P], G[:, 1, jt, :], start=False, stop=(jt == T - 1))
                            ins = mm(B[4 + i][:, 0:HW], Eb[:, n % 3, a:a + P], H[:, jt, :],
                                     start=(jt == 0), stop=(jt == T - 1))
                    ins.then_inc(gnn_mm, 1)

            turn_rows(NB, T)
            pe.wait_ge(turned_kept, 16)
            pe.wait_ge(block_w_in, 80)
            pe.wait_ge(gnn_read, CH)
            for n in range(4):
                s, g = n // 2, n % 2
                for c in range(4):
                    m = 4 * n + c
                    if m >= 2:
                        pe.wait_ge(qk_hi, m - 1)
                        pe.wait_ge(qk_lo, m - 1)
                    for k in range(KT):
                        ins = mm(B[2 + m % 2][:, :], wqkvo[:, s, k, g * P:(g + 1) * P], xT[:, k, c * QC:(c + 1) * QC],
                                 start=(k == 0), stop=(k == KT - 1))
                    ins.then_inc(qk_done, 1)
            for t in range(T):
                if t >= 2:
                    pe.wait_ge(v_kept, t - 1)
                for k in range(KT):
                    ins = mm(B[4 + t % 2][:, 0:D], xT[:, k, t * P:(t + 1) * P], wqkvo[:, 2, k, :],
                             start=(k == 0), stop=(k == KT - 1))
                ins.then_inc(v_done, 1)

            NC = N // QC

            def max_scores(u, n):
                g, c = u // NC, u % NC
                h, qt, kc = n // 16, n // 4 % 4, n % 4
                m = 64 * u + n
                if m >= 2:
                    pe.wait_ge(max_read, m - 1)
                q0 = c * QC + qt * P
                mm(B[m % 2][:, :], q_stack[0:HROWS, 4 * g + h, q0:q0 + P],
                   k_stack[0:HROWS, 4 * g + h, kc * BANK:(kc + 1) * BANK], start=True, stop=True).then_inc(max_mm, 1)

            def turn_max(u):
                pe.wait_ge(negmax, u + 1)
                if u > 0:
                    pe.wait_ge(max_placed, 4 * u)
                for h in range(4):
                    for qt in range(4):
                        ins = mm(B[2][h * DK:h * DK + 1, qt * P:(qt + 1) * P], nm16[:, 4 * h + qt:4 * h + qt + 1],
                                 ident16[:, :], start=True, stop=True)
                ins.then_inc(max_turned, 1)

            def scores(u, n):
                g, c = u // NC, u % NC
                kt, h = n // 4, n % 4
                m = 64 * u + n
                if m >= 3:
                    pe.wait_ge(p_made, m - 2)
                mm(B[3 + m % 3][:, :], k_stack[0:HROWS + 1, 4 * g + h, kt * P:(kt + 1) * P],
                   q_stack[0:HROWS + 1, 4 * g + h, c * QC:(c + 1) * QC], start=True, stop=True).then_inc(s_mm, 1)

            def weigh(u, kt):
                g = u // NC
                pe.wait_ge(p_made, 64 * u + 4 * kt + 4)
                if kt == 0 and u > 0:
                    pe.wait_ge(ctx_kept, u)
                for b, w in ((6, None), (7, onesf)):
                    for h in range(4):
                        lhs = w[:, :] if w is not None else V[:, kt, (4 * g + h) * DK:(4 * g + h + 1) * DK]
                        ins = mm(B[b][h * DK:(h + 1) * DK, :], lhs, PT[(64 * u + 4 * kt + h) % PTS],
                                 start=(kt == 0), stop=(kt == T - 1))
                ins.then_inc(pv_done, 1)

            pe.wait_ge(stacked[0], 16 * 24)
            pe.wait_ge(stacked[1], 16 * 24)
            pe.wait_ge(v_kept, T)
            pe.wait_ge(ones_row, 1)
            for n in range(64):
                max_scores(0, n)
            for u in range(UNITS):
                turn_max(u)
                pe.wait_ge(max_placed, 4 * (u + 1))
                for n in range(64):
                    scores(u, n)
                    if u + 1 < UNITS:
                        max_scores(u + 1, n)
                    if n % 4 == 3 and n > 4:
                        weigh(u, n // 4 - 1)
                weigh(u, 15)

            pe.wait_ge(ctx_kept, UNITS)
            for t in range(T):
                if t >= 2:
                    pe.wait_ge(x2_made, t - 1)
                for k in range(KT):
                    ins = mm(B[t % 2][:, 0:D], xT[:, k, t * P:(t + 1) * P], wqkvo[:, 3, k, :],
                             start=(k == 0), stop=(k == KT - 1))
                ins.then_inc(wo_done, 1)
            pe.wait_ge(x2_made, T)

            turn_rows(H2, 2 * T)
            pe.wait_ge(turned_kept, 24)
            for t in range(T):
                for k in range(KT):
                    ins = mm(B[2][:, t * EXPERTS:(t + 1) * EXPERTS], xT[:, k, t * P:(t + 1) * P], rw[:, k, :],
                             start=(k == 0), stop=(k == KT - 1))
            ins.then_inc(lg_done, 1)
            pe.wait_ge(sel_made, 1)
            mm(B[3][:, 0:T * EXPERTS], tri16[:, :], sel16[:, :, :].rearrange("p t e -> p (t e)"), start=True, stop=False)
            mm(B[3][:, 0:T * EXPERTS], ones16[:, :], pre16[:, :, :].rearrange("p t e -> p (t e)"),
               start=False, stop=True).then_inc(pos_done, 1)

            for e in range(EXPERTS):
                pe.wait_ge(xe_in[e % 2], 32 * (e // 2 + 1))
                for k in range(KT):
                    if e > 0:
                        pe.wait_ge(xe_kept, 2 * (e - 1) + k + 1)
                    for i, r in enumerate(tile_rows):
                        ins = nc.tensor.transpose(B[k][:, i * P:i * P + r], xrow[e % 2][0:r, i, k * P:(k + 1) * P],
                                                  identf[0:r, 0:r])
                    ins.then_inc(xe_turned, 1)
                pe.wait_ge(w_in[e % 4], 32 * (e // 4 + 1))
                pe.wait_ge(xe_kept, 2 * (e + 1))
                for f in range(FT):
                    m = e * FT + f
                    if m >= 2:
                        pe.wait_ge(f1_kept, m - 1)
                    for k in range(KT):
                        ins = mm(B[2 + m % 2][:, 0:CAP], w1_sb[e % 4][:, k, f * P:(f + 1) * P], xeT[e % 2][:, k, :],
                                 start=(k == 0), stop=(k == KT - 1))
                    ins.then_inc(f1_done, 1)
                for d in range(KT):
                    if e > 0:
                        pe.wait_ge(f2_kept, 2 * (e - 1) + d + 1)
                    for f in range(FT):
                        pe.wait_ge(f1_kept, e * FT + f + 1)
                        ins = mm(B[4 + d][:, 0:CAP], w2_sb[e % 4][:, f, d * P:(d + 1) * P], hid[e % 2][:, f, :],
                                 start=(f == 0), stop=(f == FT - 1))
                    ins.then_inc(f2_done, 1)
                pe.wait_ge(f2_kept, 2 * (e + 1))
                for i, r in enumerate(tile_rows):
                    m = 4 * e + i
                    if m >= 2:
                        pe.wait_ge(y_kept, m - 1)
                    for d in range(KT):
                        ins = nc.tensor.transpose(B[6 + m % 2][0:r, d * P:(d + 1) * P], yT[:, d, i * P:i * P + r], identf[:, :])
                    ins.then_inc(y_turned, 1)

        @block.scalar
        def _(act):
            act_n = [0]

            def link(ins):
                act_n[0] += 1
                ins.then_inc(act_step, 1)
                act.wait_ge(act_step, act_n[0])

            A = nc.scalar.activation

            def keep_turned(n0, scale_bias):
                for i in range(8):
                    c, k = i // KT, i % KT
                    act.wait_ge(turned, n0 + i + 1)
                    dst = xT[:, k, c * BANK:(c + 1) * BANK]
                    if scale_bias:
                        A(dst, B[(n0 + i) % 2][:, :], ACT.Identity, bias=cols[:, 1, k:k + 1], scale=cols[:, 0, k:k + 1]).then_inc(turned_kept, 1)
                    else:
                        A(dst, B[(n0 + i) % 2][:, :], ACT.Copy).then_inc(turned_kept, 1)

            keep_turned(0, False)
            for t in range(T):
                act.wait_ge(proj_done, t + 1)
                A(G[:, 0, t, :], B[4 + t % 2][:, 0:GW], ACT.Copy).then_inc(proj_act, 1)
            for c in range(4):
                act.wait_ge(sl_done, c + 1)
                A(neg_sl[:, c * BANK:(c + 1) * BANK], B[6 + c % 2][:, :], ACT.Copy, scale=-1.0).then_inc(act_step, 1)
                A(neg_leak_sl[:, c * BANK:(c + 1) * BANK], B[6 + c % 2][:, :], ACT.Copy, scale=-LEAK).then_inc(sl_kept, 1)
                act_n[0] += 1

            def gates(c):
                act.wait_ge(gate_v, c + 1)
                A(gt[:, :, 2:4], gt[:, :, 0:2], ACT.Exp, scale=-1.0).then_inc(gate_e, 1)
                act.wait_ge(gnn_v, c + 1)
                A(gv[:, :, 2, :], gv[:, :, 1, :], ACT.Exp, scale=-1.0).then_inc(gnn_e, 1)

            for c in range(CH):
                for jp in range(JP):
                    n = c * JP + jp
                    act.wait_ge(logit_made, 2 * (n + 1))
                    if n >= 2:
                        act.wait_ge(e_masked, n - 1)
                    A(ex[:, n % 2, :], tb[:, n % 2, :], ACT.Exp).then_inc(e_made, 1)
                    act.wait_ge(adjT_done, n + 1)
                    if n >= 3:
                        act.wait_ge(gnn_mm, n - 2)
                    A(Ab[:, n % 3, :], B[n % 4][:, :], ACT.Copy).then_inc(adjT_kept, 1)
                    if jp == 1 and c > 0:
                        gates(c - 1)
            gates(CH - 1)

            act.wait_ge(bias_in, 160)
            keep_turned(8, True)
            for n in range(4):
                for c in range(4):
                    act.wait_ge(qk_done, 4 * n + c + 1)
                    if n >= 2:
                        act.wait_ge(stacked[n % 2], 16 * 12)
                    A(parts[:, n % 2, 0, c * QC:(c + 1) * QC], B[2 + c % 2][:, :], ACT.Identity,
                      bias=cols[:, 2 + n // 2, n % 2:n % 2 + 1]).then_inc(qk_hi, 1)

            act.wait_ge(stacked[0], 16 * 24)
            act.wait_ge(stacked[1], 16 * 24)
            for m in range(UNITS * 64):
                act.wait_ge(s_mm, m + 1)
                if m >= PTS:
                    act.wait_ge(pv_done, (m - PTS) // 4 + 1)
                A(PT[m % PTS], B[3 + m % 3][:, :], ACT.Exp, scale=SCALE).then_inc(p_made, 1)

            keep_turned(16, False)

            act.wait_ge(experts_b_in, 32 * EXPERTS)
            for e in range(EXPERTS):
                for f in range(FT):
                    m = e * FT + f
                    act.wait_ge(f1_done, m + 1)
                    if e >= 2:
                        act.wait_ge(f2_done, KT * (e - 1))
                    A(hid[e % 2][:, f, :], B[2 + m % 2][:, 0:CAP], ACT.Gelu, bias=b1c[:, e, f:f + 1]).then_inc(f1_kept, 1)

        @block.vector
        def _(dve):
            v = nc.vector
            n_step = [0]

            def step(ins):
                n_step[0] += 1
                ins.then_inc(dve_step, 1)

            def settle():
                dve.wait_ge(dve_step, n_step[0])

            def link(ins):
                step(ins)
                settle()

            norms = [0]

            def norm_stats(src, wait=None):
                for t in range(T):
                    if wait is not None:
                        wait(t)
                    step(v.bn_stats(stats[:, t, :], src[:, t, :]))
                settle()
                for t in range(T):
                    step(v.bn_aggr(mv[:, t, :], stats[:, t, :]))
                settle()
                v.tensor_scalar(veps[:, :], mv[:, :, 1], EPS, None, ALU.add).then_inc(var_made, 1)
                norms[0] += 1
                dve.wait_ge(rstd_made, norms[0])

            def normalise(dst, src, t):
                return v.tensor_scalar(dst[:, t, :], src[:, t, :], mv[:, t, 0:1], rstd[:, t:t + 1], ALU.subtract, ALU.mult)

            norm_stats(X, lambda t: dve.wait_ge(x_in[t // 4], 16))
            for t in range(T):
                normalise(Z, X, t).then_inc(rows_ready, 1)

            dve.wait_ge(gnn_w_in, 16 * 13)
            for k in range(KT):
                for s in range(2):
                    link(v.tensor_tensor_reduce(junk[:, :], WG[:, k, 0:D], ex[:, 0, s * D:(s + 1) * D], 1.0, 0.0,
                                                ALU.mult, ALU.add, WG[:, k, D + s:D + s + 1]))
            step(v.memset(H[:, :, D:HW], 1.0))
            for k in range(KT):
                step(v.tensor_scalar(wsl_bc[:, k, :], WG[:, k, 0:P], 0.0, WG[:, k, D:D + 1], ALU.mult, ALU.add))
            dve.wait_ge(dve_step, n_step[0])
            step(v.memset(junk[:, 0:1], 0.0))
            dve.wait_ge(dve_step, n_step[0])
            v.memset(junk[:, 1:2], 0.0).then_inc(wsl_made, 1)

            for t in range(T):
                dve.wait_ge(proj_done, t + 1)
                step(v.tensor_copy(H[:, t, 0:D], B[2 + t % 2][:, 0:D]))
                step(v.tensor_copy(sc[:, t, :], B[2 + t % 2][:, D:D + 2]))
                dve.wait_ge(proj_act, t + 1)
                step(v.tensor_tensor(u2[:, t, :], B[4 + t % 2][:, GW:GW + 2], gate_b[:, :], ALU.add))
                v.tensor_tensor(G[:, 1, t, :], B[4 + t % 2][:, 0:GW], G[:, 0, t, :], ALU.subtract).then_inc(proj_dve, 1)
            settle()
            step(v.tensor_scalar(neg_sr[:, 0, :], sc[:, :, 1], -1.0, None, ALU.mult))
            step(v.tensor_scalar(neg_sr[:, 1, :], sc[:, :, 1], -LEAK, None, ALU.mult))
            settle()
            dve.wait_ge(sl_kept, 4)
            dve.wait_ge(act_step, 4)
            dve.wait_ge(bias_in, 160)

            def logits(n):
                c, jp = n // JP, n % JP
                i0 = c * PAIR * P
                if n >= 2:
                    dve.wait_ge(e_made, n - 1)
                for j in range(2):
                    jt = 2 * jp + j
                    step(v.tensor_scalar(tb[:, n % 2, j * 256:(j + 1) * 256], neg_leak_sl[:, i0:i0 + 256],
                                         neg_sr[:, 1, jt:jt + 1], None, ALU.add))
                settle()
                for j in range(2):
                    jt = 2 * jp + j
                    part = tb[:, n % 2, j * 256:(j + 1) * 256]
                    ins = v.scalar_tensor_tensor(out=part, in0=neg_sl[:, i0:i0 + 256], scalar=neg_sr[:, 0, jt:jt + 1],
                                                 in1=part, op0=ALU.add, op1=ALU.min)
                    ins.then_inc(logit_made, 1)

            def mask(n):
                dve.wait_ge(e_made, n + 1)
                dve.wait_ge(adjT_kept, n + 1)
                if n >= 3:
                    dve.wait_ge(gnn_mm, n - 2)
                v.tensor_tensor(Eb[:, n % 3, :], B[n % 4][:, :], ex[:, n % 2, :], ALU.mult).then_inc(e_masked, 1)

            def gate(c):
                t0 = c * PAIR
                dve.wait_ge(gnn_mm, (c + 1) * JP)
                for i in range(PAIR):
                    step(v.tensor_tensor(gt[:, i, 0:2], B[6 + i][:, D:GW], u2[:, t0 + i, :], ALU.add))
                    step(v.tensor_scalar(gt[:, i, 4:5], B[4 + i][:, D:HW], 1e-5, None, ALU.add))
                    step(v.tensor_tensor(gv[:, i, 0, :], B[6 + i][:, 0:D], rows[:, 0, :], ALU.add))
                settle()
                step(v.reciprocal(gt[:, :, 5:6], gt[:, :, 4:5]))
                v.memset(junk[:, 2:3], 0.0).then_inc(gate_v, 1)
                dve.wait_ge(gate_e, c + 1)
                link(v.tensor_scalar(gt[:, :, 2:4], gt[:, :, 2:4], 1.0, None, ALU.add))
                link(v.reciprocal(gt[:, :, 6:8], gt[:, :, 2:4]))
                link(v.tensor_tensor(gt[:, :, 5:6], gt[:, :, 5:6], gt[:, :, 6:7], ALU.mult))
                for i in range(PAIR):
                    step(v.tensor_scalar(gv[:, i, 0, :], gv[:, i, 0, :], gt[:, i, 7:8], None, ALU.mult))
                settle()
                for i in range(PAIR):
                    step(v.scalar_tensor_tensor(out=gv[:, i, 1, :], in0=B[4 + i][:, 0:D], scalar=gt[:, i, 5:6],
                                                in1=gv[:, i, 0, :], op0=ALU.mult, op1=ALU.add))
                settle()
                v.memset(junk[:, 3:4], 0.0).then_inc(gnn_read, 1)
                v.memset(junk[:, 4:5], 0.0).then_inc(gnn_v, 1)

            def add_gnn(c):
                t0 = c * PAIR
                dve.wait_ge(gnn_e, c + 1)
                link(v.tensor_scalar(gv[:, :, 2, :], gv[:, :, 2, :], 1.0, None, ALU.add))
                link(v.reciprocal(gv[:, :, 0, :], gv[:, :, 2, :]))
                step(v.tensor_tensor(X[:, t0:t0 + PAIR, :], X[:, t0:t0 + PAIR, :], gv[:, :, 0, :], ALU.add))

            logits(0)
            for n in range(CH * JP):
                if n + 1 < CH * JP:
                    logits(n + 1)
                mask(n)
                if n % JP == 0 and n > 0:
                    gate(n // JP - 1)
                if n % JP == 2 and n > JP:
                    add_gnn(n // JP - 1)
            gate(CH - 1)
            add_gnn(CH - 1)
            settle()

            norm_stats(X)
            for t in range(T):
                step(normalise(Z, X, t))
            settle()
            norm_stats(Z)
            for t in range(T):
                normalise(NB, Z, t).then_inc(rows_ready, 1)

            dve.wait_ge(turned, 16)
            for n in range(4):
                for c in range(4):
                    dve.wait_ge(qk_hi, 4 * n + c + 1)
                    v.scalar_tensor_tensor(out=parts[:, n % 2, 1, c * QC:(c + 1) * QC], in0=B[2 + c % 2][:, :],
                                           scalar=cols[:, 2 + n // 2, n % 2:n % 2 + 1],
                                           in1=parts[:, n % 2, 0, c * QC:(c + 1) * QC],
                                           op0=ALU.add, op1=ALU.subtract).then_inc(qk_lo, 1)
            v.memset(k_stack[HROWS:HROWS + 1, :, :], 1.0).then_inc(ones_row, 1)
            for t in range(T):
                dve.wait_ge(v_done, t + 1)
                v.tensor_tensor(V[:, t, :], B[4 + t % 2][:, 0:D], rows[:, 1, :], ALU.add).then_inc(v_kept, 1)

            NC = N // QC

            def max_of(m):
                dve.wait_ge(max_mm, m + 1)
                n = m % 64
                if n == 0 and m > 0:
                    settle()
                v.tensor_reduce(mx[:, n // 4, n % 4:n % 4 + 1], B[m % 2][:, :], AX.X, ALU.max).then_inc(max_read, 1)

            def neg_max(u):
                dve.wait_ge(max_read, 64 * (u + 1))
                link(v.tensor_reduce(nm[:, :], mx[:, :, :], AX.X, ALU.max))
                if u > 0:
                    dve.wait_ge(max_turned, u)
                v.tensor_scalar(nm16[:, :], nm[:, :], -1.0, None, ALU.mult).then_inc(negmax, 1)

            def place_max(u):
                g, c = u // NC, u % NC
                dve.wait_ge(max_turned, u + 1)
                for h in range(4):
                    ins = v.tensor_copy(q_stack[HROWS:HROWS + 1, 4 * g + h, c * QC:(c + 1) * QC],
                                        B[2][h * DK:h * DK + 1, :])
                    ins.then_inc(max_placed, 1)

            def keep_ctx(u):
                g, c = u // NC, u % NC
                dve.wait_ge(pv_done, 16 * (u + 1))
                link(v.reciprocal(rden, B[7][:, :]))
                v.tensor_tensor(xT[:, g, c * QC:(c + 1) * QC], B[6][:, :], rden, ALU.mult).then_inc(ctx_kept, 1)

            for n in range(64):
                max_of(n)
            neg_max(0)
            for u in range(UNITS):
                place_max(u)
                if u + 1 < UNITS:
                    for n in range(64):
                        max_of(64 * (u + 1) + n)
                        if n == 4 and u > 0:
                            keep_ctx(u - 1)
                    neg_max(u + 1)
                elif u > 0:
                    keep_ctx(u - 1)
            keep_ctx(UNITS - 1)

            for t in range(T):
                step(v.tensor_tensor(Z[:, t, :], Z[:, t, :], rows[:, 2, :], ALU.add))
            settle()
            for t in range(T):
                dve.wait_ge(wo_done, t + 1)
                v.tensor_tensor(Z[:, t, :], B[t % 2][:, 0:D], Z[:, t, :], ALU.add).then_inc(x2_made, 1)
            dve.wait_ge(x2_made, T)
            norm_stats(Z)
            for t in range(T):
                step(normalise(H2, Z, t))
            settle()
            for t in range(T):
                step(v.tensor_tensor(H2[:, t, :], H2[:, t, :], rows[:, 3, :], ALU.mult))
            settle()
            for t in range(T):
                v.tensor_tensor(H2[:, t, :], H2[:, t, :], rows[:, 4, :], ALU.add).then_inc(rows_ready, 1)
            for t in range(T):
                step(v.tensor_tensor(X[:, t, :], X[:, t, :], Z[:, t, :], ALU.add))

            dve.wait_ge(lg_done, 1)
            for t in range(T):
                step(v.tensor_tensor(lg[:, t, :], B[2][:, t * EXPERTS:(t + 1) * EXPERTS], rb_bc[:, :], ALU.add))
            settle()
            for t in range(T):
                step(v.max(top[:, t, :], lg[:, t, :]))
            settle()
            for t in range(T):
                step(v.max_index(topi[:, t, :], top[:, t, :], lg[:, t, :]))
            settle()
            link(v.tensor_copy(topf[:, :, :], topi[:, :, :]))
            ids = eid[:, :].unsqueeze(1).to_broadcast((P, T, EXPERTS))
            offs = eoff[:, :].unsqueeze(1).to_broadcast((P, T, EXPERTS))
            for s in range(TOPK):
                step(v.tensor_tensor(chosen[:, s, :, :], topf[:, :, s:s + 1].to_broadcast((P, T, EXPERTS)), ids, ALU.is_equal))
            settle()
            step(v.tensor_tensor(sel16[:, :, :], chosen[:, 0], chosen[:, 1], ALU.add))
            step(v.memset(pre[:, :, 0:1, :], 0.0))
            step(v.tensor_tensor(pre[:, 0, 1:T, :], chosen[:, 0, 0:T - 1], chosen[:, 1, 0:T - 1], ALU.add))
            settle()
            a, s = 0, 1
            while s < T:
                step(v.tensor_copy(pre[:, 1 - a, 0:s, :], pre[:, a, 0:s, :]))
                step(v.tensor_tensor(pre[:, 1 - a, s:T, :], pre[:, a, s:T, :], pre[:, a, 0:T - s, :], ALU.add))
                settle()
                a, s = 1 - a, 2 * s
            v.tensor_copy(pre16[:, :, :], pre[:, a]).then_inc(sel_made, 1)
            dve.wait_ge(pos_done, 1)
            pos = B[3][:, 0:T * EXPERTS].rearrange("p (t e) -> p t e", t=T)
            step(v.scalar_tensor_tensor(out=kept[:, :, :], in0=pos, scalar=float(CAP), in1=sel16[:, :, :],
                                        op0=ALU.is_le, op1=ALU.mult))
            step(v.tensor_tensor(val[:, :, :], pos, offs, ALU.add))
            settle()
            link(v.tensor_tensor(val[:, :, :], val[:, :, :], kept[:, :, :], ALU.mult))
            link(v.tensor_reduce(slot[:, :], val[:, :, :], AX.X, ALU.max))
            link(v.tensor_scalar(slot_off[:, :], slot[:, :], 0.0, float(SKIP), ALU.is_equal, ALU.mult))
            link(v.tensor_tensor(slot_sc[:, :], slot[:, :], slot_off[:, :], ALU.add))
            step(v.tensor_copy(slot_g[:, :], slot[:, :]))
            settle()
            v.tensor_copy(slot_s[:, :], slot_sc[:, :]).then_inc(slots_made, 1)

            def keep_xe(e):
                for k in range(KT):
                    dve.wait_ge(xe_turned, 2 * e + k + 1)
                    v.tensor_copy(xeT[e % 2][:, k, :], B[k][:, 0:CAP]).then_inc(xe_kept, 1)

            dve.wait_ge(experts_b_in, 32 * EXPERTS)
            for e in range(EXPERTS):
                keep_xe(e)
                for d in range(KT):
                    dve.wait_ge(f2_done, KT * e + d + 1)
                    if e > 0:
                        dve.wait_ge(y_turned, 4 * e)
                    v.tensor_scalar(yT[:, d, :], B[4 + d][:, 0:CAP], b2c[:, e, d:d + 1], None, ALU.add).then_inc(f2_kept, 1)
                for i, r in enumerate(tile_rows):
                    dve.wait_ge(y_turned, 4 * e + i + 1)
                    if e >= 2:
                        dve.wait_ge(y_out[e % 2], 32 * (e // 2))
                    v.tensor_copy(yrow[e % 2][0:r, i, :], B[6 + (4 * e + i) % 2][0:r, 0:D]).then_inc(y_kept, 1)
            dve.wait_ge(gathered, 16 * T)
            settle()
            for t in range(T):
                v.tensor_tensor(X[:, t, :], X[:, t, :], YG[:, t, :], ALU.add).then_inc(summed, 1)


_INS = ['x', 'adj', 'L0_gnn_W_sa', 'L0_gnn_a_sa', 'L0_gnn_W_gcnb', 'L0_gnn_b_gcnb', 'L0_gnn_Wa', 'L0_gnn_ba',
        'L0_gnn_Wb', 'L0_gnn_bb', 'L0_ffn_ln1_g', 'L0_ffn_ln1_b', 'L0_ffn_ln2_g', 'L0_ffn_ln2_b', 'L0_ffn_wq',
        'L0_ffn_bq', 'L0_ffn_wk', 'L0_ffn_bk', 'L0_ffn_wv', 'L0_ffn_bv', 'L0_ffn_wo', 'L0_ffn_bo',
        'L0_ffn_router_w', 'L0_ffn_router_b', 'L0_ffn_w1', 'L0_ffn_b1', 'L0_ffn_w2', 'L0_ffn_b2']


def kernel(**inputs):
    import numpy as _np
    import concourse.bacc as _bacc
    from concourse import mybir as _mybir
    from concourse.bass_utils import run_bass_kernel_spmd as _run

    nc = _bacc.Bacc("TRN2", target_bir_lowering=False, num_devices=1)
    arrays, args = {}, []
    for name in _INS:
        a = _np.ascontiguousarray(inputs[name])
        arrays[f"in_{name}_dram"] = a
        args.append(nc.dram_tensor(f"in_{name}_dram", a.shape, _mybir.dt.from_np(a.dtype), kind="ExternalInput").ap())
    args.append(nc.dram_tensor("out_dram", (N, D), _mybir.dt.from_np(_np.dtype("float32")), kind="ExternalOutput").ap())
    gnn_moe_kernel(nc, *args)
    r = _run(nc, [arrays], core_ids=[0])
    return r.results[0]["out_dram"]
```

```python
from contextlib import ExitStack

import concourse.bass as bass
from concourse import mybir

ALU = mybir.AluOpType
ACT = mybir.ActivationFunctionType
AX = mybir.AxisListType
F32 = mybir.dt.float32
F16 = mybir.dt.float16
U32 = mybir.dt.uint32

P = 128
N, D = 2048, 256
T, KT = N // P, D // P
HEADS, DK = 8, 32
FF, EXPERTS, TOPK = 1024, 8, 2
FT = FF // P
CAP = -(-N * 16 // (10 * EXPERTS))
SLOTS = EXPERTS * CAP
WSCALE = 64.0
SKIP = 2 * 4096
EPS = 1e-5
LEAK = 0.01
SCALE = 1.0 / float(DK) ** 0.5
QC = 512
PAIR = 2
BANK = 512
HROWS = 3 * DK


def gnn_moe_kernel(nc: bass.Bass, x, adj, W_sa, a_sa, W_gcnb, b_gcnb, Wa, ba, Wb, bb,
                   ln1_g, ln1_b, ln2_g, ln2_b, wq, bq, wk, bk, wv, bv, wo, bo,
                   router_w, router_b, w1, b1, w2, b2, out):
    with ExitStack() as ctx:
        def sb(name, shape, dt=F32):
            return ctx.enter_context(nc.sbuf_tensor(name, shape, dt))

        def sem(name):
            return ctx.enter_context(nc.semaphore(name))

        moe_in = nc.dram_tensor("moe_in", (SLOTS + 1, D), F32, kind="Internal").ap()
        moe_out = nc.dram_tensor("moe_out", (SLOTS + 1, D), F32, kind="Internal").ap()

        X = sb("X", [P, T, D])
        Z = sb("Z", [P, T, D])
        T3 = sb("T3", [P, KT * N])
        R1 = sb("R1", [P, 16384])
        R2 = sb("R2", [P, 12736])
        xT = T3[:, :].rearrange("p (k n) -> p k n", k=KT)

        adj_rows = R1[:, :].rearrange("p (b i n) -> p b i n", b=4, i=PAIR)
        stacks = R1[:, :].bitcast(F16).rearrange("p (s h n) -> p s h n", s=2, h=HEADS)
        q_stack, k_stack = stacks[:, 0], stacks[:, 1]
        NB = R1[:, 0:T * D].rearrange("p (t d) -> p t d", t=T)
        w_land = [R1[:, 8192 + b * 4096:8192 + (b + 1) * 4096] for b in range(2)]
        w_split = [R1[:, o:o + 4096].bitcast(F16).rearrange("p (s n) -> p s n", s=2) for o in (4096, 0)]
        w1_of = [w[:, :, 0:2048].rearrange("p s (k f) -> p s k f", k=KT) for w in w_split]
        w2_of = [w[:, :, 2048:4096].rearrange("p s (f d) -> p s f d", f=FT) for w in w_split]

        HW = D + 1
        GW = D + 2
        H = R2[:, 0:T * HW].rearrange("p (t d) -> p t d", t=T)
        o = T * HW
        G = R2[:, o:o + T * GW].bitcast(F16).rearrange("p (s t d) -> p s t d", s=2, t=T)
        o += T * GW
        neg_sl = R2[:, o:o + N]
        neg_leak_sl = R2[:, o + N:o + 2 * N]
        assert o + 2 * N <= 12736
        V = R2[:, 0:T * D].rearrange("p (t d) -> p t d", t=T)
        PTK = 4
        PT = R2[:, 4096:4096 + PTK * 4 * QC].rearrange("p (s n) -> p s n", s=PTK)
        parts = R2[:, 4096:8192].bitcast(F16).rearrange("p (b s n) -> p b s n", b=2, s=2)
        H2 = R1[:, 0:T * D].rearrange("p (t d) -> p t d", t=T)
        HIDN = FT * CAP
        hid = [R2[:, b * HIDN:(b + 1) * HIDN].bitcast(F16).rearrange("p (s f n) -> p s f n", s=2, f=FT) for b in range(2)]
        hid32 = [R2[:, 2 * HIDN + b * CAP:2 * HIDN + (b + 1) * CAP] for b in range(2)]
        o = 2 * HIDN + 2 * CAP
        yrow = [R2[:, o + b * 1024:o + (b + 1) * 1024].rearrange("p (t d) -> p t d", t=4) for b in range(2)]
        assert o + 2048 <= 12736
        YG = R1[:, 8192:12288].rearrange("p (t d) -> p t d", t=T)
        xrow = [T3[:, b * 1024:(b + 1) * 1024].rearrange("p (t d) -> p t d", t=4) for b in range(2)]
        xeT = [T3[:, 2048 + b * KT * CAP:2048 + (b + 1) * KT * CAP].bitcast(F16).rearrange(
            "p (s k n) -> p s k n", s=2, k=KT) for b in range(2)]

        WA, WB = D + 2, D + 4
        WG = sb("WG", [P, KT, WA + WB])
        wqkvo = sb("wqkvo", [P, 4, KT, D])
        rw = sb("rw", [P, KT, EXPERTS])
        rows = sb("rows", [P, 5, D])
        rb_bc = sb("rb_bc", [P, EXPERTS])
        gate_b = sb("gate_b", [P, 2])
        cols = sb("cols", [P, 4, KT])
        b1c = sb("b1c", [P, EXPERTS, FT])
        b2c = sb("b2c", [P, EXPERTS, KT])
        identf = sb("identf", [P, P])
        ident16 = sb("ident16", [P, P], F16)
        tri16 = sb("tri16", [P, P], F16)
        ones16 = sb("ones16", [P, P], F16)
        onesf = sb("onesf", [P, DK])
        zeros = sb("zeros", [P, D])
        half = sb("half", [P, T])
        stats = sb("stats", [P, T, 6])
        mv = sb("mv", [P, T, 2])
        veps = sb("veps", [P, T])
        rstd = sb("rstd", [P, T])
        sc = sb("sc", [P, T, 2])
        neg_sr = sb("neg_sr", [P, 2, T])
        u2 = sb("u2", [P, T, 2])
        junk = sb("junk", [P, D])
        scratch = sb("scratch", [P, 5888])
        tb = scratch[:, 0:1024].rearrange("p (b n) -> p b n", b=2)
        ex = scratch[:, 1024:2048].rearrange("p (b n) -> p b n", b=2)
        Eb = scratch[:, 2048:3584].rearrange("p (b n) -> p b n", b=3)
        Ab = scratch[:, 3584:4352].bitcast(F16).rearrange("p (b n) -> p b n", b=3)
        gv = scratch[:, 4352:5888].rearrange("p (i s n) -> p i s n", i=PAIR, s=3)
        wsl_bc = tb[:, 1, 0:KT * P].rearrange("p (k n) -> p k n", k=KT)
        a_bc = ex[:, 0, :]
        rden = scratch[:, 4096:4608]
        pool_sum = scratch[:, 0:2048]
        yT = scratch[:, 2048:2048 + KT * CAP].rearrange("p (k n) -> p k n", k=KT)
        gt = sb("gt", [P, PAIR, 8])
        mx = sb("mx", [P, 16, 2, 2])
        nm = sb("nm", [P, 16])
        nm16 = sb("nm16", [P, 16], F16)
        small = gv[:, :, :, :].rearrange("p a b c -> p (a b c)")

        def piece(at, words):
            return small[:, at * P:at * P + words]

        lg = piece(0, P).rearrange("p (t e) -> p t e", t=T)
        top = piece(1, P).rearrange("p (t e) -> p t e", t=T)
        topi = piece(2, P).bitcast(U32).rearrange("p (t e) -> p t e", t=T)
        topf = piece(3, P).rearrange("p (t e) -> p t e", t=T)
        chosen = piece(4, 2 * P).rearrange("p (s t e) -> p s t e", s=2, t=T)
        pre = piece(6, 2 * P).rearrange("p (s t e) -> p s t e", s=2, t=T)
        kept = piece(8, P).rearrange("p (t e) -> p t e", t=T)
        val = piece(9, P).rearrange("p (t e) -> p t e", t=T)
        sel16 = piece(10, P // 2).bitcast(F16).rearrange("p (t e) -> p t e", t=T)
        pre16 = piece(11, P // 2).bitcast(F16).rearrange("p (t e) -> p t e", t=T)
        eid = sb("eid", [P, EXPERTS])
        eoff = sb("eoff", [P, EXPERTS])
        slot = sb("slot", [P, T])
        slot_off = sb("slot_off", [P, T])
        slot_sc = sb("slot_sc", [P, T])
        slot_g = sb("slot_g", [P, T], U32)
        slot_s = sb("slot_s", [P, T], U32)

        wide = [ctx.enter_context(nc.psum_tensor(f"wide{i}", [P, 2 * BANK], F32)) for i in range(2)]
        B = [wide[i // 2][:, i % 2 * BANK:(i % 2 + 1) * BANK] for i in range(4)]
        B += [ctx.enter_context(nc.psum_tensor(f"B{i}", [P, BANK], F32))[:, :] for i in range(4, 8)]

        x_in = [sem(f"x_in{i}") for i in range(4)]
        adj_in = [sem(f"adj_in{i}") for i in range(4)]
        gnn_w_in, block_w_in, bias_in, experts_b_in = sem("gnn_w_in"), sem("block_w_in"), sem("bias_in"), sem("experts_b_in")
        moe_zeroed = sem("moe_zeroed")
        const_made = sem("const_made")
        pool_step = sem("pool_step")
        rstd_made = sem("rstd_made")
        var_made = sem("var_made")
        dve_step = sem("dve_step")
        act_step = sem("act_step")
        rows_ready = sem("rows_ready")
        turned = sem("turned")
        turned_kept = sem("turned_kept")
        wsl_made = sem("wsl_made")
        proj_done = sem("proj_done")
        proj_act = sem("proj_act")
        proj_dve = sem("proj_dve")
        sl_done = sem("sl_done")
        sl_kept = sem("sl_kept")
        adjT_done = sem("adjT_done")
        adjT_kept = sem("adjT_kept")
        logit_made = sem("logit_made")
        e_made = sem("e_made")
        e_masked = sem("e_masked")
        gnn_mm = sem("gnn_mm")
        gate_v = sem("gate_v")
        gate_e = sem("gate_e")
        gnn_v = sem("gnn_v")
        gnn_e = sem("gnn_e")
        gnn_read = sem("gnn_read")
        qk_done = sem("qk_done")
        qk_hi = sem("qk_hi")
        qk_lo = sem("qk_lo")
        stacked = [sem(f"stacked{i}") for i in range(2)]
        v_done = sem("v_done")
        v_kept = sem("v_kept")
        ones_row = sem("ones_row")
        max_mm = sem("max_mm")
        max_read = sem("max_read")
        negmax = sem("negmax")
        max_turned = sem("max_turned")
        max_placed = sem("max_placed")
        s_mm = sem("s_mm")
        p_made = sem("p_made")
        pv_done = sem("pv_done")
        ctx_saved = sem("ctx_saved")
        ctx_kept = sem("ctx_kept")
        pool_summed = sem("pool_summed")
        den_done = sem("den_done")
        sums_inverted = sem("sums_inverted")
        wo_done = sem("wo_done")
        x2_made = sem("x2_made")
        lg_done = sem("lg_done")
        sel_made = sem("sel_made")
        pos_done = sem("pos_done")
        slots_made = sem("slots_made")
        scattered = [sem(f"scattered{i}") for i in range(4)]
        w_in = [sem(f"w_in{i}") for i in range(2)]
        w_hi = sem("w_hi")
        w_lo = sem("w_lo")
        hid_hi = sem("hid_hi")
        hid_lo = sem("hid_lo")
        xe_hi = sem("xe_hi")
        xe_in = [sem(f"xe_in{i}") for i in range(2)]
        xe_turned = sem("xe_turned")
        xe_lo = sem("xe_lo")
        f1_done = sem("f1_done")
        f1_kept = sem("f1_kept")
        f2_done = sem("f2_done")
        f2_kept = sem("f2_kept")
        y_turned = sem("y_turned")
        y_kept = sem("y_kept")
        y_out = [sem(f"y_out{i}") for i in range(2)]
        gathered = [sem(f"gathered{i}") for i in range(4)]
        summed = sem("summed")
        stored = sem("stored")

        xv = x.rearrange("(t p) d -> p t d", p=P)
        outv = out.rearrange("(t p) d -> p t d", p=P)
        CH = T // PAIR
        JP = T // 2
        UNITS = (HEADS // 4) * (N // QC)
        POOL_KT = (0, 1, 2, 3, 4, 6, 8, 10, 12, 13)
        PE_KT = (5, 7, 9, 11, 14, 15)
        POOL_OPS = len(POOL_KT) - 1
        STEPS = 4 * T
        PAIRS = 32
        RING = [("scores", i) for i in range(PAIRS)]
        for h in range(4):
            RING.insert(min(8 * (h + 1) + 2 + h, PAIRS + h), ("row", h))

        RING_STEPS = (1, 1, 5, 7, 8, 9, 13, 13, 16, 18, 19, 21, 21, 24, 26, 27, 28, 30, 32, 34, 35, 35, 37, 38,
                      40, 41, 44, 46, 47, 49, 49, 53, 53, 57, 57, 62)
        assert len(RING_STEPS) == len(RING)

        def ring_at(n):
            return [k for k in range(len(RING)) if RING_STEPS[k] == n]

        def ring_readers(u, k):
            if k < 2:
                u, k = u - 1, k + len(RING)
            if u < 0:
                return None
            kind, i = RING[k - 2]
            return (kind, PAIRS * u + i + 1) if kind == "scores" else (kind, 4 * u + i + 1)

        full = CAP // P
        rest = CAP - full * P
        tile_rows = [P] * full + [rest]

        def column(v):
            return v.rearrange("(k p) -> p k", p=P)

        block = ctx.enter_context(nc.Block())

        @block.sync
        def _(sp):
            with nc.allow_non_contiguous_dma(reason="small vectors"):
                for i in range(4):
                    sp.dma_start(X[:, 4 * i:4 * i + 4, :], xv[:, 4 * i:4 * i + 4, :]).then_inc(x_in[i], 16)
                sp.dma_start(WG[:, :, 0:D], W_sa.rearrange("(k p) d -> p k d", p=P)).then_inc(gnn_w_in, 16)
                sp.dma_start(WG[:, :, WA:WA + D], W_gcnb.rearrange("(k p) d -> p k d", p=P)).then_inc(gnn_w_in, 16)
                for w, at in ((Wa, 0), (Wb, 1)):
                    wv_ = w.rearrange("o (s k p) -> p (o s) k", s=2, p=P)
                    for s in range(2):
                        for k in range(KT):
                            c = WA + D + 2 * s + at
                            sp.dma_start(WG[:, k, c:c + 1], wv_[:, s, k:k + 1]).then_inc(gnn_w_in, 16)
                sp.dma_start(a_bc, a_sa.to_broadcast((P, 2 * D))).then_inc(gnn_w_in, 16)
                sp.dma_start(gate_b[:, 0:1], ba.rearrange("(o d) -> o d", o=1).to_broadcast((P, 1))).then_inc(gnn_w_in, 16)
                sp.dma_start(gate_b[:, 1:2], bb.rearrange("(o d) -> o d", o=1).to_broadcast((P, 1))).then_inc(gnn_w_in, 16)
                for c in range(CH):
                    if c >= 4:
                        sp.wait_ge(adjT_done, (c - 3) * JP)
                    sp.dma_start(adj_rows[:, c % 4],
                                 adj.rearrange("(c i p) n -> c p i n", i=PAIR, p=P)[c]).then_inc(adj_in[c % 4], 16)
                    if c == 1:
                        for i, b in enumerate((b_gcnb, bv, bo, ln2_g, ln2_b)):
                            sp.dma_start(rows[:, i, :], b.rearrange("(o d) -> o d", o=1).to_broadcast((P, D))).then_inc(bias_in, 16)
                        sp.dma_start(rb_bc[:, :], router_b.rearrange("(o d) -> o d", o=1).to_broadcast((P, EXPERTS))).then_inc(bias_in, 16)
                        for i, b in enumerate((ln1_g, ln1_b, bq, bk)):
                            sp.dma_start(cols[:, i, :], column(b)).then_inc(bias_in, 16)
                    if c == 3:
                        for i, w in enumerate((wq, wk, wv, wo)):
                            sp.dma_start(wqkvo[:, i], w.rearrange("(k p) d -> p k d", p=P)).then_inc(block_w_in, 16)
                        sp.dma_start(rw[:, :, :], router_w.rearrange("(k p) e -> p k e", p=P)).then_inc(block_w_in, 16)
                        for e in range(EXPERTS):
                            sp.dma_start(b1c[:, e, :], column(b1[e])).then_inc(experts_b_in, 16)
                            sp.dma_start(b2c[:, e, :], column(b2[e])).then_inc(experts_b_in, 16)
                sp.wait_ge(const_made, 7)
                full_rows = (SLOTS + 1) // P * P
                sp.dma_start(moe_in[0:full_rows].rearrange("(t p) d -> p t d", p=P),
                             zeros[:, :].unsqueeze(1).to_broadcast((P, full_rows // P, D))).then_inc(moe_zeroed, 16)
                sp.dma_start(moe_in[full_rows:SLOTS + 1], zeros[0:SLOTS + 1 - full_rows, :]).then_inc(moe_zeroed, 16)
                sp.dma_start(moe_out[0:1], zeros[0:1, :]).then_inc(moe_zeroed, 16)
                for n in range(4):
                    s, g = n // 2, n % 2
                    sp.wait_ge(qk_hi, 4 * (n + 1))
                    sp.wait_ge(qk_lo, 4 * (n + 1))
                    for j in range(4):
                        for r, part in enumerate(((0, 0, 1), (0, 1, 0))[s]):
                            sp.dma_start(stacks[r * DK:(r + 1) * DK, s, 4 * g + j, :],
                                         parts[j * DK:(j + 1) * DK, n % 2, part, :]).then_inc(stacked[n % 2], 16)
                def load_w(e):
                    sp.dma_start(w_land[e % 2][:, 0:2048].rearrange("p (k f) -> p k f", k=KT),
                                 w1[e].rearrange("(k p) f -> p k f", p=P)).then_inc(w_in[e % 2], 16)
                    sp.dma_start(w_land[e % 2][:, 2048:4096].rearrange("p (f d) -> p f d", f=FT),
                                 w2[e].rearrange("(f p) d -> p f d", p=P)).then_inc(w_in[e % 2], 16)

                def load_xe(e):
                    r = 1 + e * CAP
                    sp.dma_start(xrow[e % 2][:, 0:full, :],
                                 moe_in[r:r + full * P].rearrange("(t p) d -> p t d", p=P)).then_inc(xe_in[e % 2], 16)
                    sp.dma_start(xrow[e % 2][0:rest, full, :], moe_in[r + full * P:r + CAP]).then_inc(xe_in[e % 2], 16)

                def store_y(e):
                    sp.wait_ge(y_kept, 4 * (e + 1))
                    r = 1 + e * CAP
                    sp.dma_start(moe_out[r:r + full * P].rearrange("(t p) d -> p t d", p=P),
                                 yrow[e % 2][:, 0:full, :]).then_inc(y_out[e % 2], 16)
                    sp.dma_start(moe_out[r + full * P:r + CAP], yrow[e % 2][0:rest, full, :]).then_inc(y_out[e % 2], 16)

                sp.wait_ge(s_mm, UNITS // 2 * STEPS)
                load_w(0)
                sp.wait_ge(s_mm, UNITS * STEPS)
                load_w(1)
                for i in range(4):
                    sp.wait_ge(scattered[i], 16 * 4)
                sp.wait_ge(lg_done, 1)
                load_xe(0)
                load_xe(1)
                for e in range(EXPERTS):
                    if e + 2 < EXPERTS:
                        sp.wait_ge(w_hi, 4 * (e + 1))
                        sp.wait_ge(w_lo, 4 * (e + 1))
                        load_w(e + 2)
                        sp.wait_ge(xe_turned, 2 * (e + 1))
                        load_xe(e + 2)
                    if e > 0:
                        store_y(e - 1)
                store_y(EXPERTS - 1)
                for i in range(4):
                    sp.wait_ge(summed, 4 * (i + 1))
                    sp.dma_start(outv[:, 4 * i:4 * i + 4, :], X[:, 4 * i:4 * i + 4, :]).then_inc(stored, 16)
                sp.wait_ge(stored, 64)

        @block.gpsimd
        def _(pool):
            nc.gpsimd.memset(identf[:, :], 0.0).then_inc(pool_step, 1)
            nc.gpsimd.memset(tri16[:, :], 1.0).then_inc(pool_step, 1)
            nc.gpsimd.memset(zeros[:, :], 0.0).then_inc(const_made, 1)
            nc.gpsimd.memset(ones16[:, :], 1.0).then_inc(const_made, 1)
            nc.gpsimd.memset(onesf[:, :], 1.0).then_inc(const_made, 1)
            nc.gpsimd.memset(half[:, :], -0.5).then_inc(const_made, 1)
            nc.gpsimd.iota(eid[:, :], [[1, EXPERTS]], base=0, channel_multiplier=0,
                           allow_small_or_imprecise_dtypes=True).then_inc(const_made, 1)
            nc.gpsimd.iota(eoff[:, :], [[CAP, EXPERTS]], base=0, channel_multiplier=0,
                           allow_small_or_imprecise_dtypes=True).then_inc(const_made, 1)
            pool.wait_ge(pool_step, 2)
            nc.gpsimd.affine_select(out=identf[:, :], in_=identf[:, :], compare_op=ALU.not_equal, fill=1.0,
                                    base=0, pattern=[[-1, P]], channel_multiplier=1).then_inc(pool_step, 1)
            nc.gpsimd.affine_select(out=tri16[:, :], in_=tri16[:, :], compare_op=ALU.is_ge, fill=0.0,
                                    base=0, pattern=[[1, P]], channel_multiplier=-1).then_inc(const_made, 1)
            pool.wait_ge(pool_step, 3)
            nc.gpsimd.tensor_copy(ident16[:, :], identf[:, :]).then_inc(const_made, 1)
            pool.wait_ge(const_made, 8)
            def inv_std(n):
                pool.wait_ge(var_made, n + 1)
                nc.gpsimd.tensor_tensor(rstd[:, :], veps[:, :], half[:, :], ALU.pow).then_inc(rstd_made, 1)

            for n in range(3):
                inv_std(n)
            for u in range(UNITS):
                for i in range(1, len(POOL_KT)):
                    kt = POOL_KT[i]
                    first = i == 1
                    if first and u > 0:
                        pool.wait_ge(den_done, u)
                    else:
                        pool.wait_ge(pool_summed, u * POOL_OPS + i - 1)
                    pool.wait_ge(p_made, STEPS * u + 4 * kt + 4)
                    nc.gpsimd.tensor_tensor(pool_sum, PT[:, POOL_KT[0] % PTK, :] if first else pool_sum,
                                            PT[:, kt % PTK, :], ALU.add).then_inc(pool_summed, 1)
            inv_std(3)
            pool.wait_ge(slots_made, 1)
            pool.wait_ge(moe_zeroed, 48)
            for t in range(T):
                pool.indirect_dma_start(moe_in[:, :], bass.IndirectOffsetOnAxis(ap=slot_s[:, t:t + 1], axis=0),
                                        H2[:, t, :], None, bounds_check=SLOTS, oob_is_err=False).then_inc(scattered[t // 4], 16)
            for b in range(2):
                pool.wait_ge(y_out[b], 16 * EXPERTS)
            pool.wait_ge(w_hi, 4 * EXPERTS)
            pool.wait_ge(w_lo, 4 * EXPERTS)
            for t in range(T):
                pool.indirect_dma_start(YG[:, t, :], None, moe_out[:, :],
                                        bass.IndirectOffsetOnAxis(ap=slot_g[:, t:t + 1], axis=0),
                                        bounds_check=SLOTS, oob_is_err=False).then_inc(gathered[t // 4], 16)

        @block.tensor
        def _(pe):
            mm = nc.tensor.matmul
            pe.wait_ge(const_made, 8)

            turn_n = [0]

            def turn_rows(src, ready0):
                for c in range(4):
                    pe.wait_ge(rows_ready, ready0 + 4 * (c + 1))
                    for k in range(KT):
                        i = turn_n[0]
                        if i >= 2:
                            pe.wait_ge(turned_kept, i - 1)
                        for j in range(4):
                            ins = nc.tensor.transpose(B[i % 2][:, j * P:(j + 1) * P],
                                                      src[:, 4 * c + j, k * P:(k + 1) * P], identf[:, :])
                        ins.then_inc(turned, 1)
                        turn_n[0] += 1

            turn_rows(Z, 0)
            pe.wait_ge(turned_kept, 8)
            pe.wait_ge(wsl_made, 1)
            for t in range(T):
                if t >= 2:
                    pe.wait_ge(proj_act, t - 1)
                    pe.wait_ge(proj_dve, t - 1)
                for lo, hi, b in ((0, WA, 2 + t % 2), (WA, WA + WB, 4 + t % 2)):
                    for k in range(KT):
                        ins = mm(B[b][:, 0:hi - lo], xT[:, k, t * P:(t + 1) * P], WG[:, k, lo:hi],
                                 start=(k == 0), stop=(k == KT - 1))
                ins.then_inc(proj_done, 1)
            for c in range(4):
                if c >= 2:
                    pe.wait_ge(sl_kept, c - 1)
                for k in range(KT):
                    ins = mm(B[6 + c % 2][:, :], wsl_bc[:, k, :], xT[:, k, c * BANK:(c + 1) * BANK],
                             start=(k == 0), stop=(k == KT - 1))
                ins.then_inc(sl_done, 1)

            def turn_adj(c, jp):
                n = c * JP + jp
                if jp == 0:
                    pe.wait_ge(adj_in[c % 4], 16 * (c // 4 + 1))
                if n >= 4:
                    pe.wait_ge(adjT_kept, n - 3)
                    pe.wait_ge(e_masked, n - 3)
                for j in range(2):
                    for i in range(PAIR):
                        ins = nc.tensor.transpose(B[n % 4][:, (j * PAIR + i) * P:(j * PAIR + i + 1) * P],
                                                  adj_rows[:, c % 4, i, (2 * jp + j) * P:(2 * jp + j + 1) * P], identf[:, :])
                ins.then_inc(adjT_done, 1)

            pe.wait_ge(proj_dve, T)
            pe.wait_ge(proj_act, T)
            pe.wait_ge(sl_kept, 4)
            for n in range(3):
                turn_adj(n // JP, n % JP)
            for c in range(CH):
                for jp in range(JP):
                    n = c * JP + jp
                    if n + 3 < CH * JP:
                        turn_adj((n + 3) // JP, (n + 3) % JP)
                    if jp == 0 and c > 0:
                        pe.wait_ge(gnn_read, c)
                    pe.wait_ge(adjT_kept, n + 1)
                    pe.wait_ge(e_masked, n + 1)
                    for j in range(2):
                        jt = 2 * jp + j
                        for i in range(PAIR):
                            a = (j * PAIR + i) * P
                            mm(B[6 + i][:, 0:GW], Ab[:, n % 3, a:a + P], G[:, 0, jt, :], start=(jt == 0), stop=False)
                            mm(B[6 + i][:, 0:GW], Ab[:, n % 3, a:a + P], G[:, 1, jt, :], start=False, stop=(jt == T - 1))
                            ins = mm(B[4 + i][:, 0:HW], Eb[:, n % 3, a:a + P], H[:, jt, :],
                                     start=(jt == 0), stop=(jt == T - 1))
                    ins.then_inc(gnn_mm, 1)

            turn_rows(NB, T)
            pe.wait_ge(turned_kept, 16)
            pe.wait_ge(block_w_in, 80)
            pe.wait_ge(gnn_read, CH)
            for n in range(4):
                s, g = n // 2, n % 2
                for c in range(4):
                    m = 4 * n + c
                    if m >= 2:
                        pe.wait_ge(qk_hi, m - 1)
                        pe.wait_ge(qk_lo, m - 1)
                    for k in range(KT):
                        ins = mm(B[2 + m % 2], wqkvo[:, s, k, g * P:(g + 1) * P], xT[:, k, c * QC:(c + 1) * QC],
                                 start=(k == 0), stop=(k == KT - 1))
                    ins.then_inc(qk_done, 1)
            for t in range(T):
                if t >= 2:
                    pe.wait_ge(v_kept, t - 1)
                for k in range(KT):
                    ins = mm(B[4 + t % 2][:, 0:D], xT[:, k, t * P:(t + 1) * P], wqkvo[:, 2, k, :],
                             start=(k == 0), stop=(k == KT - 1))
                ins.then_inc(v_done, 1)

            NC = N // QC

            def make_max(u, k):
                g, c = u // NC, u % NC
                kind, i = RING[k]
                reader = ring_readers(u, k)
                if reader is not None:
                    pe.wait_ge(max_read if reader[0] == "scores" else max_placed, reader[1])
                if kind == "scores":
                    h, qt, part = i // 8, i // 2 % 4, i % 2
                    q0 = c * QC + qt * P
                    for j in range(2):
                        k0 = (2 * part + j) * BANK
                        ins = mm(wide[k % 2][:, j * BANK:(j + 1) * BANK], q_stack[0:HROWS, 4 * g + h, q0:q0 + P],
                                 k_stack[0:HROWS, 4 * g + h, k0:k0 + BANK], start=True, stop=True)
                    ins.then_inc(max_mm, 1)
                else:
                    pe.wait_ge(negmax, 4 * u + i + 1)
                    for qt in range(4):
                        ins = mm(wide[k % 2][0:1, qt * P:(qt + 1) * P], nm16[:, 4 * i + qt:4 * i + qt + 1],
                                 ident16[:, :], start=True, stop=True)
                    ins.then_inc(max_turned, 1)

            def scores(u, n):
                g, c = u // NC, u % NC
                kt, h = n // 4, n % 4
                m = STEPS * u + n
                if m >= 2:
                    pe.wait_ge(p_made, m - 1)
                mm(B[4 + m % 2], k_stack[0:HROWS + 1, 4 * g + h, kt * P:(kt + 1) * P],
                   q_stack[0:HROWS + 1, 4 * g + h, c * QC:(c + 1) * QC], start=True, stop=True).then_inc(s_mm, 1)

            def sum_rows(src, first, last):
                for h in range(4):
                    ins = mm(B[7][h * DK:(h + 1) * DK, :], onesf[:, :], src[:, h * QC:(h + 1) * QC], start=first, stop=last)
                return ins

            def weigh(u, kt):
                g = u // NC
                pe.wait_ge(p_made, STEPS * u + 4 * kt + 4)
                if kt == 0 and u > 0:
                    pe.wait_ge(ctx_saved, u)
                if kt == PE_KT[0] and u > 0:
                    pe.wait_ge(sums_inverted, 4 * u)
                for h in range(4):
                    ins = mm(B[6][h * DK:(h + 1) * DK, :], V[:, kt, (4 * g + h) * DK:(4 * g + h + 1) * DK],
                             PT[:, kt % PTK, h * QC:(h + 1) * QC], start=(kt == 0), stop=(kt == T - 1))
                if kt in PE_KT:
                    ins = sum_rows(PT[:, kt % PTK, :], kt == PE_KT[0], False)
                ins.then_inc(pv_done, 1)

            def sum_p(u):
                pe.wait_ge(pool_summed, (u + 1) * POOL_OPS)
                sum_rows(pool_sum, False, True).then_inc(den_done, 1)

            pe.wait_ge(stacked[0], 16 * 24)
            pe.wait_ge(stacked[1], 16 * 24)
            pe.wait_ge(v_kept, T)
            pe.wait_ge(ones_row, 1)
            for k in range(len(RING)):
                make_max(0, k)
            for u in range(UNITS):
                for n in range(STEPS):
                    if n < 4:
                        pe.wait_ge(max_placed, 4 * u + n + 1)
                    scores(u, n)
                    if u + 1 < UNITS:
                        for k in ring_at(n):
                            make_max(u + 1, k)
                    if n == 3 and u > 0:
                        weigh(u - 1, T - 1)
                    if n == 5 and u > 0:
                        sum_p(u - 1)
                    if n % 4 == 3 and n > 4:
                        weigh(u, n // 4 - 1)
            weigh(UNITS - 1, T - 1)
            sum_p(UNITS - 1)

            pe.wait_ge(ctx_kept, UNITS)
            for t in range(T):
                if t >= 2:
                    pe.wait_ge(x2_made, t - 1)
                for k in range(KT):
                    ins = mm(B[t % 2][:, 0:D], xT[:, k, t * P:(t + 1) * P], wqkvo[:, 3, k, :],
                             start=(k == 0), stop=(k == KT - 1))
                ins.then_inc(wo_done, 1)
            pe.wait_ge(x2_made, T)

            turn_rows(H2, 2 * T)
            pe.wait_ge(turned_kept, 24)
            for t in range(T):
                for k in range(KT):
                    ins = mm(B[2][:, t * EXPERTS:(t + 1) * EXPERTS], xT[:, k, t * P:(t + 1) * P], rw[:, k, :],
                             start=(k == 0), stop=(k == KT - 1))
            ins.then_inc(lg_done, 1)
            pe.wait_ge(sel_made, 1)
            mm(B[3][:, 0:T * EXPERTS], tri16[:, :], sel16[:, :, :].rearrange("p t e -> p (t e)"), start=True, stop=False)
            mm(B[3][:, 0:T * EXPERTS], ones16[:, :], pre16[:, :, :].rearrange("p t e -> p (t e)"),
               start=False, stop=True).then_inc(pos_done, 1)

            PARTS = ((0, 0), (0, 1), (1, 0))

            def turn_xe(e):
                pe.wait_ge(xe_in[e % 2], 32 * (e // 2 + 1))
                for k in range(KT):
                    if e > 0:
                        pe.wait_ge(xe_lo, 2 * (e - 1) + k + 1)
                    for i, r in enumerate(tile_rows):
                        ins = nc.tensor.transpose(B[k][:, i * P:i * P + r], xrow[e % 2][0:r, i, k * P:(k + 1) * P],
                                                  identf[0:r, 0:r])
                    ins.then_inc(xe_turned, 1)

            def turn_y(e, i):
                pe.wait_ge(f2_kept, 2 * (e + 1))
                m, r = 4 * e + i, tile_rows[i]
                if m >= 2:
                    pe.wait_ge(y_kept, m - 1)
                for d in range(KT):
                    ins = nc.tensor.transpose(B[6 + m % 2][0:r, d * P:(d + 1) * P], yT[:, d, i * P:i * P + r], identf[:, :])
                ins.then_inc(y_turned, 1)

            turn_xe(0)
            for e in range(EXPERTS):
                pe.wait_ge(w_hi, 4 * (e + 1))
                pe.wait_ge(w_lo, 4 * (e + 1))
                pe.wait_ge(xe_hi, 2 * (e + 1))
                pe.wait_ge(xe_lo, 2 * (e + 1))
                for f in range(FT):
                    m = e * FT + f
                    if m >= 2:
                        pe.wait_ge(f1_kept, m - 1)
                    for n, (a, b) in enumerate(PARTS):
                        for k in range(KT):
                            ins = mm(B[2 + m % 2][:, 0:CAP], w1_of[e % 2][:, a, k, f * P:(f + 1) * P], xeT[e % 2][:, b, k, :],
                                     start=(n == 0 and k == 0), stop=(n == 2 and k == KT - 1))
                    ins.then_inc(f1_done, 1)
                    if 1 <= f <= 4 and e > 0:
                        turn_y(e - 1, f - 1)
                if e + 1 < EXPERTS:
                    turn_xe(e + 1)
                for d in range(KT):
                    if e > 0:
                        pe.wait_ge(f2_kept, 2 * (e - 1) + d + 1)
                    for f in range(FT):
                        pe.wait_ge(hid_hi, e * FT + f + 1)
                        pe.wait_ge(hid_lo, e * FT + f + 1)
                        for n, (a, b) in enumerate(PARTS):
                            ins = mm(B[4 + d][:, 0:CAP], w2_of[e % 2][:, a, f, d * P:(d + 1) * P], hid[e % 2][:, b, f, :],
                                     start=(f == 0 and n == 0), stop=(f == FT - 1 and n == 2))
                    ins.then_inc(f2_done, 1)
            for i in range(4):
                turn_y(EXPERTS - 1, i)

        @block.scalar
        def _(act):
            act_n = [0]

            def link(ins):
                act_n[0] += 1
                ins.then_inc(act_step, 1)
                act.wait_ge(act_step, act_n[0])

            A = nc.scalar.activation

            def keep_turned(n0, scale_bias):
                for i in range(8):
                    c, k = i // KT, i % KT
                    act.wait_ge(turned, n0 + i + 1)
                    dst = xT[:, k, c * BANK:(c + 1) * BANK]
                    if scale_bias:
                        A(dst, B[(n0 + i) % 2][:, :], ACT.Identity, bias=cols[:, 1, k:k + 1], scale=cols[:, 0, k:k + 1]).then_inc(turned_kept, 1)
                    else:
                        A(dst, B[(n0 + i) % 2][:, :], ACT.Copy).then_inc(turned_kept, 1)

            keep_turned(0, False)
            for t in range(T):
                act.wait_ge(proj_done, t + 1)
                A(G[:, 0, t, :], B[4 + t % 2][:, 0:GW], ACT.Copy).then_inc(proj_act, 1)
            for c in range(4):
                act.wait_ge(sl_done, c + 1)
                A(neg_sl[:, c * BANK:(c + 1) * BANK], B[6 + c % 2][:, :], ACT.Copy, scale=-1.0).then_inc(act_step, 1)
                A(neg_leak_sl[:, c * BANK:(c + 1) * BANK], B[6 + c % 2][:, :], ACT.Copy, scale=-LEAK).then_inc(sl_kept, 1)
                act_n[0] += 1

            def gates(c):
                act.wait_ge(gate_v, c + 1)
                A(gt[:, :, 2:4], gt[:, :, 0:2], ACT.Tanh, scale=0.5).then_inc(gate_e, 1)
                act.wait_ge(gnn_v, c + 1)
                A(gv[:, :, 2, :], gv[:, :, 1, :], ACT.Tanh, scale=0.5).then_inc(gnn_e, 1)

            for c in range(CH):
                for jp in range(JP):
                    n = c * JP + jp
                    act.wait_ge(logit_made, 2 * (n + 1))
                    if n >= 2:
                        act.wait_ge(e_masked, n - 1)
                    A(ex[:, n % 2, :], tb[:, n % 2, :], ACT.Exp).then_inc(e_made, 1)
                    act.wait_ge(adjT_done, n + 1)
                    if n >= 3:
                        act.wait_ge(gnn_mm, n - 2)
                    A(Ab[:, n % 3, :], B[n % 4][:, :], ACT.Copy).then_inc(adjT_kept, 1)
                    if jp == 1 and c > 0:
                        gates(c - 1)
            gates(CH - 1)

            act.wait_ge(bias_in, 160)
            keep_turned(8, True)
            for n in range(4):
                for c in range(4):
                    act.wait_ge(qk_done, 4 * n + c + 1)
                    if n >= 2:
                        act.wait_ge(stacked[n % 2], 16 * 12)
                    A(parts[:, n % 2, 0, c * QC:(c + 1) * QC], B[2 + c % 2][:, :], ACT.Identity,
                      bias=cols[:, 2 + n // 2, n % 2:n % 2 + 1]).then_inc(qk_hi, 1)

            act.wait_ge(stacked[0], 16 * 24)
            act.wait_ge(stacked[1], 16 * 24)
            def place_max(u, h):
                g, c = u // NC, u % NC
                act.wait_ge(max_turned, 4 * u + h + 1)
                A(q_stack[HROWS:HROWS + 1, 4 * g + h, c * QC:(c + 1) * QC],
                  wide[RING.index(("row", h)) % 2][0:1, 0:QC], ACT.Copy).then_inc(max_placed, 1)

            NC = N // QC
            for h in range(4):
                place_max(0, h)
            row_steps = {}
            for h in range(4):
                k = RING.index(("row", h))
                row_steps[min(RING_STEPS[k] + 2, STEPS - 1)] = h
            for m in range(UNITS * STEPS):
                u, kt, h = m // STEPS, m % STEPS // 4, m % 4
                if u + 1 < UNITS and m % STEPS in row_steps:
                    place_max(u + 1, row_steps[m % STEPS])
                act.wait_ge(s_mm, m + 1)
                if h == 0 and m >= 4 * PTK:
                    k0 = m // 4 - PTK
                    u0, kt0 = k0 // T, k0 % T
                    act.wait_ge(pv_done, k0 + 1)
                    if kt0 in POOL_KT:
                        act.wait_ge(pool_summed, u0 * POOL_OPS + max(POOL_KT.index(kt0), 1))
                A(PT[:, kt % PTK, h * QC:(h + 1) * QC], B[4 + m % 2], ACT.Exp, scale=SCALE).then_inc(p_made, 1)

            keep_turned(16, False)

            def weight_hi(e, q):
                part = slice(q * 1024, (q + 1) * 1024)
                if q == 0:
                    act.wait_ge(w_in[e % 2], 32 * (e // 2 + 1))
                    if e >= 2:
                        act.wait_ge(f2_done, KT * (e - 1))
                A(w_split[e % 2][:, 0, part], w_land[e % 2][:, part], ACT.Copy, scale=WSCALE).then_inc(w_hi, 1)

            def x_hi(e):
                for k in range(KT):
                    act.wait_ge(xe_turned, 2 * e + k + 1)
                    A(xeT[e % 2][:, 0, k, :], B[k][:, 0:CAP], ACT.Copy).then_inc(xe_hi, 1)

            act.wait_ge(experts_b_in, 32 * EXPERTS)
            act.wait_ge(lg_done, 1)
            for q in range(4):
                weight_hi(0, q)
            x_hi(0)
            for e in range(EXPERTS):
                for f in range(FT):
                    m = e * FT + f
                    act.wait_ge(f1_done, m + 1)
                    if m >= 2:
                        act.wait_ge(hid_lo, m - 1)
                    A(hid32[m % 2], B[2 + m % 2][:, 0:CAP], ACT.Gelu, bias=b1c[:, e, f:f + 1],
                      scale=1.0 / WSCALE).then_inc(f1_kept, 1)
                    act.wait_ge(f1_kept, m + 1)
                    A(hid[e % 2][:, 0, f, :], hid32[m % 2], ACT.Copy).then_inc(hid_hi, 1)
                if e + 1 < EXPERTS:
                    x_hi(e + 1)
                    for q in range(4):
                        weight_hi(e + 1, q)

        @block.vector
        def _(dve):
            v = nc.vector
            n_step = [0]

            def step(ins):
                n_step[0] += 1
                ins.then_inc(dve_step, 1)

            def settle():
                dve.wait_ge(dve_step, n_step[0])

            def link(ins):
                step(ins)
                settle()

            norms = [0]

            def norm_stats(src, wait=None):
                for t in range(T):
                    if wait is not None:
                        wait(t)
                    step(v.bn_stats(stats[:, t, :], src[:, t, :]))
                settle()
                for t in range(T):
                    step(v.bn_aggr(mv[:, t, :], stats[:, t, :]))
                settle()
                v.tensor_scalar(veps[:, :], mv[:, :, 1], EPS, None, ALU.add).then_inc(var_made, 1)
                norms[0] += 1
                dve.wait_ge(rstd_made, norms[0])

            def normalise(dst, src, t):
                return v.tensor_scalar(dst[:, t, :], src[:, t, :], mv[:, t, 0:1], rstd[:, t:t + 1], ALU.subtract, ALU.mult)

            norm_stats(X, lambda t: dve.wait_ge(x_in[t // 4], 16))
            for t in range(T):
                normalise(Z, X, t).then_inc(rows_ready, 1)

            dve.wait_ge(gnn_w_in, 16 * 13)
            for k in range(KT):
                for s in range(2):
                    link(v.tensor_tensor_reduce(junk[:, :], WG[:, k, 0:D], ex[:, 0, s * D:(s + 1) * D], 1.0, 0.0,
                                                ALU.mult, ALU.add, WG[:, k, D + s:D + s + 1]))
            step(v.memset(H[:, :, D:HW], 1.0))
            for k in range(KT):
                step(v.tensor_scalar(wsl_bc[:, k, :], WG[:, k, 0:P], 0.0, WG[:, k, D:D + 1], ALU.mult, ALU.add))
            dve.wait_ge(dve_step, n_step[0])
            step(v.memset(junk[:, 0:1], 0.0))
            dve.wait_ge(dve_step, n_step[0])
            v.memset(junk[:, 1:2], 0.0).then_inc(wsl_made, 1)

            for t in range(T):
                dve.wait_ge(proj_done, t + 1)
                step(v.tensor_copy(H[:, t, 0:D], B[2 + t % 2][:, 0:D]))
                step(v.tensor_copy(sc[:, t, :], B[2 + t % 2][:, D:D + 2]))
                dve.wait_ge(proj_act, t + 1)
                step(v.tensor_tensor(u2[:, t, :], B[4 + t % 2][:, GW:GW + 2], gate_b[:, :], ALU.add))
                v.tensor_tensor(G[:, 1, t, :], B[4 + t % 2][:, 0:GW], G[:, 0, t, :], ALU.subtract).then_inc(proj_dve, 1)
            settle()
            step(v.tensor_scalar(neg_sr[:, 0, :], sc[:, :, 1], -1.0, None, ALU.mult))
            step(v.tensor_scalar(neg_sr[:, 1, :], sc[:, :, 1], -LEAK, None, ALU.mult))
            settle()
            dve.wait_ge(sl_kept, 4)
            dve.wait_ge(act_step, 4)
            dve.wait_ge(bias_in, 160)

            def logits(n):
                c, jp = n // JP, n % JP
                i0 = c * PAIR * P
                if n >= 2:
                    dve.wait_ge(e_made, n - 1)
                for j in range(2):
                    jt = 2 * jp + j
                    step(v.tensor_scalar(tb[:, n % 2, j * 256:(j + 1) * 256], neg_leak_sl[:, i0:i0 + 256],
                                         neg_sr[:, 1, jt:jt + 1], None, ALU.add))
                settle()
                for j in range(2):
                    jt = 2 * jp + j
                    part = tb[:, n % 2, j * 256:(j + 1) * 256]
                    ins = v.scalar_tensor_tensor(out=part, in0=neg_sl[:, i0:i0 + 256], scalar=neg_sr[:, 0, jt:jt + 1],
                                                 in1=part, op0=ALU.add, op1=ALU.min)
                    ins.then_inc(logit_made, 1)

            def mask(n):
                dve.wait_ge(e_made, n + 1)
                dve.wait_ge(adjT_kept, n + 1)
                if n >= 3:
                    dve.wait_ge(gnn_mm, n - 2)
                v.tensor_tensor(Eb[:, n % 3, :], B[n % 4][:, :], ex[:, n % 2, :], ALU.mult).then_inc(e_masked, 1)

            def gate(c):
                t0 = c * PAIR
                dve.wait_ge(gnn_mm, (c + 1) * JP)
                for i in range(PAIR):
                    step(v.tensor_tensor(gt[:, i, 0:2], B[6 + i][:, D:GW], u2[:, t0 + i, :], ALU.add))
                    step(v.tensor_scalar(gt[:, i, 4:5], B[4 + i][:, D:HW], 1e-5, None, ALU.add))
                    step(v.tensor_tensor(gv[:, i, 0, :], B[6 + i][:, 0:D], rows[:, 0, :], ALU.add))
                settle()
                step(v.reciprocal(gt[:, :, 5:6], gt[:, :, 4:5]))
                v.memset(junk[:, 2:3], 0.0).then_inc(gate_v, 1)
                dve.wait_ge(gate_e, c + 1)
                link(v.tensor_scalar(gt[:, :, 6:8], gt[:, :, 2:4], 0.5, 0.5, ALU.mult, ALU.add))
                link(v.tensor_tensor(gt[:, :, 5:6], gt[:, :, 5:6], gt[:, :, 6:7], ALU.mult))
                for i in range(PAIR):
                    step(v.tensor_scalar(gv[:, i, 0, :], gv[:, i, 0, :], gt[:, i, 7:8], None, ALU.mult))
                settle()
                for i in range(PAIR):
                    step(v.scalar_tensor_tensor(out=gv[:, i, 1, :], in0=B[4 + i][:, 0:D], scalar=gt[:, i, 5:6],
                                                in1=gv[:, i, 0, :], op0=ALU.mult, op1=ALU.add))
                settle()
                v.memset(junk[:, 3:4], 0.0).then_inc(gnn_read, 1)
                v.memset(junk[:, 4:5], 0.0).then_inc(gnn_v, 1)

            def add_gnn(c):
                t0 = c * PAIR
                dve.wait_ge(gnn_e, c + 1)
                link(v.tensor_scalar(gv[:, :, 0, :], gv[:, :, 2, :], 0.5, 0.5, ALU.mult, ALU.add))
                step(v.tensor_tensor(X[:, t0:t0 + PAIR, :], X[:, t0:t0 + PAIR, :], gv[:, :, 0, :], ALU.add))

            logits(0)
            for n in range(CH * JP):
                if n + 1 < CH * JP:
                    logits(n + 1)
                mask(n)
                if n % JP == 0 and n > 0:
                    gate(n // JP - 1)
                if n % JP == 2 and n > JP:
                    add_gnn(n // JP - 1)
            gate(CH - 1)
            add_gnn(CH - 1)
            settle()

            norm_stats(X)
            for t in range(T):
                step(normalise(Z, X, t))
            settle()
            norm_stats(Z)
            for t in range(T):
                normalise(NB, Z, t).then_inc(rows_ready, 1)

            dve.wait_ge(turned, 16)
            for n in range(4):
                for c in range(4):
                    dve.wait_ge(qk_hi, 4 * n + c + 1)
                    v.scalar_tensor_tensor(out=parts[:, n % 2, 1, c * QC:(c + 1) * QC], in0=B[2 + c % 2][:, :],
                                           scalar=cols[:, 2 + n // 2, n % 2:n % 2 + 1],
                                           in1=parts[:, n % 2, 0, c * QC:(c + 1) * QC],
                                           op0=ALU.add, op1=ALU.subtract).then_inc(qk_lo, 1)
            v.memset(k_stack[HROWS:HROWS + 1, :, :], 1.0).then_inc(ones_row, 1)
            for t in range(T):
                dve.wait_ge(v_done, t + 1)
                v.tensor_tensor(V[:, t, :], B[4 + t % 2][:, 0:D], rows[:, 1, :], ALU.add).then_inc(v_kept, 1)

            NC = N // QC

            DIVIDE_STEPS = (9, 13, 16, 19, 21)

            def read_max(u, k):
                kind, i = RING[k]
                if kind == "row":
                    return
                m = PAIRS * u + i
                dve.wait_ge(max_mm, m + 1)
                v.tensor_reduce(mx[:, i // 2, i % 2, :], wide[k % 2][:, :].rearrange("p (a n) -> p a n", a=2),
                                AX.X, ALU.max).then_inc(max_read, 1)
                if i % 8 == 7:
                    h = i // 8
                    hs = slice(4 * h, 4 * h + 4)
                    dve.wait_ge(max_read, m + 1)
                    link(v.tensor_reduce(nm[:, hs], mx[:, hs, :, :].rearrange("p n a b -> p n (a b)"), AX.X, ALU.max))
                    if u > 0:
                        dve.wait_ge(max_turned, 4 * (u - 1) + h + 1)
                    v.tensor_scalar(nm16[:, hs], nm[:, hs], -1.0, None, ALU.mult).then_inc(negmax, 1)

            def save_ctx(u):
                g, c = u // NC, u % NC
                dve.wait_ge(pv_done, T * (u + 1))
                v.tensor_copy(xT[:, g, c * QC:(c + 1) * QC], B[6]).then_inc(ctx_saved, 1)

            def invert_sums(u, q):
                dve.wait_ge(den_done, u + 1)
                if u > 0 and q == 0:
                    dve.wait_ge(ctx_kept, u)
                part = slice(q * P, (q + 1) * P)
                v.reciprocal(rden[:, part], B[7][:, part]).then_inc(sums_inverted, 1)

            def divide_ctx(u):
                g, c = u // NC, u % NC
                dve.wait_ge(sums_inverted, 4 * (u + 1))
                dve.wait_ge(ctx_saved, u + 1)
                part = xT[:, g, c * QC:(c + 1) * QC]
                v.tensor_tensor(part, part, rden, ALU.mult).then_inc(ctx_kept, 1)

            for k in range(len(RING)):
                read_max(0, k)
            for u in range(UNITS):
                for n in range(STEPS):
                    if u + 1 < UNITS:
                        for k in ring_at(n):
                            read_max(u + 1, k)
                    if n == 4 and u > 0:
                        save_ctx(u - 1)
                    if n in DIVIDE_STEPS[:-1] and u > 0:
                        invert_sums(u - 1, DIVIDE_STEPS.index(n))
                    if n == DIVIDE_STEPS[-1] and u > 0:
                        divide_ctx(u - 1)
            save_ctx(UNITS - 1)
            for q in range(4):
                invert_sums(UNITS - 1, q)
            divide_ctx(UNITS - 1)

            for t in range(T):
                step(v.tensor_tensor(Z[:, t, :], Z[:, t, :], rows[:, 2, :], ALU.add))
            settle()
            for t in range(T):
                dve.wait_ge(wo_done, t + 1)
                v.tensor_tensor(Z[:, t, :], B[t % 2][:, 0:D], Z[:, t, :], ALU.add).then_inc(x2_made, 1)
            dve.wait_ge(x2_made, T)
            norm_stats(Z)
            for t in range(T):
                step(normalise(H2, Z, t))
            settle()
            for t in range(T):
                step(v.tensor_tensor(H2[:, t, :], H2[:, t, :], rows[:, 3, :], ALU.mult))
            settle()
            for t in range(T):
                v.tensor_tensor(H2[:, t, :], H2[:, t, :], rows[:, 4, :], ALU.add).then_inc(rows_ready, 1)
            for t in range(T):
                step(v.tensor_tensor(X[:, t, :], X[:, t, :], Z[:, t, :], ALU.add))

            dve.wait_ge(lg_done, 1)
            for t in range(T):
                step(v.tensor_tensor(lg[:, t, :], B[2][:, t * EXPERTS:(t + 1) * EXPERTS], rb_bc[:, :], ALU.add))
            settle()
            for t in range(T):
                step(v.max(top[:, t, :], lg[:, t, :]))
            settle()
            for t in range(T):
                step(v.max_index(topi[:, t, :], top[:, t, :], lg[:, t, :]))
            settle()
            link(v.tensor_copy(topf[:, :, :], topi[:, :, :]))
            ids = eid[:, :].unsqueeze(1).to_broadcast((P, T, EXPERTS))
            offs = eoff[:, :].unsqueeze(1).to_broadcast((P, T, EXPERTS))
            for s in range(TOPK):
                step(v.tensor_tensor(chosen[:, s, :, :], topf[:, :, s:s + 1].to_broadcast((P, T, EXPERTS)), ids, ALU.is_equal))
            settle()
            step(v.tensor_tensor(sel16[:, :, :], chosen[:, 0], chosen[:, 1], ALU.add))
            step(v.memset(pre[:, :, 0:1, :], 0.0))
            step(v.tensor_tensor(pre[:, 0, 1:T, :], chosen[:, 0, 0:T - 1], chosen[:, 1, 0:T - 1], ALU.add))
            settle()
            a, s = 0, 1
            while s < T:
                step(v.tensor_copy(pre[:, 1 - a, 0:s, :], pre[:, a, 0:s, :]))
                step(v.tensor_tensor(pre[:, 1 - a, s:T, :], pre[:, a, s:T, :], pre[:, a, 0:T - s, :], ALU.add))
                settle()
                a, s = 1 - a, 2 * s
            v.tensor_copy(pre16[:, :, :], pre[:, a]).then_inc(sel_made, 1)
            dve.wait_ge(pos_done, 1)
            pos = B[3][:, 0:T * EXPERTS].rearrange("p (t e) -> p t e", t=T)
            step(v.scalar_tensor_tensor(out=kept[:, :, :], in0=pos, scalar=float(CAP), in1=sel16[:, :, :],
                                        op0=ALU.is_le, op1=ALU.mult))
            step(v.tensor_tensor(val[:, :, :], pos, offs, ALU.add))
            settle()
            link(v.tensor_tensor(val[:, :, :], val[:, :, :], kept[:, :, :], ALU.mult))
            link(v.tensor_reduce(slot[:, :], val[:, :, :], AX.X, ALU.max))
            link(v.tensor_scalar(slot_off[:, :], slot[:, :], 0.0, float(SKIP), ALU.is_equal, ALU.mult))
            link(v.tensor_tensor(slot_sc[:, :], slot[:, :], slot_off[:, :], ALU.add))
            step(v.tensor_copy(slot_g[:, :], slot[:, :]))
            settle()
            v.tensor_copy(slot_s[:, :], slot_sc[:, :]).then_inc(slots_made, 1)

            def weight_lo(e, q):
                part = slice(q * 1024, (q + 1) * 1024)
                dve.wait_ge(w_hi, 4 * e + q + 1)
                v.scalar_tensor_tensor(out=w_split[e % 2][:, 1, part], in0=w_land[e % 2][:, part], scalar=WSCALE,
                                       in1=w_split[e % 2][:, 0, part], op0=ALU.mult, op1=ALU.subtract).then_inc(w_lo, 1)

            def x_lo(e):
                for k in range(KT):
                    dve.wait_ge(xe_hi, 2 * e + k + 1)
                    v.tensor_tensor(xeT[e % 2][:, 1, k, :], B[k][:, 0:CAP], xeT[e % 2][:, 0, k, :],
                                    ALU.subtract).then_inc(xe_lo, 1)

            def keep_y(e, i):
                r = tile_rows[i]
                dve.wait_ge(y_turned, 4 * e + i + 1)
                if i == 0 and e >= 2:
                    dve.wait_ge(y_out[e % 2], 32 * (e // 2))
                v.tensor_copy(yrow[e % 2][0:r, i, :], B[6 + (4 * e + i) % 2][0:r, 0:D]).then_inc(y_kept, 1)

            for q in range(4):
                weight_lo(0, q)
            x_lo(0)
            for e in range(EXPERTS):
                for f in range(FT):
                    m = e * FT + f
                    dve.wait_ge(hid_hi, m + 1)
                    v.tensor_tensor(hid[e % 2][:, 1, f, :], hid32[m % 2], hid[e % 2][:, 0, f, :],
                                    ALU.subtract).then_inc(hid_lo, 1)
                    if 1 <= f <= 4 and e > 0:
                        keep_y(e - 1, f - 1)
                if e + 1 < EXPERTS:
                    x_lo(e + 1)
                    for q in range(4):
                        weight_lo(e + 1, q)
                for d in range(KT):
                    dve.wait_ge(f2_done, KT * e + d + 1)
                    if e > 0:
                        dve.wait_ge(y_turned, 4 * e)
                    v.tensor_scalar(yT[:, d, :], B[4 + d][:, 0:CAP], 1.0 / WSCALE, b2c[:, e, d:d + 1],
                                    ALU.mult, ALU.add).then_inc(f2_kept, 1)
            for i in range(4):
                keep_y(EXPERTS - 1, i)
            settle()
            for t in range(T):
                if t % 4 == 0:
                    dve.wait_ge(gathered[t // 4], 16 * 4)
                v.tensor_tensor(X[:, t, :], X[:, t, :], YG[:, t, :], ALU.add).then_inc(summed, 1)


_INS = ['x', 'adj', 'L0_gnn_W_sa', 'L0_gnn_a_sa', 'L0_gnn_W_gcnb', 'L0_gnn_b_gcnb', 'L0_gnn_Wa', 'L0_gnn_ba',
        'L0_gnn_Wb', 'L0_gnn_bb', 'L0_ffn_ln1_g', 'L0_ffn_ln1_b', 'L0_ffn_ln2_g', 'L0_ffn_ln2_b', 'L0_ffn_wq',
        'L0_ffn_bq', 'L0_ffn_wk', 'L0_ffn_bk', 'L0_ffn_wv', 'L0_ffn_bv', 'L0_ffn_wo', 'L0_ffn_bo',
        'L0_ffn_router_w', 'L0_ffn_router_b', 'L0_ffn_w1', 'L0_ffn_b1', 'L0_ffn_w2', 'L0_ffn_b2']


def kernel(**inputs):
    import numpy as _np
    import concourse.bacc as _bacc
    from concourse import mybir as _mybir
    from concourse.bass_utils import run_bass_kernel_spmd as _run

    nc = _bacc.Bacc("TRN2", target_bir_lowering=False, num_devices=1)
    arrays, args = {}, []
    for name in _INS:
        a = _np.ascontiguousarray(inputs[name])
        arrays[f"in_{name}_dram"] = a
        args.append(nc.dram_tensor(f"in_{name}_dram", a.shape, _mybir.dt.from_np(a.dtype), kind="ExternalInput").ap())
    args.append(nc.dram_tensor("out_dram", (N, D), _mybir.dt.from_np(_np.dtype("float32")), kind="ExternalOutput").ap())
    gnn_moe_kernel(nc, *args)
    r = _run(nc, [arrays], core_ids=[0])
    return r.results[0]["out_dram"]
```

```python
from contextlib import ExitStack

import concourse.bass as bass
from concourse import mybir

ALU = mybir.AluOpType
ACT = mybir.ActivationFunctionType
AX = mybir.AxisListType
F32 = mybir.dt.float32
F16 = mybir.dt.float16
U32 = mybir.dt.uint32

P = 128
N, D = 2048, 256
T, KT = N // P, D // P
HEADS, DK = 8, 32
FF, EXPERTS, TOPK = 1024, 8, 2
FT = FF // P
CAP = -(-N * 16 // (10 * EXPERTS))
SLOTS = EXPERTS * CAP
WSCALE = 64.0
ESCALE = 1024.0
SKIP = 2 * 4096
EPS = 1e-5
LEAK = 0.01
SCALE = 1.0 / float(DK) ** 0.5
QC = 512
PAIR = 2
BANK = 512
HROWS = 3 * DK


def gnn_moe_kernel(nc: bass.Bass, x, adj, W_sa, a_sa, W_gcnb, b_gcnb, Wa, ba, Wb, bb,
                   ln1_g, ln1_b, ln2_g, ln2_b, wq, bq, wk, bk, wv, bv, wo, bo,
                   router_w, router_b, w1, b1, w2, b2, out):
    with ExitStack() as ctx:
        def sb(name, shape, dt=F32):
            return ctx.enter_context(nc.sbuf_tensor(name, shape, dt))

        def sem(name):
            return ctx.enter_context(nc.semaphore(name))

        moe_in = nc.dram_tensor("moe_in", (SLOTS + 1, D), F32, kind="Internal").ap()
        moe_x = nc.dram_tensor("moe_x", (SLOTS + 1, D + 1), F32, kind="Internal").ap()

        XI = sb("XI", [P, T, D + 2])
        X, token = XI[:, :, 0:D], XI[:, :, D:D + 1].bitcast(U32)
        Z = sb("Z", [P, T, D])
        T3 = sb("T3", [P, KT * N])
        R1 = sb("R1", [P, 16384])
        R2 = sb("R2", [P, 12736])
        xT = T3[:, :].rearrange("p (k n) -> p k n", k=KT)

        zT = T3[:, :].bitcast(F16).rearrange("p (s k n) -> p s k n", s=2, k=KT)

        adj_rows = R1[:, :].rearrange("p (b i n) -> p b i n", b=4, i=PAIR)
        stacks = R1[:, :].bitcast(F16).rearrange("p (s h n) -> p s h n", s=2, h=HEADS)
        q_stack, k_stack = stacks[:, 0], stacks[:, 1]
        NB = R1[:, T * D:2 * T * D].rearrange("p (t d) -> p t d", t=T)
        w_land = [R1[:, 8192 + b * 4096:8192 + (b + 1) * 4096] for b in range(2)]
        w_split = [R1[:, o:o + 4096].bitcast(F16).rearrange("p (s n) -> p s n", s=2) for o in (4096, 0)]
        w1_of = [w[:, :, 0:2048].rearrange("p s (k f) -> p s k f", k=KT) for w in w_split]
        w2_of = [w[:, :, 2048:4096].rearrange("p s (f d) -> p s f d", f=FT) for w in w_split]

        HW = D + 2
        GW = D + 2
        H = R2[:, 0:T * HW].bitcast(F16).rearrange("p (s t d) -> p s t d", s=2, t=T)
        o = T * HW
        G = R2[:, o:o + T * GW].bitcast(F16).rearrange("p (s t d) -> p s t d", s=2, t=T)
        o += T * GW
        neg_sl = R2[:, o:o + N]
        o += N
        xa = R2[:, o:o + PAIR * HW].rearrange("p (i d) -> p i d", i=PAIR)
        o += PAIR * HW
        xb = R2[:, o:o + PAIR * GW].rearrange("p (i d) -> p i d", i=PAIR)
        assert o + PAIR * GW <= 12736
        V = R2[:, 0:T * D].rearrange("p (t d) -> p t d", t=T)
        PTK = 4
        PT = R2[:, 4096:4096 + PTK * 4 * QC].rearrange("p (s n) -> p s n", s=PTK)
        parts = [R2[:, o:o + 2048].bitcast(F16).rearrange("p (s n) -> p s n", s=2) for o in (4096, 6144, 8192, 10240)]
        N2 = R1[:, 0:T * D].rearrange("p (t d) -> p t d", t=T)
        HIDN = FT * CAP
        hid = [R2[:, b * HIDN:(b + 1) * HIDN].bitcast(F16).rearrange("p (s f n) -> p s f n", s=2, f=FT) for b in range(2)]
        hid32 = [R2[:, 2 * HIDN + b * CAP:2 * HIDN + (b + 1) * CAP] for b in range(2)]
        o = 2 * HIDN + 2 * CAP
        yrow = [R2[:, o + b * 1024:o + (b + 1) * 1024].rearrange("p (t d) -> p t d", t=4) for b in range(2)]
        o += 2048
        xslot = [R2[:, o + b * 4 * (D + 1):o + (b + 1) * 4 * (D + 1)].rearrange("p (t d) -> p t d", t=4) for b in range(2)]
        assert o + 8 * (D + 1) <= 12736
        xrow = [T3[:, b * 1024:(b + 1) * 1024].rearrange("p (t d) -> p t d", t=4) for b in range(2)]
        xeT = [T3[:, 2048 + b * KT * CAP:2048 + (b + 1) * KT * CAP].bitcast(F16).rearrange(
            "p (s k n) -> p s k n", s=2, k=KT) for b in range(2)]

        WA, WB = D + 2, D + 4
        WG = sb("WG", [P, KT, WA + WB])
        wqkvo = sb("wqkvo", [P, 4, KT, D])
        rw = sb("rw", [P, KT, EXPERTS])
        rows = sb("rows", [P, 5, D])
        rb_bc = sb("rb_bc", [P, EXPERTS])
        gate_b = sb("gate_b", [P, 2])
        cols = sb("cols", [P, 6, KT])
        b1c = sb("b1c", [P, EXPERTS, FT])
        b2c = sb("b2c", [P, EXPERTS, KT])
        identf = sb("identf", [P, P])
        ident16 = sb("ident16", [P, P], F16)
        tri16 = sb("tri16", [P, P], F16)
        ones16 = sb("ones16", [P, P], F16)
        onesf = sb("onesf", [P, DK])
        blank = sb("blank", [P, D + 1])
        zeros = blank[:, 0:D]
        half = sb("half", [P, T])
        stats = sb("stats", [P, T, 6])
        mv = sb("mv", [P, T, 2])
        veps = sb("veps", [P, T])
        rstd = sb("rstd", [P, T])
        sc = sb("sc", [P, T, 2])
        neg_sr = sb("neg_sr", [P, T])
        u2 = sb("u2", [P, T, 2])
        junk = sb("junk", [P, D])
        scratch = sb("scratch", [P, 5888])
        W = scratch[:, 0:2048].rearrange("p (b n) -> p b n", b=4)
        E16 = scratch[:, 2048:3584].bitcast(F16).rearrange("p (b s n) -> p b s n", b=3, s=2)
        Ab = scratch[:, 3584:4352].bitcast(F16).rearrange("p (b n) -> p b n", b=3)
        gv = scratch[:, 4352:5888].rearrange("p (i s n) -> p i s n", i=PAIR, s=3)
        wsl_bc = W[:, 0, 0:KT * P].rearrange("p (k n) -> p k n", k=KT)
        a_bc = W[:, 1, :]
        WG16 = scratch[:, 2048:2048 + KT * (WA + WB)].bitcast(F16).rearrange("p (s k n) -> p s k n", s=2, k=KT)
        wsl16 = scratch[:, 3584:3584 + KT * P].bitcast(F16).rearrange("p (s k n) -> p s k n", s=2, k=KT)
        rden = scratch[:, 2048:2560]
        p_sum = scratch[:, 0:2048]
        qk32 = scratch[:, 4608:5632].rearrange("p (b n) -> p b n", b=2)
        yT = scratch[:, 2048:2048 + KT * CAP].rearrange("p (k n) -> p k n", k=KT)
        gt = sb("gt", [P, PAIR, 8])
        mx = sb("mx", [P, 16, 2, 2])
        nm = sb("nm", [P, 16])
        nm16 = sb("nm16", [P, 16], F16)
        small = gv[:, :, :, :].rearrange("p a b c -> p (a b c)")

        def piece(at, words):
            return small[:, at * P:at * P + words]

        lg = piece(0, P).rearrange("p (t e) -> p t e", t=T)
        top = piece(1, P).rearrange("p (t e) -> p t e", t=T)
        topi = piece(2, P).bitcast(U32).rearrange("p (t e) -> p t e", t=T)
        topf = piece(3, P).rearrange("p (t e) -> p t e", t=T)
        chosen = piece(4, 2 * P).rearrange("p (s t e) -> p s t e", s=2, t=T)
        kept = piece(8, P).rearrange("p (t e) -> p t e", t=T)
        val = piece(9, P).rearrange("p (t e) -> p t e", t=T)
        sel16 = piece(10, P // 2).bitcast(F16).rearrange("p (t e) -> p t e", t=T)
        pre16 = piece(11, P // 2).bitcast(F16).rearrange("p (t e) -> p t e", t=T)
        eid = sb("eid", [P, EXPERTS])
        eoff = sb("eoff", [P, EXPERTS])
        slot = sb("slot", [P, T])
        slot_off = sb("slot_off", [P, T])
        slot_sc = sb("slot_sc", [P, T])
        slot_s = sb("slot_s", [P, T], U32)

        wide = [ctx.enter_context(nc.psum_tensor(f"wide{i}", [P, 2 * BANK], F32)) for i in range(2)]
        B = [wide[i // 2][:, i % 2 * BANK:(i % 2 + 1) * BANK] for i in range(4)]
        B += [ctx.enter_context(nc.psum_tensor(f"B{i}", [P, BANK], F32))[:, :] for i in range(4, 8)]

        x_in = [sem(f"x_in{i}") for i in range(4)]
        adj_in = [sem(f"adj_in{i}") for i in range(4)]
        gnn_w_in, block_w_in, bias_in, experts_b_in = sem("gnn_w_in"), sem("block_w_in"), sem("bias_in"), sem("experts_b_in")
        moe_zeroed = sem("moe_zeroed")
        const_made = sem("const_made")
        pool_step = sem("pool_step")
        rstd_made = sem("rstd_made")
        var_made = sem("var_made")
        dve_step = sem("dve_step")
        rows_ready = sem("rows_ready")
        turned = sem("turned")
        turned_kept = sem("turned_kept")
        z_lo = sem("z_lo")
        wg_summed = sem("wg_summed")
        wg_hi = sem("wg_hi")
        wg_lo = sem("wg_lo")
        proj_done = sem("proj_done")
        proj_act = sem("proj_act")
        proj_dve = sem("proj_dve")
        sl_done = sem("sl_done")
        sl_kept = sem("sl_kept")
        adjT_done = sem("adjT_done")
        adjT_kept = sem("adjT_kept")
        s_made = sem("s_made")
        logit_made = sem("logit_made")
        e_made = sem("e_made")
        e_masked = sem("e_masked")
        e_hi = sem("e_hi")
        e_lo = sem("e_lo")
        neg_sr_made = sem("neg_sr_made")
        gnn_mm = sem("gnn_mm")
        gate_v = sem("gate_v")
        gate_e = sem("gate_e")
        gnn_v = sem("gnn_v")
        gnn_e = sem("gnn_e")
        gnn_read_act = sem("gnn_read_act")
        gnn_read_dve = sem("gnn_read_dve")
        xb_made = sem("xb_made")
        gnn_half = sem("gnn_half")
        x1_made = sem("x1_made")
        qk_done = sem("qk_done")
        qk_hi = sem("qk_hi")
        qk_lo = sem("qk_lo")
        qk_kept = sem("qk_kept")
        qk_lo2 = sem("qk_lo2")
        v_copied = sem("v_copied")
        stacked = [sem(f"stacked{i}") for i in range(5)]
        v_done = sem("v_done")
        v_kept = sem("v_kept")
        ones_row = sem("ones_row")
        max_mm = sem("max_mm")
        max_read = sem("max_read")
        negmax = sem("negmax")
        max_turned = sem("max_turned")
        max_placed = sem("max_placed")
        s_mm = sem("s_mm")
        p_made = sem("p_made")
        pv_done = sem("pv_done")
        ctx_saved = sem("ctx_saved")
        ctx_kept = sem("ctx_kept")
        last_ctx_kept = sem("last_ctx_kept")
        p_summed = sem("p_summed")
        den_done = sem("den_done")
        sums_inverted = sem("sums_inverted")
        wo_done = sem("wo_done")
        x2_made = sem("x2_made")
        h2_pool = sem("h2_pool")
        h2_dve = sem("h2_dve")
        normed = sem("normed")
        x12_pool = sem("x12_pool")
        lg_read = sem("lg_read")
        pos_read = sem("pos_read")
        lg_done = sem("lg_done")
        sel_made = sem("sel_made")
        pos_done = sem("pos_done")
        slots_made = sem("slots_made")
        scattered = [sem(f"scattered{i}") for i in range(4)]
        w_in = [sem(f"w_in{i}") for i in range(2)]
        w_hi = sem("w_hi")
        w_lo = sem("w_lo")
        hid_hi = sem("hid_hi")
        hid_lo = sem("hid_lo")
        xe_hi = sem("xe_hi")
        xe_in = [sem(f"xe_in{i}") for i in range(2)]
        xe_turned = sem("xe_turned")
        xe_lo = sem("xe_lo")
        f1_done = sem("f1_done")
        f1_kept = sem("f1_kept")
        f2_done = sem("f2_done")
        f2_kept = sem("f2_kept")
        y_turned = sem("y_turned")
        y_kept = sem("y_kept")
        y_out = [sem(f"y_out{i}") for i in range(2)]
        x_scattered = sem("x_scattered")
        xs_in = [sem(f"xs_in{i}") for i in range(2)]
        x12_dve = sem("x12_dve")
        stored = sem("stored")

        xv = x.rearrange("(t p) d -> p t d", p=P)
        outv = out.rearrange("(t p) d -> p t d", p=P)
        CH = T // PAIR
        JP = T // 2
        UNITS = (HEADS // 4) * (N // QC)
        SUM_KT = (0, 1, 2, 3, 4, 6, 8, 9, 10, 12, 13, 14)
        PE_KT = (5, 7, 11, 15)
        DVE_SUMS = (5, 10)
        SUM_OPS = len(SUM_KT) - 1
        STEPS = 4 * T
        PAIRS = 32
        RING = [("scores", i) for i in range(PAIRS)]
        for h in range(4):
            RING.insert(min(8 * (h + 1) + 2 + h, PAIRS + h), ("row", h))

        RING_STEPS = (0, 2, 3, 4, 5, 6, 7, 8, 9, 13, 14, 16, 17, 20, 22, 24, 26, 29, 29, 32, 34, 34, 37, 37,
                      41, 41, 45, 45, 48, 49, 50, 53, 53, 57, 57, 62)
        assert len(RING_STEPS) == len(RING)

        def ring_at(n):
            return [k for k in range(len(RING)) if RING_STEPS[k] == n]

        def ring_readers(u, k):
            if k < 2:
                u, k = u - 1, k + len(RING)
            if u < 0:
                return None
            kind, i = RING[k - 2]
            return (kind, PAIRS * u + i + 1) if kind == "scores" else (kind, 4 * u + i + 1)

        H_BANK, G_BANK = (2, 3, 6), (4, 5, 7)
        QK_JOBS = [(0, 0, 0)] + [(1, 0, c) for c in range(4)] + [(0, 0, c) for c in range(1, 4)]
        QK_JOBS += [(1, 1, c) for c in range(4)] + [(0, 1, c) for c in range(4)]
        TURN_JOBS = (2, 4)
        V_GAP = 4
        STACKS = ((0, 0, 0, 1, 1), (1, 0, 0, 4, 5), (0, 0, 1, 4, 8), (1, 1, 0, 4, 12), (0, 1, 0, 4, 16))

        def part_of(s, g):
            return parts[2 * g + 1 - s]

        V_EARLY = 6
        SIDE_JOBS = [("v", t) for t in range(V_EARLY, T)] + [("qk", m) for m in range(8, 16)]

        def side_jobs(k):
            return [job for j, job in enumerate(SIDE_JOBS) if j * 34 // len(SIDE_JOBS) == k]

        TC = QC // P
        CHUNKS = N // QC

        def stage_of(n, first):
            c = (n - first) // 14
            return c if n >= first and (n - first) % 14 == 0 and c < CHUNKS - 1 else None

        WO_STEP, STATS_STEP, NORM_STEP, TURN_STEP, ROUTER_STEP, TOP_STEP, POS_STEP, SLOT_STEP = 2, 6, 10, 22, 25, 28, 31, 34

        full = CAP // P
        rest = CAP - full * P
        tile_rows = [P] * full + [rest]

        def column(v):
            return v.rearrange("(k p) -> p k", p=P)

        block = ctx.enter_context(nc.Block())

        @block.sync
        def _(sp):
            with nc.allow_non_contiguous_dma(reason="small vectors"):
                def load_x(i):
                    sp.dma_start(X[:, 4 * i:4 * i + 4, :], xv[:, 4 * i:4 * i + 4, :]).then_inc(x_in[i], 16)

                load_x(0)
                load_x(1)
                sp.dma_start(WG[:, :, 0:D], W_sa.rearrange("(k p) d -> p k d", p=P)).then_inc(gnn_w_in, 16)
                sp.dma_start(WG[:, :, WA:WA + D], W_gcnb.rearrange("(k p) d -> p k d", p=P)).then_inc(gnn_w_in, 16)
                for w, at in ((Wa, 0), (Wb, 1)):
                    wv_ = w.rearrange("o (s k p) -> p (o s) k", s=2, p=P)
                    for s in range(2):
                        for k in range(KT):
                            c = WA + D + 2 * s + at
                            sp.dma_start(WG[:, k, c:c + 1], wv_[:, s, k:k + 1]).then_inc(gnn_w_in, 16)
                sp.dma_start(a_bc, a_sa.to_broadcast((P, 2 * D))).then_inc(gnn_w_in, 16)
                sp.dma_start(gate_b[:, 0:1], ba.rearrange("(o d) -> o d", o=1).to_broadcast((P, 1))).then_inc(gnn_w_in, 16)
                sp.dma_start(gate_b[:, 1:2], bb.rearrange("(o d) -> o d", o=1).to_broadcast((P, 1))).then_inc(gnn_w_in, 16)
                load_x(2)
                load_x(3)
                for c in range(CH):
                    if c >= 4:
                        sp.wait_ge(adjT_done, (c - 3) * JP)
                    sp.dma_start(adj_rows[:, c % 4],
                                 adj.rearrange("(c i p) n -> c p i n", i=PAIR, p=P)[c]).then_inc(adj_in[c % 4], 16)
                    if c == 1:
                        for i, b in enumerate((b_gcnb, bv, bo, ln2_g, ln2_b)):
                            sp.dma_start(rows[:, i, :], b.rearrange("(o d) -> o d", o=1).to_broadcast((P, D))).then_inc(bias_in, 16)
                        sp.dma_start(rb_bc[:, :], router_b.rearrange("(o d) -> o d", o=1).to_broadcast((P, EXPERTS))).then_inc(bias_in, 16)
                        for i, b in enumerate((ln1_g, ln1_b, bq, bk, ln2_g, ln2_b)):
                            sp.dma_start(cols[:, i, :], column(b)).then_inc(bias_in, 16)
                    if c == 3:
                        for i, w in enumerate((wq, wk, wv, wo)):
                            sp.dma_start(wqkvo[:, i], w.rearrange("(k p) d -> p k d", p=P)).then_inc(block_w_in, 16)
                        sp.dma_start(rw[:, :, :], router_w.rearrange("(k p) e -> p k e", p=P)).then_inc(block_w_in, 16)
                        for e in range(EXPERTS):
                            sp.dma_start(b1c[:, e, :], column(b1[e])).then_inc(experts_b_in, 16)
                            sp.dma_start(b2c[:, e, :], column(b2[e])).then_inc(experts_b_in, 16)
                sp.wait_ge(const_made, 10)
                full_rows = (SLOTS + 1) // P * P
                sp.dma_start(moe_in[0:full_rows].rearrange("(t p) d -> p t d", p=P),
                             zeros.unsqueeze(1).to_broadcast((P, full_rows // P, D))).then_inc(moe_zeroed, 16)
                sp.dma_start(moe_in[full_rows:SLOTS + 1], zeros[0:SLOTS + 1 - full_rows, :]).then_inc(moe_zeroed, 16)
                sp.dma_start(moe_x[0:full_rows].rearrange("(t p) d -> p t d", p=P),
                             blank[:, :].unsqueeze(1).to_broadcast((P, full_rows // P, D + 1))).then_inc(moe_zeroed, 16)
                sp.dma_start(moe_x[full_rows:SLOTS + 1], blank[0:SLOTS + 1 - full_rows, :]).then_inc(moe_zeroed, 16)
                sp.wait_ge(adjT_done, CH * JP)
                sp.dma_start(k_stack[HROWS:HROWS + 1, :, :].rearrange("o h (a b) -> o (h a) b", b=P),
                             ones16[0:1, :].unsqueeze(1).to_broadcast((1, HEADS * N // P, P))).then_inc(ones_row, 16)
                for i, (s, g, c0, c1, made) in enumerate(STACKS):
                    sp.wait_ge(qk_hi, made)
                    if made <= 8:
                        sp.wait_ge(qk_lo, made)
                    else:
                        sp.wait_ge(qk_lo2, made - 8)
                    cs = slice(c0 * QC, c1 * QC)
                    for j in range(4):
                        for r, part in enumerate(((0, 0, 1), (0, 1, 0))[s]):
                            sp.dma_start(stacks[r * DK:(r + 1) * DK, s, 4 * g + j, cs],
                                         part_of(s, g)[j * DK:(j + 1) * DK, part, cs]).then_inc(stacked[i], 16)

                def load_w(e):
                    sp.dma_start(w_land[e % 2][:, 0:2048].rearrange("p (k f) -> p k f", k=KT),
                                 w1[e].rearrange("(k p) f -> p k f", p=P)).then_inc(w_in[e % 2], 16)
                    sp.dma_start(w_land[e % 2][:, 2048:4096].rearrange("p (f d) -> p f d", f=FT),
                                 w2[e].rearrange("(f p) d -> p f d", p=P)).then_inc(w_in[e % 2], 16)

                def load_xe(e):
                    r = 1 + e * CAP
                    sp.dma_start(xrow[e % 2][:, 0:full, :],
                                 moe_in[r:r + full * P].rearrange("(t p) d -> p t d", p=P)).then_inc(xe_in[e % 2], 16)
                    sp.dma_start(xrow[e % 2][0:rest, full, :], moe_in[r + full * P:r + CAP]).then_inc(xe_in[e % 2], 16)

                def load_xslot(e):
                    if e >= 2:
                        sp.wait_ge(y_out[e % 2], 16 * 4 * (e // 2))
                    r = 1 + e * CAP
                    sp.dma_start(xslot[e % 2][:, 0:full, :],
                                 moe_x[r:r + full * P].rearrange("(t p) d -> p t d", p=P)).then_inc(xs_in[e % 2], 16)
                    sp.dma_start(xslot[e % 2][0:rest, full, :], moe_x[r + full * P:r + CAP]).then_inc(xs_in[e % 2], 16)

                sp.wait_ge(s_mm, UNITS // 2 * STEPS)
                load_w(0)
                sp.wait_ge(s_mm, UNITS * STEPS)
                load_w(1)
                for i in range(4):
                    sp.wait_ge(scattered[i], 16 * 4)
                sp.wait_ge(lg_done, CHUNKS)
                load_xe(0)
                load_xe(1)
                sp.wait_ge(x12_pool, T - TC)
                sp.wait_ge(x12_dve, TC)
                for i in range(4):
                    sp.dma_start(outv[:, 4 * i:4 * i + 4, :], X[:, 4 * i:4 * i + 4, :]).then_inc(stored, 16)
                sp.wait_ge(x_scattered, 16 * T)
                load_xslot(0)
                load_xslot(1)
                for e in range(EXPERTS):
                    if e + 2 < EXPERTS:
                        sp.wait_ge(w_hi, 4 * (e + 1))
                        sp.wait_ge(w_lo, 4 * (e + 1))
                        load_w(e + 2)
                        sp.wait_ge(xe_turned, 2 * (e + 1))
                        load_xe(e + 2)
                    if e > 0 and e + 1 < EXPERTS:
                        load_xslot(e + 1)
                sp.wait_ge(stored, 64)
                for b in range(2):
                    sp.wait_ge(y_out[b], 16 * 4 * EXPERTS // 2)

        @block.gpsimd
        def _(pool):
            nc.gpsimd.memset(identf[:, :], 0.0).then_inc(pool_step, 1)
            nc.gpsimd.memset(tri16[:, :], 1.0).then_inc(pool_step, 1)
            nc.gpsimd.memset(zeros[:, :], 0.0).then_inc(const_made, 1)
            nc.gpsimd.memset(ones16[:, :], 1.0).then_inc(const_made, 1)
            nc.gpsimd.memset(onesf[:, :], 1.0).then_inc(const_made, 1)
            nc.gpsimd.memset(half[:, :], -0.5).then_inc(const_made, 1)
            nc.gpsimd.iota(eid[:, :], [[1, EXPERTS]], base=0, channel_multiplier=0,
                           allow_small_or_imprecise_dtypes=True).then_inc(const_made, 1)
            nc.gpsimd.iota(eoff[:, :], [[CAP, EXPERTS]], base=0, channel_multiplier=0,
                           allow_small_or_imprecise_dtypes=True).then_inc(const_made, 1)
            nc.gpsimd.iota(token, [[P, T], [0, 1]], base=0, channel_multiplier=1).then_inc(const_made, 1)
            nc.gpsimd.iota(blank[:, D:D + 1].bitcast(U32), [[0, 1]], base=SKIP, channel_multiplier=0).then_inc(const_made, 1)
            pool.wait_ge(pool_step, 2)
            nc.gpsimd.affine_select(out=identf[:, :], in_=identf[:, :], compare_op=ALU.not_equal, fill=1.0,
                                    base=0, pattern=[[-1, P]], channel_multiplier=1).then_inc(pool_step, 1)
            nc.gpsimd.affine_select(out=tri16[:, :], in_=tri16[:, :], compare_op=ALU.is_ge, fill=0.0,
                                    base=0, pattern=[[1, P]], channel_multiplier=-1).then_inc(const_made, 1)
            pool.wait_ge(pool_step, 3)
            nc.gpsimd.tensor_copy(ident16[:, :], identf[:, :]).then_inc(const_made, 1)
            pool.wait_ge(const_made, 10)
            n_var = [0]

            def inv_std(t0, t1):
                n_var[0] += 1
                pool.wait_ge(var_made, n_var[0])
                nc.gpsimd.tensor_tensor(rstd[:, t0:t1], veps[:, t0:t1], half[:, t0:t1], ALU.pow).then_inc(rstd_made, 1)

            for i in range(4):
                inv_std(4 * i, 4 * i + 4)

            def add_s(n):
                c, jp = n // JP, n % JP
                if n >= 4:
                    pool.wait_ge(e_lo, n - 3)
                nc.gpsimd.tensor_tensor(
                    W[:, n % 4, :].rearrange("p (j i) -> p j i", j=2),
                    neg_sl[:, c * PAIR * P:(c + 1) * PAIR * P].unsqueeze(1).to_broadcast((P, 2, PAIR * P)),
                    neg_sr[:, 2 * jp:2 * jp + 2].unsqueeze(2).to_broadcast((P, 2, PAIR * P)), ALU.add).then_inc(s_made, 1)

            def add_bias(c):
                pool.wait_ge(gnn_read_dve, (c + 1) * PAIR)
                nc.gpsimd.tensor_tensor(gv[:, :, 0, :], xb[:, :, 0:D],
                                        rows[:, 0, :].unsqueeze(1).to_broadcast((P, PAIR, D)), ALU.add).then_inc(xb_made, 1)

            def add_gnn(c):
                t0 = c * PAIR
                pool.wait_ge(gnn_e, c + 1)
                nc.gpsimd.tensor_scalar(gv[:, :, 2, :], gv[:, :, 2, :], 0.5, 0.5, ALU.mult, ALU.add).then_inc(gnn_half, 1)
                pool.wait_ge(gnn_half, c + 1)
                nc.gpsimd.tensor_tensor(X[:, t0:t0 + PAIR, :], X[:, t0:t0 + PAIR, :], gv[:, :, 2, :], ALU.add).then_inc(x1_made, 1)

            pool.wait_ge(neg_sr_made, 1)
            pool.wait_ge(bias_in, 192)
            pool.wait_ge(sl_kept, 4)
            for n in range(CH * JP):
                add_s(n)
                if n % JP == 4 and n > JP:
                    add_bias(n // JP - 1)
                if n % JP == 7 and n > JP:
                    add_gnn(n // JP - 1)
                if n % JP in (0, 3) and n >= 2 * JP:
                    inv_std((n // JP - 2) * PAIR, (n // JP - 1) * PAIR)
            for _ in range(2):
                inv_std((CH - 2) * PAIR, (CH - 1) * PAIR)
            add_bias(CH - 1)
            add_gnn(CH - 1)
            inv_std(T - PAIR, T)
            inv_std(T - PAIR, T)

            def add_bv(t):
                pool.wait_ge(v_copied, t + 1)
                nc.gpsimd.tensor_tensor(V[:, t, :], V[:, t, :], rows[:, 1, :], ALU.add).then_inc(v_kept, 1)

            pool.wait_ge(bias_in, 192)
            for t in range(V_EARLY):
                add_bv(t)
            for kind, m in SIDE_JOBS:
                if kind == "v":
                    add_bv(m)
                else:
                    s, g, c = QK_JOBS[m]
                    pool.wait_ge(qk_kept, m - 7)
                    cs = slice(c * QC, (c + 1) * QC)
                    nc.gpsimd.tensor_tensor(part_of(s, g)[:, 1, cs], qk32[:, m % 2, :], part_of(s, g)[:, 0, cs],
                                            ALU.subtract).then_inc(qk_lo2, 1)
            for u in range(UNITS - 1):
                for i in range(1, len(SUM_KT)):
                    if i in DVE_SUMS:
                        continue
                    if i == 1 and u > 0:
                        pool.wait_ge(den_done, u)
                    elif i > 1:
                        pool.wait_ge(p_summed, u * SUM_OPS + i - 1)
                    pool.wait_ge(p_made, STEPS * u + 4 * SUM_KT[i] + 4)
                    nc.gpsimd.tensor_tensor(p_sum, PT[:, SUM_KT[0] % PTK, :] if i == 1 else p_sum,
                                            PT[:, SUM_KT[i] % PTK, :], ALU.add).then_inc(p_summed, 1)

            def finish_h2(c):
                inv_std(c * TC, (c + 1) * TC)
                if c == CHUNKS - 1:
                    return
                pool.wait_ge(normed, (c + 1) * TC)
                for t in range(c * TC, (c + 1) * TC):
                    nc.gpsimd.tensor_tensor(X[:, t, :], X[:, t, :], Z[:, t, :], ALU.add).then_inc(x12_pool, 1)
                pool.wait_ge(x12_pool, (c + 1) * TC)
                for t in range(c * TC, (c + 1) * TC):
                    nc.gpsimd.tensor_tensor(Z[:, t, :], N2[:, t, :], rows[:, 3, :], ALU.mult).then_inc(pool_step, 1)
                pool.wait_ge(pool_step, 3 + (c + 1) * TC)
                for t in range(c * TC, (c + 1) * TC):
                    nc.gpsimd.tensor_tensor(Z[:, t, :], Z[:, t, :], rows[:, 4, :], ALU.add).then_inc(h2_pool, 1)

            def scatter(c):
                pool.wait_ge(slots_made, c + 1)
                if c < CHUNKS - 1:
                    pool.wait_ge(h2_pool, (c + 1) * TC)
                else:
                    pool.wait_ge(h2_dve, TC)
                for t in range(c * TC, (c + 1) * TC):
                    pool.indirect_dma_start(moe_in[:, :], bass.IndirectOffsetOnAxis(ap=slot_s[:, t:t + 1], axis=0),
                                            Z[:, t, :], None, bounds_check=SLOTS, oob_is_err=False).then_inc(scattered[c], 16)

            pool.wait_ge(moe_zeroed, 64)
            finish_h2(0)
            finish_h2(1)
            for c in range(CHUNKS):
                scatter(c)
                if c + 2 < CHUNKS:
                    finish_h2(c + 2)

            pool.wait_ge(x12_pool, T - TC)
            pool.wait_ge(x12_dve, TC)
            pool.wait_ge(xe_in[0], 32)
            for t in range(T):
                pool.indirect_dma_start(moe_x[:, :], bass.IndirectOffsetOnAxis(ap=slot_s[:, t:t + 1], axis=0),
                                        XI[:, t, 0:D + 1], None, bounds_check=SLOTS, oob_is_err=False).then_inc(x_scattered, 16)
            pool.wait_ge(stored, 64)
            for e in range(EXPERTS):
                for i, r in enumerate(tile_rows):
                    pool.wait_ge(y_kept, 4 * e + i + 1)
                    pool.indirect_dma_start(out[:, :], bass.IndirectOffsetOnAxis(
                        ap=xslot[e % 2][0:r, i, D:D + 1].bitcast(U32), axis=0),
                        yrow[e % 2][0:r, i, :], None, bounds_check=N - 1, oob_is_err=False).then_inc(y_out[e % 2], 16)

        @block.tensor
        def _(pe):
            mm = nc.tensor.matmul
            pe.wait_ge(const_made, 10)

            turn_n = [0]

            def turn_rows(src, ready0, c):
                pe.wait_ge(rows_ready, ready0 + 4 * (c + 1))
                for k in range(KT):
                    i = turn_n[0]
                    if i >= 2:
                        pe.wait_ge(turned_kept, i - 1)
                        pe.wait_ge(z_lo, min(i - 1, 8))
                    for j in range(4):
                        ins = nc.tensor.transpose(B[i % 2][:, j * P:(j + 1) * P],
                                                  src[:, 4 * c + j, k * P:(k + 1) * P], identf[:, :])
                    ins.then_inc(turned, 1)
                    turn_n[0] += 1

            PARTS = ((0, 0), (0, 1), (1, 0))

            def project(t):
                pe.wait_ge(turned_kept, 2 * (t // 4 + 1))
                pe.wait_ge(z_lo, 2 * (t // 4 + 1))
                if t >= 3:
                    pe.wait_ge(proj_act, 2 * (t - 2))
                    pe.wait_ge(proj_dve, t - 2)
                for lo, hi, b in ((0, WA, H_BANK[t % 3]), (WA, WA + WB, G_BANK[t % 3])):
                    for n, (a, q) in enumerate(PARTS):
                        for k in range(KT):
                            ins = mm(B[b][:, 0:hi - lo], zT[:, a, k, t * P:(t + 1) * P], WG16[:, q, k, lo:hi],
                                     start=(n == 0 and k == 0), stop=(n == 2 and k == KT - 1))
                ins.then_inc(proj_done, 1)

            turn_rows(Z, 0, 0)
            turn_rows(Z, 0, 1)
            pe.wait_ge(wg_hi, 2)
            pe.wait_ge(wg_lo, 2)
            for c in range(4):
                for t in range(4 * c, 4 * c + 4):
                    project(t)
                if c + 2 < 4:
                    turn_rows(Z, 0, c + 2)
            pe.wait_ge(proj_act, 2 * (T - 1))
            pe.wait_ge(proj_dve, T - 1)
            for c in range(4):
                if c >= 2:
                    pe.wait_ge(sl_kept, c - 1)
                for n, (a, q) in enumerate(PARTS):
                    for k in range(KT):
                        ins = mm(B[6 + c % 2][:, :], wsl16[:, a, k, :], zT[:, q, k, c * BANK:(c + 1) * BANK],
                                 start=(n == 0 and k == 0), stop=(n == 2 and k == KT - 1))
                ins.then_inc(sl_done, 1)

            def turn_adj(c, jp):
                n = c * JP + jp
                if jp == 0:
                    pe.wait_ge(adj_in[c % 4], 16 * (c // 4 + 1))
                if n >= 4:
                    pe.wait_ge(adjT_kept, n - 3)
                    pe.wait_ge(e_masked, n - 3)
                for j in range(2):
                    for i in range(PAIR):
                        ins = nc.tensor.transpose(B[n % 4][:, (j * PAIR + i) * P:(j * PAIR + i + 1) * P],
                                                  adj_rows[:, c % 4, i, (2 * jp + j) * P:(2 * jp + j + 1) * P], identf[:, :])
                ins.then_inc(adjT_done, 1)

            pe.wait_ge(proj_dve, T)
            pe.wait_ge(proj_act, 2 * T)
            pe.wait_ge(sl_kept, 4)
            for n in range(3):
                turn_adj(n // JP, n % JP)
            for c in range(CH):
                for jp in range(JP):
                    n = c * JP + jp
                    if n + 3 < CH * JP:
                        turn_adj((n + 3) // JP, (n + 3) % JP)
                    if jp == 0 and c > 0:
                        pe.wait_ge(gnn_read_act, c * PAIR)
                        pe.wait_ge(gnn_read_dve, c * PAIR)
                    pe.wait_ge(adjT_kept, n + 1)
                    pe.wait_ge(e_hi, n + 1)
                    pe.wait_ge(e_lo, n + 1)
                    for j in range(2):
                        jt = 2 * jp + j
                        for i in range(PAIR):
                            a = (j * PAIR + i) * P
                            mm(B[6 + i][:, 0:GW], Ab[:, n % 3, a:a + P], G[:, 0, jt, :], start=(jt == 0), stop=False)
                            mm(B[6 + i][:, 0:GW], Ab[:, n % 3, a:a + P], G[:, 1, jt, :], start=False, stop=(jt == T - 1))
                            for k, (r, q) in enumerate(((0, 0), (0, 1), (1, 0))):
                                ins = mm(B[4 + i][:, 0:D + 1], E16[:, n % 3, r, a:a + P], H[:, q, jt, 0:D + 1],
                                         start=(jt == 0 and k == 0), stop=(jt == T - 1 and k == 2))
                    ins.then_inc(gnn_mm, 1)

            for c in range(2):
                turn_rows(NB, T, c)
            pe.wait_ge(block_w_in, 80)
            pe.wait_ge(gnn_read_act, CH * PAIR)
            pe.wait_ge(gnn_read_dve, CH * PAIR)

            def make_qk(m):
                s, g, c = QK_JOBS[m]
                if m < 8:
                    pe.wait_ge(turned_kept, 8 + 2 * (c + 1))
                if m >= 2:
                    pe.wait_ge(qk_hi, m - 1)
                    if m < 10:
                        pe.wait_ge(qk_lo, m - 1)
                    else:
                        pe.wait_ge(qk_kept, m - 9)
                for k in range(KT):
                    ins = mm(B[4 + m % 2], wqkvo[:, s, k, g * P:(g + 1) * P], xT[:, k, c * QC:(c + 1) * QC],
                             start=(k == 0), stop=(k == KT - 1))
                ins.then_inc(qk_done, 1)

            def make_v(t):
                if t >= 2:
                    pe.wait_ge(v_copied, t - 1)
                for k in range(KT):
                    ins = mm(B[6 + t % 2][:, 0:D], xT[:, k, t * P:(t + 1) * P], wqkvo[:, 2, k, :],
                             start=(k == 0), stop=(k == KT - 1))
                ins.then_inc(v_done, 1)

            for m in range(8):
                if m in TURN_JOBS:
                    turn_rows(NB, T, TURN_JOBS.index(m) + 2)
                if m == 3:
                    for t in range(V_GAP):
                        make_v(t)
                make_qk(m)
            for t in range(V_GAP, V_EARLY):
                make_v(t)

            NC = N // QC

            def make_max(u, k):
                g, c = u // NC, u % NC
                kind, i = RING[k]
                reader = ring_readers(u, k)
                if reader is not None:
                    pe.wait_ge(max_read if reader[0] == "scores" else max_placed, reader[1])
                if kind == "scores":
                    h, qt, part = i // 8, i // 2 % 4, i % 2
                    q0 = c * QC + qt * P
                    for j in range(2):
                        k0 = (2 * part + j) * BANK
                        ins = mm(wide[k % 2][:, j * BANK:(j + 1) * BANK], q_stack[0:HROWS, 4 * g + h, q0:q0 + P],
                                 k_stack[0:HROWS, 4 * g + h, k0:k0 + BANK], start=True, stop=True)
                    ins.then_inc(max_mm, 1)
                else:
                    pe.wait_ge(negmax, 4 * u + i + 1)
                    for qt in range(4):
                        ins = mm(wide[k % 2][0:1, qt * P:(qt + 1) * P], nm16[:, 4 * i + qt:4 * i + qt + 1],
                                 ident16[:, :], start=True, stop=True)
                    ins.then_inc(max_turned, 1)

            def scores(u, n):
                g, c = u // NC, u % NC
                kt, h = n // 4, n % 4
                m = STEPS * u + n
                if m >= 2:
                    pe.wait_ge(p_made, m - 1)
                mm(B[4 + m % 2], k_stack[0:HROWS + 1, 4 * g + h, kt * P:(kt + 1) * P],
                   q_stack[0:HROWS + 1, 4 * g + h, c * QC:(c + 1) * QC], start=True, stop=True).then_inc(s_mm, 1)

            def sum_rows(src, first, last):
                for h in range(4):
                    ins = mm(B[7][h * DK:(h + 1) * DK, :], onesf[:, :], src[:, h * QC:(h + 1) * QC], start=first, stop=last)
                return ins

            def weigh(u, kt):
                g = u // NC
                pe.wait_ge(p_made, STEPS * u + 4 * kt + 4)
                if kt == 0 and u > 0:
                    pe.wait_ge(ctx_saved, u)
                if kt == PE_KT[0] and u > 0:
                    pe.wait_ge(sums_inverted, 4 * u)
                for h in range(4):
                    ins = mm(B[6][h * DK:(h + 1) * DK, :], V[:, kt, (4 * g + h) * DK:(4 * g + h + 1) * DK],
                             PT[:, kt % PTK, h * QC:(h + 1) * QC], start=(kt == 0), stop=(kt == T - 1))
                if kt in PE_KT:
                    ins = sum_rows(PT[:, kt % PTK, :], kt == PE_KT[0], False)
                ins.then_inc(pv_done, 1)

            def sum_p(u):
                pe.wait_ge(p_summed, (u + 1) * SUM_OPS)
                sum_rows(p_sum, False, True).then_inc(den_done, 1)

            def make_wo(t):
                pe.wait_ge(ctx_kept, UNITS - CHUNKS + t // TC + 1)
                if t >= 2:
                    pe.wait_ge(x2_made, t - 1)
                for k in range(KT):
                    ins = mm(B[t % 2][:, 0:D], xT[:, k, t * P:(t + 1) * P], wqkvo[:, 3, k, :],
                             start=(k == 0), stop=(k == KT - 1))
                ins.then_inc(wo_done, 1)

            def turn_h2(c):
                pe.wait_ge(normed, (c + 1) * TC)
                if c > 0:
                    pe.wait_ge(lg_read, c)
                    pe.wait_ge(pos_read, 2 * c)
                for k in range(KT):
                    for j in range(TC):
                        ins = nc.tensor.transpose(B[2 + k][:, j * P:(j + 1) * P],
                                                  N2[:, c * TC + j, k * P:(k + 1) * P], identf[:, :])
                    ins.then_inc(turned, 1)

            def make_logits(c):
                pe.wait_ge(turned_kept, 16 + KT * (c + 1))
                for j in range(TC):
                    t = c * TC + j
                    for k in range(KT):
                        ins = mm(B[2][:, j * EXPERTS:(j + 1) * EXPERTS], xT[:, k, t * P:(t + 1) * P], rw[:, k, :],
                                 start=(k == 0), stop=(k == KT - 1))
                ins.then_inc(lg_done, 1)

            def make_pos(c):
                pe.wait_ge(sel_made, c + 1)
                ts = slice(c * TC, (c + 1) * TC)
                mm(B[3][:, 0:TC * EXPERTS], tri16[:, :], sel16[:, ts, :].rearrange("p t e -> p (t e)"), start=True, stop=False)
                mm(B[3][:, 0:TC * EXPERTS], ones16[:, :], pre16[:, ts, :].rearrange("p t e -> p (t e)"),
                   start=False, stop=True).then_inc(pos_done, 1)

            def start_last_wo():
                pe.wait_ge(x2_made, T - TC)
                pe.wait_ge(lg_read, CHUNKS - 1)
                pe.wait_ge(pos_read, 2 * (CHUNKS - 1))
                for j in range(TC):
                    t = T - TC + j
                    mm(B[j][:, 0:D], xT[:, 0, t * P:(t + 1) * P], wqkvo[:, 3, 0, :], start=True, stop=False)

            def make_end(c):
                for j in range(TC):
                    t = c * TC + j
                    pe.wait_ge(last_ctx_kept, j + 1)
                    mm(B[j][:, 0:D], xT[:, 1, t * P:(t + 1) * P], wqkvo[:, 3, 1, :], start=False, stop=True).then_inc(wo_done, 1)
                turn_h2(c)
                make_logits(c)
                make_pos(c)

            for i in range(2):
                pe.wait_ge(stacked[i], 16 * 12)
            pe.wait_ge(ones_row, 16)
            for k in range(len(RING)):
                make_max(0, k)
                for kind, i in side_jobs(k):
                    if kind == "v":
                        make_v(i)
                    else:
                        make_qk(i)
            pe.wait_ge(v_kept, T)
            pe.wait_ge(qk_kept, 8)
            pe.wait_ge(stacked[2], 16 * 12)
            for u in range(UNITS):
                if u == UNITS // 2 - 1:
                    for i in range(3, 5):
                        pe.wait_ge(stacked[i], 16 * 12)
                for n in range(STEPS):
                    if n < 4:
                        pe.wait_ge(max_placed, 4 * u + n + 1)
                    scores(u, n)
                    if u + 1 < UNITS:
                        for k in ring_at(n):
                            make_max(u + 1, k)
                    if n == 3 and u > 0:
                        weigh(u - 1, T - 1)
                    if n == 5 and u > 0:
                        sum_p(u - 1)
                    if n % 4 == 3 and n > 4:
                        weigh(u, n // 4 - 1)
                    if u == UNITS - 1:
                        for j in range(TC):
                            if stage_of(n, WO_STEP + j) is not None:
                                make_wo(stage_of(n, WO_STEP + j) * TC + j)
                        for stage, first in ((turn_h2, TURN_STEP), (make_logits, ROUTER_STEP), (make_pos, POS_STEP)):
                            if stage_of(n, first) is not None:
                                stage(stage_of(n, first))
            weigh(UNITS - 1, T - 1)
            sum_p(UNITS - 1)

            start_last_wo()
            make_end(CHUNKS - 1)


            def turn_xe(e):
                pe.wait_ge(xe_in[e % 2], 32 * (e // 2 + 1))
                for k in range(KT):
                    if e > 0:
                        pe.wait_ge(xe_lo, 2 * (e - 1) + k + 1)
                    for i, r in enumerate(tile_rows):
                        ins = nc.tensor.transpose(B[k][:, i * P:i * P + r], xrow[e % 2][0:r, i, k * P:(k + 1) * P],
                                                  identf[0:r, 0:r])
                    ins.then_inc(xe_turned, 1)

            def turn_y(e, i):
                pe.wait_ge(f2_kept, 2 * (e + 1))
                m, r = 4 * e + i, tile_rows[i]
                if m >= 2:
                    pe.wait_ge(y_kept, m - 1)
                for d in range(KT):
                    ins = nc.tensor.transpose(B[6 + m % 2][0:r, d * P:(d + 1) * P], yT[:, d, i * P:i * P + r], identf[:, :])
                ins.then_inc(y_turned, 1)

            turn_xe(0)
            for e in range(EXPERTS):
                pe.wait_ge(w_hi, 4 * (e + 1))
                pe.wait_ge(w_lo, 4 * (e + 1))
                pe.wait_ge(xe_hi, 2 * (e + 1))
                pe.wait_ge(xe_lo, 2 * (e + 1))
                for f in range(FT):
                    m = e * FT + f
                    if m >= 2:
                        pe.wait_ge(f1_kept, m - 1)
                    for n, (a, b) in enumerate(PARTS):
                        for k in range(KT):
                            ins = mm(B[2 + m % 2][:, 0:CAP], w1_of[e % 2][:, a, k, f * P:(f + 1) * P], xeT[e % 2][:, b, k, :],
                                     start=(n == 0 and k == 0), stop=(n == 2 and k == KT - 1))
                    ins.then_inc(f1_done, 1)
                    if 1 <= f <= 4 and e > 0:
                        turn_y(e - 1, f - 1)
                if e + 1 < EXPERTS:
                    turn_xe(e + 1)
                for d in range(KT):
                    if e > 0:
                        pe.wait_ge(f2_kept, 2 * (e - 1) + d + 1)
                    for f in range(FT):
                        pe.wait_ge(hid_hi, e * FT + f + 1)
                        pe.wait_ge(hid_lo, e * FT + f + 1)
                        for n, (a, b) in enumerate(PARTS):
                            ins = mm(B[4 + d][:, 0:CAP], w2_of[e % 2][:, a, f, d * P:(d + 1) * P], hid[e % 2][:, b, f, :],
                                     start=(f == 0 and n == 0), stop=(f == FT - 1 and n == 2))
                    ins.then_inc(f2_done, 1)
            for i in range(4):
                turn_y(EXPERTS - 1, i)

        @block.scalar
        def _(act):
            A = nc.scalar.activation

            def high_z(c):
                for i in range(2 * c, 2 * c + 2):
                    act.wait_ge(turned, i + 1)
                    A(zT[:, 0, i % 2, c * BANK:(c + 1) * BANK], B[i % 2][:, :], ACT.Copy).then_inc(turned_kept, 1)

            def keep_projection(t):
                act.wait_ge(proj_done, t + 1)
                A(H[:, 0, t, 0:D], B[H_BANK[t % 3]][:, 0:D], ACT.Copy, scale=1.0 / WSCALE).then_inc(proj_act, 1)
                A(G[:, 0, t, :], B[G_BANK[t % 3]][:, 0:GW], ACT.Copy, scale=1.0 / WSCALE).then_inc(proj_act, 1)

            high_z(0)
            high_z(1)
            act.wait_ge(wg_summed, 1)
            A(WG16[:, 0], WG[:, :, :], ACT.Copy, scale=WSCALE).then_inc(wg_hi, 1)
            A(wsl16[:, 0], wsl_bc, ACT.Copy, scale=WSCALE).then_inc(wg_hi, 1)
            for t in range(T):
                keep_projection(t)
                if t in (3, 7):
                    high_z(t // 4 + 2)
            for c in range(4):
                act.wait_ge(sl_done, c + 1)
                A(neg_sl[:, c * BANK:(c + 1) * BANK], B[6 + c % 2][:, :], ACT.Copy, scale=-1.0 / WSCALE).then_inc(sl_kept, 1)

            def read_sums(c):
                act.wait_ge(gnn_mm, (c + 1) * JP)
                if c > 0:
                    act.wait_ge(gnn_v, c)
                for i in range(PAIR):
                    A(xa[:, i, 0:D + 1], B[4 + i][:, 0:D + 1], ACT.Copy).then_inc(gnn_read_act, 1)

            def tanh_gates(c):
                act.wait_ge(gate_v, c + 1)
                A(gt[:, :, 2:4], gt[:, :, 0:2], ACT.Tanh, scale=0.5).then_inc(gate_e, 1)

            def tanh_gnn(c):
                act.wait_ge(gnn_v, c + 1)
                A(gv[:, :, 2, :], gv[:, :, 1, :], ACT.Tanh, scale=0.5).then_inc(gnn_e, 1)

            def exp_e(n):
                act.wait_ge(logit_made, n + 1)
                A(W[:, n % 4, :], W[:, n % 4, :], ACT.Exp).then_inc(e_made, 1)

            def keep_adj(n):
                act.wait_ge(adjT_done, n + 1)
                if n >= 3:
                    act.wait_ge(gnn_mm, n - 2)
                A(Ab[:, n % 3, :], B[n % 4][:, :], ACT.Copy).then_inc(adjT_kept, 1)

            def high_e(n):
                act.wait_ge(e_masked, n + 1)
                if n >= 3:
                    act.wait_ge(gnn_mm, n - 2)
                A(E16[:, n % 3, 0, :], W[:, n % 4, :], ACT.Copy, scale=ESCALE).then_inc(e_hi, 1)

            for n in range(-2, CH * JP):
                if n > 0 and n % JP == 0:
                    read_sums(n // JP - 1)
                if n + 2 < CH * JP:
                    keep_adj(n + 2)
                if 0 <= n + 1 < CH * JP:
                    high_e(n + 1)
                if n + 2 < CH * JP:
                    exp_e(n + 2)
                if n > 0 and n % JP == 0:
                    tanh_gates(n // JP - 1)
                if n > JP and n % JP == 2:
                    tanh_gnn(n // JP - 1)
            act.wait_ge(bias_in, 192)

            def keep_h(c):
                for k in range(KT):
                    act.wait_ge(turned, 8 + 2 * c + k + 1)
                    A(xT[:, k, c * BANK:(c + 1) * BANK], B[k][:, :], ACT.Identity, bias=cols[:, 1, k:k + 1],
                      scale=cols[:, 0, k:k + 1]).then_inc(turned_kept, 1)

            read_sums(CH - 1)
            tanh_gates(CH - 1)
            keep_h(0)
            tanh_gnn(CH - 1)
            keep_h(1)

            def keep_qk(m):
                s, g, c = QK_JOBS[m]
                cs = slice(c * QC, (c + 1) * QC)
                bias = cols[:, 2 + s, g:g + 1]
                act.wait_ge(qk_done, m + 1)
                A(part_of(s, g)[:, 0, cs], B[4 + m % 2][:, :], ACT.Identity, bias=bias).then_inc(qk_hi, 1)
                if m >= 8:
                    if m >= 10:
                        act.wait_ge(qk_lo2, m - 9)
                    A(qk32[:, m % 2, :], B[4 + m % 2][:, :], ACT.Identity, bias=bias).then_inc(qk_kept, 1)

            def copy_v(t):
                act.wait_ge(v_done, t + 1)
                A(V[:, t, :], B[6 + t % 2][:, 0:D], ACT.Copy).then_inc(v_copied, 1)

            for m in range(8):
                if m in TURN_JOBS:
                    keep_h(TURN_JOBS.index(m) + 2)
                if m == 3:
                    for t in range(V_GAP):
                        copy_v(t)
                keep_qk(m)
            for t in range(V_GAP, V_EARLY):
                copy_v(t)

            def place_max(u, h):
                g, c = u // NC, u % NC
                act.wait_ge(max_turned, 4 * u + h + 1)
                A(q_stack[HROWS:HROWS + 1, 4 * g + h, c * QC:(c + 1) * QC],
                  wide[RING.index(("row", h)) % 2][0:1, 0:QC], ACT.Copy).then_inc(max_placed, 1)

            NC = N // QC
            for k in range(len(RING)):
                if RING[k][0] == "row":
                    place_max(0, RING[k][1])
                for kind, i in side_jobs(k):
                    if kind == "v":
                        copy_v(i)
                    else:
                        keep_qk(i)
            for i in range(3):
                act.wait_ge(stacked[i], 16 * 12)
            def keep_h2(c):
                for k in range(KT):
                    act.wait_ge(turned, 16 + KT * c + k + 1)
                    A(xT[:, k, c * QC:(c + 1) * QC], B[2 + k][:, :], ACT.Identity, bias=cols[:, 5, k:k + 1],
                      scale=cols[:, 4, k:k + 1]).then_inc(turned_kept, 1)

            def save_ctx(u):
                g, c = u // NC, u % NC
                act.wait_ge(pv_done, T * (u + 1))
                A(xT[:, g, c * QC:(c + 1) * QC], B[6], ACT.Copy).then_inc(ctx_saved, 1)

            def weight_hi(e, q):
                part = slice(q * 1024, (q + 1) * 1024)
                if q == 0:
                    act.wait_ge(w_in[e % 2], 32 * (e // 2 + 1))
                    if e >= 2:
                        act.wait_ge(f2_done, KT * (e - 1))
                A(w_split[e % 2][:, 0, part], w_land[e % 2][:, part], ACT.Copy, scale=WSCALE).then_inc(w_hi, 1)

            row_steps = {}
            for h in range(4):
                k = RING.index(("row", h))
                row_steps[min(RING_STEPS[k] + 2, STEPS - 1)] = h
            for m in range(UNITS * STEPS):
                u, kt, h = m // STEPS, m % STEPS // 4, m % 4
                if u + 1 < UNITS and m % STEPS in row_steps:
                    place_max(u + 1, row_steps[m % STEPS])
                if u == UNITS - 1 and stage_of(m % STEPS, TURN_STEP) is not None:
                    keep_h2(stage_of(m % STEPS, TURN_STEP))
                if u > 0 and m % STEPS == 5:
                    save_ctx(u - 1)
                act.wait_ge(s_mm, m + 1)
                if h == 0 and m in (8, 12):
                    act.wait_ge(stacked[m // 4 + 1], 16 * 12)
                if h == 0 and m >= 4 * PTK:
                    k0 = m // 4 - PTK
                    u0, kt0 = k0 // T, k0 % T
                    act.wait_ge(pv_done, k0 + 1)
                    if kt0 in SUM_KT:
                        act.wait_ge(p_summed, u0 * SUM_OPS + max(SUM_KT.index(kt0), 1))
                A(PT[:, kt % PTK, h * QC:(h + 1) * QC], B[4 + m % 2], ACT.Exp, scale=SCALE).then_inc(p_made, 1)

            save_ctx(UNITS - 1)
            for q in range(4):
                weight_hi(0, q)
            keep_h2(CHUNKS - 1)

            def x_hi(e):
                for k in range(KT):
                    act.wait_ge(xe_turned, 2 * e + k + 1)
                    A(xeT[e % 2][:, 0, k, :], B[k][:, 0:CAP], ACT.Copy).then_inc(xe_hi, 1)

            act.wait_ge(experts_b_in, 32 * EXPERTS)
            act.wait_ge(lg_done, CHUNKS)
            x_hi(0)
            for e in range(EXPERTS):
                for f in range(FT):
                    m = e * FT + f
                    act.wait_ge(f1_done, m + 1)
                    if m >= 2:
                        act.wait_ge(hid_lo, m - 1)
                    A(hid32[m % 2], B[2 + m % 2][:, 0:CAP], ACT.Gelu, bias=b1c[:, e, f:f + 1],
                      scale=1.0 / WSCALE).then_inc(f1_kept, 1)
                    act.wait_ge(f1_kept, m + 1)
                    A(hid[e % 2][:, 0, f, :], hid32[m % 2], ACT.Copy).then_inc(hid_hi, 1)
                if e + 1 < EXPERTS:
                    x_hi(e + 1)
                    for q in range(4):
                        weight_hi(e + 1, q)

        @block.vector
        def _(dve):
            v = nc.vector
            n_step = [0]

            def step(ins):
                n_step[0] += 1
                ins.then_inc(dve_step, 1)

            def settle():
                dve.wait_ge(dve_step, n_step[0])

            def link(ins):
                step(ins)
                settle()

            norms = [0]

            def norm_stats(src, t0=0, t1=T, wait=None):
                for t in range(t0, t1):
                    if wait is not None:
                        wait(t)
                    step(v.bn_stats(stats[:, t, :], src[:, t, :]))
                settle()
                for t in range(t0, t1):
                    step(v.bn_aggr(mv[:, t, :], stats[:, t, :]))
                settle()
                v.tensor_scalar(veps[:, t0:t1], mv[:, t0:t1, 1], EPS, None, ALU.add).then_inc(var_made, 1)
                norms[0] += 1

            def await_rstd():
                dve.wait_ge(rstd_made, norms[0])

            def normalise(dst, src, t):
                return v.tensor_scalar(dst[:, t, :], src[:, t, :], mv[:, t, 0:1], rstd[:, t:t + 1], ALU.subtract, ALU.mult)

            def stats_x(c):
                norm_stats(X, 4 * c, 4 * c + 4, wait=lambda t: dve.wait_ge(x_in[c], 16))

            def norm_x(c):
                dve.wait_ge(rstd_made, c + 1)
                for t in range(4 * c, 4 * c + 4):
                    normalise(Z, X, t).then_inc(rows_ready, 1)

            def low_z(c):
                for i in range(2 * c, 2 * c + 2):
                    dve.wait_ge(turned_kept, i + 1)
                    part = zT[:, :, i % 2, c * BANK:(c + 1) * BANK]
                    v.tensor_tensor(part[:, 1], B[i % 2][:, :], part[:, 0], ALU.subtract).then_inc(z_lo, 1)

            stats_x(0)
            stats_x(1)
            norm_x(0)

            dve.wait_ge(gnn_w_in, 16 * 13)
            for k in range(KT):
                for s in range(2):
                    link(v.tensor_tensor_reduce(junk[:, :], WG[:, k, 0:D], a_bc[:, s * D:(s + 1) * D], 1.0, 0.0,
                                                ALU.mult, ALU.add, WG[:, k, D + s:D + s + 1]))
            for k in range(KT):
                step(v.tensor_scalar(wsl_bc[:, k, :], WG[:, k, 0:P], 0.0, WG[:, k, D:D + 1], ALU.mult, ALU.add))
            settle()
            v.memset(junk[:, 0:1], 0.0).then_inc(wg_summed, 1)
            norm_x(1)
            low_z(0)
            low_z(1)
            dve.wait_ge(wg_hi, 2)
            v.scalar_tensor_tensor(out=WG16[:, 1], in0=WG[:, :, :], scalar=WSCALE, in1=WG16[:, 0],
                                   op0=ALU.mult, op1=ALU.subtract).then_inc(wg_lo, 1)
            v.scalar_tensor_tensor(out=wsl16[:, 1], in0=wsl_bc, scalar=WSCALE, in1=wsl16[:, 0],
                                   op0=ALU.mult, op1=ALU.subtract).then_inc(wg_lo, 1)
            stats_x(2)
            stats_x(3)
            norm_x(2)
            norm_x(3)
            step(v.memset(H[:, 0, :, D:D + 1], 1.0))
            step(v.memset(H[:, 1, :, D:D + 1], 0.0))

            for t in range(T):
                dve.wait_ge(proj_act, 2 * (t + 1))
                step(v.scalar_tensor_tensor(out=H[:, 1, t, 0:D], in0=B[H_BANK[t % 3]][:, 0:D], scalar=1.0 / WSCALE,
                                            in1=H[:, 0, t, 0:D], op0=ALU.mult, op1=ALU.subtract))
                step(v.tensor_scalar(sc[:, t, :], B[H_BANK[t % 3]][:, D:D + 2], 1.0 / WSCALE, None, ALU.mult))
                step(v.scalar_tensor_tensor(out=u2[:, t, :], in0=B[G_BANK[t % 3]][:, GW:GW + 2], scalar=1.0 / WSCALE,
                                            in1=gate_b[:, :], op0=ALU.mult, op1=ALU.add))
                v.scalar_tensor_tensor(out=G[:, 1, t, :], in0=B[G_BANK[t % 3]][:, 0:GW], scalar=1.0 / WSCALE,
                                       in1=G[:, 0, t, :], op0=ALU.mult, op1=ALU.subtract).then_inc(proj_dve, 1)
                if t in (3, 7):
                    low_z(t // 4 + 2)
            settle()
            v.tensor_scalar(neg_sr[:, :], sc[:, :, 1], -1.0, None, ALU.mult).then_inc(neg_sr_made, 1)
            dve.wait_ge(bias_in, 192)

            def logits(n):
                dve.wait_ge(s_made, n + 1)
                v.scalar_tensor_tensor(out=W[:, n % 4, :], in0=W[:, n % 4, :], scalar=LEAK, in1=W[:, n % 4, :],
                                       op0=ALU.mult, op1=ALU.min).then_inc(logit_made, 1)

            def mask(n):
                dve.wait_ge(e_made, n + 1)
                dve.wait_ge(adjT_kept, n + 1)
                v.tensor_tensor(W[:, n % 4, :], B[n % 4][:, :], W[:, n % 4, :], ALU.mult).then_inc(e_masked, 1)

            def low_e(n):
                dve.wait_ge(e_hi, n + 1)
                if n >= 3:
                    dve.wait_ge(gnn_mm, n - 2)
                v.scalar_tensor_tensor(out=E16[:, n % 3, 1, :], in0=W[:, n % 4, :], scalar=ESCALE, in1=E16[:, n % 3, 0, :],
                                       op0=ALU.mult, op1=ALU.subtract).then_inc(e_lo, 1)

            def read_sums(c):
                dve.wait_ge(gnn_mm, (c + 1) * JP)
                for i in range(PAIR):
                    v.tensor_copy(xb[:, i, :], B[6 + i][:, 0:GW]).then_inc(gnn_read_dve, 1)

            def gate(c):
                t0 = c * PAIR
                dve.wait_ge(gnn_read_dve, (c + 1) * PAIR)
                v.tensor_tensor(gt[:, :, 0:2], xb[:, :, D:GW], u2[:, t0:t0 + PAIR, :], ALU.add).then_inc(gate_v, 1)
                dve.wait_ge(gnn_read_act, (c + 1) * PAIR)
                link(v.tensor_scalar(gt[:, :, 4:5], xa[:, :, D:D + 1], ESCALE * 1e-5, None, ALU.add))
                step(v.reciprocal(gt[:, :, 5:6], gt[:, :, 4:5]))

            def apply_gate(c):
                dve.wait_ge(gate_e, c + 1)
                dve.wait_ge(xb_made, c + 1)
                link(v.tensor_scalar(gt[:, :, 6:8], gt[:, :, 2:4], 0.5, 0.5, ALU.mult, ALU.add))
                step(v.tensor_tensor(gt[:, :, 5:6], gt[:, :, 5:6], gt[:, :, 6:7], ALU.mult))
                for i in range(PAIR):
                    step(v.tensor_scalar(gv[:, i, 0, :], gv[:, i, 0, :], gt[:, i, 7:8], None, ALU.mult))
                settle()
                for i in range(PAIR):
                    step(v.scalar_tensor_tensor(out=gv[:, i, 1, :], in0=xa[:, i, 0:D], scalar=gt[:, i, 5:6],
                                                in1=gv[:, i, 0, :], op0=ALU.mult, op1=ALU.add))
                settle()
                v.memset(junk[:, 4:5], 0.0).then_inc(gnn_v, 1)

            def x1_stats(c):
                dve.wait_ge(x1_made, c + 1)
                norm_stats(X, c * PAIR, (c + 1) * PAIR)

            def norm_x1(c):
                dve.wait_ge(rstd_made, 4 + 2 * c + 1)
                for t in range(c * PAIR, (c + 1) * PAIR):
                    step(normalise(Z, X, t))

            def z1_stats(c):
                settle()
                norm_stats(Z, c * PAIR, (c + 1) * PAIR)

            def norm_z1(c0, c1):
                dve.wait_ge(rstd_made, 4 + 2 * c1)
                dve.wait_ge(adjT_done, 6 * JP)
                for t in range(c0 * PAIR, c1 * PAIR):
                    normalise(NB, Z, t).then_inc(rows_ready, 1)

            def low_qk(m):
                s, g, c = QK_JOBS[m]
                cs = slice(c * QC, (c + 1) * QC)
                dve.wait_ge(qk_hi, m + 1)
                v.scalar_tensor_tensor(out=part_of(s, g)[:, 1, cs], in0=B[4 + m % 2][:, :], scalar=cols[:, 2 + s, g:g + 1],
                                       in1=part_of(s, g)[:, 0, cs], op0=ALU.add, op1=ALU.subtract).then_inc(qk_lo, 1)

            EARLY = CH - 2
            for n in range(-2, CH * JP):
                if n >= 0:
                    low_e(n)
                if n > 0 and n % JP == 0:
                    read_sums(n // JP - 1)
                if 0 <= n + 1 < CH * JP:
                    mask(n + 1)
                if n + 2 < CH * JP:
                    logits(n + 2)
                if n > 0 and n % JP == 0:
                    gate(n // JP - 1)
                if n > JP and n % JP == 2:
                    apply_gate(n // JP - 1)
                if n > JP and n % JP == 5:
                    x1_stats(n // JP - 1)
                if n > JP and n % JP == 6:
                    norm_x1(n // JP - 1)
                if n > JP and n % JP == 7:
                    z1_stats(n // JP - 1)
                c = (1, 3, 4, 5, 6, 7).index(n % JP) if n % JP in (1, 3, 4, 5, 6, 7) else EARLY
                if n > (CH - 1) * JP and c < EARLY:
                    norm_z1(c, c + 1)
            read_sums(CH - 1)
            gate(CH - 1)
            norm_z1(EARLY, CH - 1)
            apply_gate(CH - 1)
            low_qk(0)
            x1_stats(CH - 1)
            low_qk(1)
            norm_x1(CH - 1)
            z1_stats(CH - 1)
            low_qk(2)
            norm_z1(CH - 1, CH)
            for m in range(3, 8):
                low_qk(m)

            NC = N // QC

            DIVIDE_STEPS = (9, 13, 18, 22, 23)

            def read_max(u, k):
                kind, i = RING[k]
                if kind == "row":
                    return
                m = PAIRS * u + i
                dve.wait_ge(max_mm, m + 1)
                v.tensor_reduce(mx[:, i // 2, i % 2, :], wide[k % 2][:, :].rearrange("p (a n) -> p a n", a=2),
                                AX.X, ALU.max).then_inc(max_read, 1)
                if i % 8 == 7:
                    h = i // 8
                    hs = slice(4 * h, 4 * h + 4)
                    dve.wait_ge(max_read, m + 1)
                    link(v.tensor_reduce(nm[:, hs], mx[:, hs, :, :].rearrange("p n a b -> p n (a b)"), AX.X, ALU.max))
                    if u > 0:
                        dve.wait_ge(max_turned, 4 * (u - 1) + h + 1)
                    v.tensor_scalar(nm16[:, hs], nm[:, hs], -1.0, None, ALU.mult).then_inc(negmax, 1)

            def invert_sums(u, q):
                dve.wait_ge(den_done, u + 1)
                if u > 0 and q == 0:
                    dve.wait_ge(ctx_kept, u)
                part = slice(q * P, (q + 1) * P)
                v.reciprocal(rden[:, part], B[7][:, part]).then_inc(sums_inverted, 1)

            def divide_ctx(u):
                g, c = u // NC, u % NC
                dve.wait_ge(sums_inverted, 4 * (u + 1))
                dve.wait_ge(ctx_saved, u + 1)
                part = xT[:, g, c * QC:(c + 1) * QC]
                v.tensor_tensor(part, part, rden, ALU.mult).then_inc(ctx_kept, 1)

            def sum_probs(u, i):
                if i == 1:
                    dve.wait_ge(den_done, u)
                else:
                    dve.wait_ge(p_summed, u * SUM_OPS + i - 1)
                dve.wait_ge(p_made, STEPS * u + 4 * SUM_KT[i] + 4)
                v.tensor_tensor(p_sum, PT[:, SUM_KT[0] % PTK, :] if i == 1 else p_sum,
                                PT[:, SUM_KT[i] % PTK, :], ALU.add).then_inc(p_summed, 1)

            def sum_x2(c):
                tiles = range(c * TC, (c + 1) * TC)
                for t in tiles:
                    bank = B[t % 2] if c < CHUNKS - 1 else B[t - tiles[0]]
                    dve.wait_ge(wo_done, t + 1)
                    v.tensor_tensor(Z[:, t, :], bank[:, 0:D], Z[:, t, :], ALU.add).then_inc(x2_made, 1)
                norm_stats(Z, tiles[0], tiles[-1] + 1, wait=lambda t: dve.wait_ge(x2_made, t + 1))

            def norm_x2(c):
                await_rstd()
                for t in range(c * TC, (c + 1) * TC):
                    normalise(N2, Z, t).then_inc(normed, 1)

            def finish_h2(c):
                tiles = range(c * TC, (c + 1) * TC)
                for t in tiles:
                    v.tensor_tensor(X[:, t, :], X[:, t, :], Z[:, t, :], ALU.add).then_inc(x12_dve, 1)
                dve.wait_ge(normed, (c + 1) * TC)
                dve.wait_ge(x12_dve, TC)
                for t in tiles:
                    step(v.tensor_tensor(Z[:, t, :], N2[:, t, :], rows[:, 3, :], ALU.mult))
                settle()
                for t in tiles:
                    v.tensor_tensor(Z[:, t, :], Z[:, t, :], rows[:, 4, :], ALU.add).then_inc(h2_dve, 1)

            chunk_shape = (P, TC, EXPERTS)
            ids = eid[:, :].unsqueeze(1).to_broadcast(chunk_shape)
            offs = eoff[:, :].unsqueeze(1).to_broadcast(chunk_shape)

            def rank(c):
                ts = slice(c * TC, (c + 1) * TC)
                tiles = range(c * TC, (c + 1) * TC)
                dve.wait_ge(lg_done, c + 1)
                v.tensor_tensor(lg[:, ts, :], B[2][:, 0:TC * EXPERTS].rearrange("p (t e) -> p t e", t=TC),
                                rb_bc[:, :].unsqueeze(1).to_broadcast(chunk_shape), ALU.add).then_inc(lg_read, 1)
                dve.wait_ge(lg_read, c + 1)
                for t in tiles:
                    step(v.max(top[:, t, :], lg[:, t, :]))
                settle()
                for t in tiles:
                    step(v.max_index(topi[:, t, :], top[:, t, :], lg[:, t, :]))
                settle()
                link(v.tensor_copy(topf[:, ts, :], topi[:, ts, :]))
                for s in range(TOPK):
                    step(v.tensor_tensor(chosen[:, s, ts, :], topf[:, ts, s:s + 1].to_broadcast(chunk_shape), ids, ALU.is_equal))
                settle()
                step(v.tensor_tensor(sel16[:, ts, :], chosen[:, 0, ts, :], chosen[:, 1, ts, :], ALU.add))
                if c == 0:
                    step(v.memset(pre16[:, 0, :], 0.0))
                settle()
                for t in tiles:
                    if t + 1 < T:
                        link(v.tensor_tensor(pre16[:, t + 1, :], pre16[:, t, :], sel16[:, t, :], ALU.add))
                v.memset(junk[:, 6:7], 0.0).then_inc(sel_made, 1)

            def give_slots(c):
                ts = slice(c * TC, (c + 1) * TC)
                dve.wait_ge(pos_done, c + 1)
                pos = B[3][:, 0:TC * EXPERTS].rearrange("p (t e) -> p t e", t=TC)
                v.scalar_tensor_tensor(out=kept[:, ts, :], in0=pos, scalar=float(CAP), in1=sel16[:, ts, :],
                                       op0=ALU.is_le, op1=ALU.mult).then_inc(pos_read, 1)
                v.tensor_tensor(val[:, ts, :], pos, offs, ALU.add).then_inc(pos_read, 1)
                dve.wait_ge(pos_read, 2 * (c + 1))
                link(v.tensor_tensor(val[:, ts, :], val[:, ts, :], kept[:, ts, :], ALU.mult))
                link(v.tensor_reduce(slot[:, ts], val[:, ts, :], AX.X, ALU.max))
                link(v.tensor_scalar(slot_off[:, ts], slot[:, ts], 0.0, float(SKIP), ALU.is_equal, ALU.mult))
                link(v.tensor_tensor(slot_sc[:, ts], slot[:, ts], slot_off[:, ts], ALU.add))
                v.tensor_copy(slot_s[:, ts], slot_sc[:, ts]).then_inc(slots_made, 1)

            for k in range(len(RING)):
                read_max(0, k)
            for t in range(T):
                step(v.tensor_tensor(Z[:, t, :], Z[:, t, :], rows[:, 2, :], ALU.add))
            settle()
            for u in range(UNITS):
                for n in range(STEPS):
                    if u + 1 < UNITS:
                        for k in ring_at(n):
                            read_max(u + 1, k)
                    if n in DIVIDE_STEPS[:-1] and u > 0:
                        invert_sums(u - 1, DIVIDE_STEPS.index(n))
                    if n == DIVIDE_STEPS[-1] and u > 0:
                        divide_ctx(u - 1)
                    for i in range(1, len(SUM_KT)) if u == UNITS - 1 else DVE_SUMS:
                        if n == 4 * SUM_KT[i] + 5:
                            sum_probs(u, i)
                    if u == UNITS - 1:
                        for stage, first in ((sum_x2, STATS_STEP), (norm_x2, NORM_STEP), (rank, TOP_STEP), (give_slots, SLOT_STEP)):
                            if stage_of(n, first) is not None:
                                stage(stage_of(n, first))
            g, c = (UNITS - 1) // NC, (UNITS - 1) % NC
            for q in range(4):
                invert_sums(UNITS - 1, q)
                dve.wait_ge(sums_inverted, 4 * (UNITS - 1) + q + 1)
                dve.wait_ge(ctx_saved, UNITS)
                part = xT[:, g, c * QC + q * P:c * QC + (q + 1) * P]
                v.tensor_tensor(part, part, rden[:, q * P:(q + 1) * P], ALU.mult).then_inc(last_ctx_kept, 1)

            sum_x2(CHUNKS - 1)
            norm_x2(CHUNKS - 1)
            finish_h2(CHUNKS - 1)
            rank(CHUNKS - 1)
            give_slots(CHUNKS - 1)

            def weight_lo(e, q):
                part = slice(q * 1024, (q + 1) * 1024)
                dve.wait_ge(w_hi, 4 * e + q + 1)
                v.scalar_tensor_tensor(out=w_split[e % 2][:, 1, part], in0=w_land[e % 2][:, part], scalar=WSCALE,
                                       in1=w_split[e % 2][:, 0, part], op0=ALU.mult, op1=ALU.subtract).then_inc(w_lo, 1)

            def x_lo(e):
                for k in range(KT):
                    dve.wait_ge(xe_hi, 2 * e + k + 1)
                    v.tensor_tensor(xeT[e % 2][:, 1, k, :], B[k][:, 0:CAP], xeT[e % 2][:, 0, k, :],
                                    ALU.subtract).then_inc(xe_lo, 1)

            def keep_y(e, i):
                r = tile_rows[i]
                dve.wait_ge(y_turned, 4 * e + i + 1)
                if i == 0:
                    dve.wait_ge(xs_in[e % 2], 32 * (e // 2 + 1))
                    if e >= 2:
                        dve.wait_ge(y_out[e % 2], 16 * 4 * (e // 2))
                v.tensor_tensor(yrow[e % 2][0:r, i, :], B[6 + (4 * e + i) % 2][0:r, 0:D], xslot[e % 2][0:r, i, 0:D],
                                ALU.add).then_inc(y_kept, 1)

            for q in range(4):
                weight_lo(0, q)
            x_lo(0)
            for e in range(EXPERTS):
                for f in range(FT):
                    m = e * FT + f
                    dve.wait_ge(hid_hi, m + 1)
                    v.tensor_tensor(hid[e % 2][:, 1, f, :], hid32[m % 2], hid[e % 2][:, 0, f, :],
                                    ALU.subtract).then_inc(hid_lo, 1)
                    if 1 <= f <= 4 and e > 0:
                        keep_y(e - 1, f - 1)
                if e + 1 < EXPERTS:
                    x_lo(e + 1)
                    for q in range(4):
                        weight_lo(e + 1, q)
                for d in range(KT):
                    dve.wait_ge(f2_done, KT * e + d + 1)
                    if e > 0:
                        dve.wait_ge(y_turned, 4 * e)
                    v.tensor_scalar(yT[:, d, :], B[4 + d][:, 0:CAP], 1.0 / WSCALE, b2c[:, e, d:d + 1],
                                    ALU.mult, ALU.add).then_inc(f2_kept, 1)
            for i in range(4):
                keep_y(EXPERTS - 1, i)


_INS = ['x', 'adj', 'L0_gnn_W_sa', 'L0_gnn_a_sa', 'L0_gnn_W_gcnb', 'L0_gnn_b_gcnb', 'L0_gnn_Wa', 'L0_gnn_ba',
        'L0_gnn_Wb', 'L0_gnn_bb', 'L0_ffn_ln1_g', 'L0_ffn_ln1_b', 'L0_ffn_ln2_g', 'L0_ffn_ln2_b', 'L0_ffn_wq',
        'L0_ffn_bq', 'L0_ffn_wk', 'L0_ffn_bk', 'L0_ffn_wv', 'L0_ffn_bv', 'L0_ffn_wo', 'L0_ffn_bo',
        'L0_ffn_router_w', 'L0_ffn_router_b', 'L0_ffn_w1', 'L0_ffn_b1', 'L0_ffn_w2', 'L0_ffn_b2']


def kernel(**inputs):
    import numpy as _np
    import concourse.bacc as _bacc
    from concourse import mybir as _mybir
    from concourse.bass_utils import run_bass_kernel_spmd as _run

    nc = _bacc.Bacc("TRN2", target_bir_lowering=False, num_devices=1)
    arrays, args = {}, []
    for name in _INS:
        a = _np.ascontiguousarray(inputs[name])
        arrays[f"in_{name}_dram"] = a
        args.append(nc.dram_tensor(f"in_{name}_dram", a.shape, _mybir.dt.from_np(a.dtype), kind="ExternalInput").ap())
    args.append(nc.dram_tensor("out_dram", (N, D), _mybir.dt.from_np(_np.dtype("float32")), kind="ExternalOutput").ap())
    gnn_moe_kernel(nc, *args)
    r = _run(nc, [arrays], core_ids=[0])
    return r.results[0]["out_dram"]
```
